# Optimizing a Trainium2 kernel written in Bass

```python
import numpy as np
import jax
import jax.numpy as jnp

def _softmax(x, axis=-1):
    return jax.nn.softmax(x, axis=axis)

def _gelu(x):
    return jax.nn.gelu(x, approximate=True)

def _silu(x):
    return jax.nn.silu(x)

def _sigmoid(x):
    return jax.nn.sigmoid(x)

def _layernorm(x, axis=-1, eps=1e-05):
    m = jnp.mean(x, axis=axis, keepdims=True)
    v = jnp.var(x, axis=axis, keepdims=True)
    return (x - m) / jnp.sqrt(v + eps)

def _scatter_add(tgt, idx, src, axis=0):
    return tgt.at[idx].add(src)

def _segment_sum(src, seg, n):
    return jax.ops.segment_sum(src, seg, n)
kernel_name = 'mk_adaln_d1_jaxref_r4_5d569c'

def setup_inputs(seed: int=0):
    np.random.seed(seed)
    _w = jnp.asarray

    def _L0_attn_setup():
        import jax, jax.numpy as jnp
        import numpy as np
        HEAD_DIM = 128
        HIDDEN_DIM = 256
        B, S = (4, 1024)
        key = jax.random.key(seed)
        k_x, k_q, k_k, k_v, k_o = jax.random.split(key, 5)
        scale = 1.0 / np.sqrt(HIDDEN_DIM)
        return {'x': jax.random.normal(k_x, (B, S, HIDDEN_DIM), dtype=jnp.float32), 'head_dim_mask': jnp.ones((HEAD_DIM,), dtype=jnp.int32), 'w_q': jax.random.normal(k_q, (HIDDEN_DIM, HEAD_DIM), dtype=jnp.float32) * scale, 'w_k': jax.random.normal(k_k, (HIDDEN_DIM, HEAD_DIM), dtype=jnp.float32) * scale, 'w_v': jax.random.normal(k_v, (HIDDEN_DIM, HEAD_DIM), dtype=jnp.float32) * scale, 'w_o': jax.random.normal(k_o, (HEAD_DIM, HIDDEN_DIM), dtype=jnp.float32) * (1.0 / np.sqrt(HEAD_DIM))}
    _L0_attn_in = _L0_attn_setup()

    def _L0_ffn_setup():
        import jax, jax.numpy as jnp
        import numpy as np
        B, S, H = (2, 512, 256)
        E_ROUTED = 8
        TOP_K = 2
        I = 512
        key = jax.random.key(seed)
        ks = jax.random.split(key, 9)
        s = 0.02
        return {'x': jax.random.normal(ks[0], (B, S, H), dtype=jnp.float32), 'shared_gate': jax.random.normal(ks[1], (I, H), dtype=jnp.float32) * s, 'shared_up': jax.random.normal(ks[2], (I, H), dtype=jnp.float32) * s, 'shared_down': jax.random.normal(ks[3], (H, I), dtype=jnp.float32) * s, 'gate_w': jax.random.normal(ks[4], (E_ROUTED, H, I), dtype=jnp.float32) * s, 'up_w': jax.random.normal(ks[5], (E_ROUTED, H, I), dtype=jnp.float32) * s, 'down_w': jax.random.normal(ks[6], (E_ROUTED, I, H), dtype=jnp.float32) * s, 'router_w': jax.random.normal(ks[7], (E_ROUTED, H), dtype=jnp.float32) * s, 'routing_bias': jnp.zeros((E_ROUTED,), dtype=jnp.float32)}
    _L0_ffn_in = _L0_ffn_setup()
    _L0_c = _w((lambda *s: np.random.randn(*s).astype(np.float32) * 0.05)(4, 256))
    _L0_wmod = _w((lambda *s: np.random.randn(*s).astype(np.float32) * 0.05)(256, 6 * 256) * 256 ** (-0.5))
    _d = {'L0_attn_x': _L0_attn_in['x'], 'L0_attn_head_dim_mask': _L0_attn_in['head_dim_mask'], 'L0_attn_w_q': _L0_attn_in['w_q'], 'L0_attn_w_k': _L0_attn_in['w_k'], 'L0_attn_w_v': _L0_attn_in['w_v'], 'L0_attn_w_o': _L0_attn_in['w_o'], 'L0_ffn_shared_gate': _L0_ffn_in['shared_gate'], 'L0_ffn_shared_up': _L0_ffn_in['shared_up'], 'L0_ffn_shared_down': _L0_ffn_in['shared_down'], 'L0_ffn_gate_w': _L0_ffn_in['gate_w'], 'L0_ffn_up_w': _L0_ffn_in['up_w'], 'L0_ffn_down_w': _L0_ffn_in['down_w'], 'L0_ffn_router_w': _L0_ffn_in['router_w'], 'L0_ffn_routing_bias': _L0_ffn_in['routing_bias'], 'L0_c': _L0_c, 'L0_wmod': _L0_wmod}
    _x0 = _d['L0_attn_x']
    _d['L0_attn_x'] = jax.random.normal(jax.random.fold_in(jax.random.key(seed), 1), (4, 2048, 256), dtype=_x0.dtype)
    del _x0
    return _d

def reference(L0_attn_x, L0_attn_head_dim_mask, L0_attn_w_q, L0_attn_w_k, L0_attn_w_v, L0_attn_w_o, L0_ffn_shared_gate, L0_ffn_shared_up, L0_ffn_shared_down, L0_ffn_gate_w, L0_ffn_up_w, L0_ffn_down_w, L0_ffn_router_w, L0_ffn_routing_bias, L0_c, L0_wmod):

    def _L0_attn_ref(x, head_dim_mask, w_q, w_k, w_v, w_o):
        import jax, jax.numpy as jnp
        import numpy as np
        HEAD_DIM = 128
        HIDDEN_DIM = 256
        B, S = (4, 1024)
        q = jnp.einsum('bsh,hd->bsd', x, w_q)
        k = jnp.einsum('bsh,hd->bsd', x, w_k)
        v = jnp.einsum('bsh,hd->bsd', x, w_v)
        scale = 1.0 / jnp.sqrt(jnp.asarray(HEAD_DIM, dtype=x.dtype))
        scores = jnp.einsum('bqd,bkd->bqk', q, k) * scale
        A = jax.nn.softmax(scores, axis=-1)
        h = jnp.einsum('bqk,bkd->bqd', A, v)
        h = h * head_dim_mask.astype(h.dtype)
        y = jnp.einsum('bsd,dh->bsh', h, w_o)
        return y

    def _L0_ffn_ref(x, shared_gate, shared_up, shared_down, gate_w, up_w, down_w, router_w, routing_bias):
        import jax, jax.numpy as jnp
        import numpy as np
        B, S, H = (2, 512, 256)
        E_ROUTED = 8
        TOP_K = 2
        I = 512
        b, s, h = x.shape
        shared = jnp.einsum('bsi,hi->bsh', jax.nn.silu(jnp.einsum('bsh,ih->bsi', x, shared_gate)) * jnp.einsum('bsh,ih->bsi', x, shared_up), shared_down)
        logits = jnp.einsum('bsh,eh->bse', x, router_w) + routing_bias
        probs = jax.nn.sigmoid(logits)
        scores, indices = jax.lax.top_k(probs, TOP_K)
        scores = scores / jnp.sum(scores, axis=-1, keepdims=True)
        t = b * s
        xf = x.reshape(t, h)
        idx = indices.reshape(t, TOP_K)
        sc = scores.reshape(t, TOP_K)
        w = jnp.zeros((t, E_ROUTED), dtype=x.dtype)
        w = w.at[jnp.arange(t)[:, None], idx].add(sc)
        g = jax.nn.silu(jnp.einsum('th,ehi->tei', xf, gate_w))
        u = jnp.einsum('th,ehi->tei', xf, up_w)
        combined = jnp.einsum('tei,eih,te->th', g * u, down_w, w)
        return shared + combined.reshape(b, s, h)
    x = L0_attn_x
    mod = (_silu(L0_c) @ L0_wmod).reshape(L0_c.shape[0], 6, 1, -1)
    sa, ca, ga, sb, cb, gb = (mod[:, 0], mod[:, 1], mod[:, 2], mod[:, 3], mod[:, 4], mod[:, 5])
    ga = (2 * (ga >= 0) - 1) * jnp.maximum(jnp.abs(ga), 0.25)
    gb = (2 * (gb >= 0) - 1) * jnp.maximum(jnp.abs(gb), 0.25)
    h = _layernorm(x, axis=-1) * (1 + ca) + sa
    x = x + ga * _L0_attn_ref(h, L0_attn_head_dim_mask, L0_attn_w_q, L0_attn_w_k, L0_attn_w_v, L0_attn_w_o)
    h = _layernorm(x, axis=-1) * (1 + cb) + sb
    x = x + gb * _L0_ffn_ref(h, L0_ffn_shared_gate, L0_ffn_shared_up, L0_ffn_shared_down, L0_ffn_gate_w, L0_ffn_up_w, L0_ffn_down_w, L0_ffn_router_w, L0_ffn_routing_bias)
    return x

_drawn_inputs = setup_inputs


def setup_inputs(seed=0):
    import zlib

    import numpy as np

    out = dict(_drawn_inputs(seed))
    spreads = {'L0_ffn_routing_bias': (0.0, 0.8)}
    factors = {'L0_attn_w_q': 3.309,
     'L0_attn_w_k': 3.311,
     'L0_attn_w_v': 3.154,
     'L0_attn_w_o': 3.13,
     'L0_ffn_shared_gate': 8.0,
     'L0_ffn_shared_up': 8.0,
     'L0_ffn_shared_down': 8.0,
     'L0_ffn_gate_w': 8.0,
     'L0_ffn_up_w': 8.0,
     'L0_ffn_down_w': 8.0,
     'L0_ffn_router_w': 8.0,
     'L0_c': 2.892,
     'L0_wmod': 2.89}
    for name, (base, spread) in spreads.items():
        noise = np.random.default_rng([zlib.crc32(name.encode()), seed]).standard_normal(out[name].shape)
        drawn = base * np.exp(spread * noise) if base else spread * noise
        out[name] = jnp.asarray(drawn.astype(out[name].dtype))
    for name, factor in factors.items():
        out[name] = (out[name] * factor).astype(out[name].dtype)
    return out
```

```python
from contextlib import ExitStack

import numpy as np

import concourse.bass as bass
from concourse import mybir

F32 = mybir.dt.float32
F32R = mybir.dt.float32r
BF16 = mybir.dt.bfloat16
I32 = mybir.dt.int32
U32 = mybir.dt.uint32
ALU = mybir.AluOpType
ACT = mybir.ActivationFunctionType
AX_X = mybir.AxisListType.X

P = 128
EPS = 1e-5
FLOOR = 0.25
ds = bass.ds


def product(pe, out, l_hi, l_lo, r_hi, r_lo, first=True, last=True):
    pe.matmul(out, l_hi, r_hi, start=first, stop=False)
    pe.matmul(out, l_hi, r_lo, start=False, stop=False)
    return pe.matmul(out, l_lo, r_hi, start=False, stop=last)


def hold(eng, d, semaphore, value):
    eng.wait_ge(semaphore, value)
    eng.sem_inc(d.passed, 1)


def attention_phase(nc, d, x, cT_in, wmod, wqkv, wo, mask):
    NB, S, H = x.shape
    D = P
    HC = H // P
    NT = S // P
    NBLK = S // 512
    GQ = 256
    NG = S // GQ
    SCALE = float(D) ** -0.5
    MOD_FIXED = 5
    PV_STEPS = (7, 1, 0, 0)

    with ExitStack() as ctx:
        sb = lambda n, s, t: ctx.enter_context(nc.sbuf_tensor(n, s, t))
        sem = lambda n: ctx.enter_context(nc.semaphore(n))
        bank = [ctx.enter_context(nc.psum_tensor(f"a_bank{i}", [P, 512], F32)) for i in range(8)]
        s_bank, t_bank, o_bank = bank[0:4], bank[4:6], bank[6:8]
        rows, ident = d.mod_rows, d.ident

        X = sb("X", [P, 2, NT, H], F32)
        w_hi = sb("w_hi", [P, HC, 3 * D], F32R)
        w_lo = sb("w_lo", [P, HC, 3 * D], F32R)
        wo_masked = sb("wo_masked", [P, H], F32)
        wo_hi = sb("wo_hi", [P, H], F32R)
        wo_lo = sb("wo_lo", [P, H], F32R)
        mask_i = sb("mask_i", [P, 1], I32)
        mask_f = sb("mask_f", [P, 1], F32)
        cT = sb("cT", [P, HC, NB], F32)
        ce = sb("ce", [P, HC, NB], F32)
        silu_rows = sb("silu_rows", [P, HC, NB, P], F32)
        mod_cols = sb("mod_cols", [P, 2, HC, NB], F32)
        stats = sb("stats", [P, NT, 6], F32)
        mv = sb("mv", [P, NT, 2], F32)
        veps = sb("veps", [P, NT], F32)
        rstd = sb("rstd", [P, NT], F32)
        vt = sb("vt", [P, 2, 512], F32)
        wo_gated = vt[:, 0, 0:H]
        kT_hi = sb("kT_hi", [P, S], F32R)
        kT_lo = sb("kT_lo", [P, S], F32R)
        qT_hi = sb("qT_hi", [P, S], F32R)
        qT_lo = sb("qT_lo", [P, S], F32R)
        v_hi = sb("v_hi", [P, NT, D], F32R)
        v_lo = sb("v_lo", [P, NT, D], F32R)
        q_hi = sb("q_hi", [P, 2, GQ], F32R)
        q_lo = sb("q_lo", [P, 2, GQ], F32R)
        prob = sb("prob", [P, 2, S], F32)
        xhat = prob[:, :, :].rearrange("p a (t h) -> p (a t) h", h=H)
        flat = prob[:, :, :].rearrange("p a s -> p (a s)")
        wmod_sb = flat[:, 0:HC * 6 * H].rearrange("p (k n) -> p k n", k=HC)
        w_raw = flat[:, HC * 6 * H:HC * (6 * H + 3 * D)].rearrange("p (k n) -> p k n", k=HC)
        wo_raw = flat[:, HC * (6 * H + 3 * D):HC * (6 * H + 3 * D) + H]
        pT_hi = sb("pT_hi", [P, 2, NT, GQ], F32R)
        pT_lo = sb("pT_lo", [P, 2, NT, GQ], F32R)
        hT_hi = pT_hi[:, 0, :, :].rearrange("p k q -> p (k q)").rearrange("p (c s) -> p c s", c=HC)
        hT_lo = pT_lo[:, 0, :, :].rearrange("p k q -> p (k q)").rearrange("p (c s) -> p c s", c=HC)
        oT_hi = sb("oT_hi", [P, 2, GQ], F32R)
        oT_lo = sb("oT_lo", [P, 2, GQ], F32R)
        bmax = sb("bmax", [P, 2, 4], F32)
        negmax = sb("negmax", [P, 2], F32)
        esum = sb("esum", [P, 2, 2, 4], F32)
        den = sb("den", [P, 2, 2], F32)
        rden = sb("rden", [P, 2, 2], F32)

        w_loaded = sem("w_loaded")
        x_loaded = sem("x_loaded")
        x1_stored = sem("x1_stored")
        exp_c = sem("exp_c")
        silu_c = sem("silu_c")
        w_split = sem("w_split")
        mod_mm = sem("mod_mm")
        mod_out = sem("mod_out")
        mod_fix = sem("mod_fix")
        stats_done = sem("stats_done")
        mv_done = sem("mv_done")
        veps_done = sem("veps_done")
        rstd_done = sem("rstd_done")
        xhat_done = sem("xhat_done")
        hT_mm = sem("hT_mm")
        vt_done = sem("vt_done")
        hT_hi_done = sem("hT_hi_done")
        hT_lo_done = sem("hT_lo_done")
        qkv_mm = sem("qkv_mm")
        qkv_hi = sem("qkv_hi")
        qkv_lo = sem("qkv_lo")
        q_copied = sem("q_copied")
        s_mm = sem("s_mm")
        bmax_done = sem("bmax_done")
        negmax_done = sem("negmax_done")
        exp_done = sem("exp_done")
        pT_mm = sem("pT_mm")
        pT_hi_done = sem("pT_hi_done")
        pT_lo_done = sem("pT_lo_done")
        den_done = sem("den_done")
        rden_done = sem("rden_done")
        o_mm = sem("o_mm")
        oT_hi_done = sem("oT_hi_done")
        oT_lo_done = sem("oT_lo_done")
        y_mm = sem("y_mm")
        wo_split = sem("wo_split")
        x1_done = sem("x1_done")

        x_v = x.rearrange("b (t p) h -> b p t h", p=P)
        x1_v = d.x1.rearrange("(b t p) h -> b p t h", p=P, t=NT)
        block = ctx.enter_context(nc.Block())

        def groups(eng, G0, body):
            body(0, G0, 0, 0)
            body(1, G0 + 1, 1, 1)
            with eng.Fori(2, NG - 2, 2) as g:
                body(2, G0 + g, 0, g)
                body(3, G0 + (g + 1), 1, g + 1)
            body(NG - 2, G0 + (NG - 2), 0, NG - 2)
            body(NG - 1, G0 + (NG - 1), 1, NG - 1)

        def qkv_places(k):
            t = slice(512 * k, 512 * k + 512)
            return [(bank[k % 2][:], (kT_hi[:, t], kT_lo[:, t])),
                    (bank[2 + k % 2][:], (qT_hi[:, t], qT_lo[:, t])),
                    (bank[6 + k % 2][:].rearrange("p (t d) -> p t d", d=D),
                     (v_hi[:, 4 * k:4 * k + 4, :], v_lo[:, 4 * k:4 * k + 4, :]))]

        @block.sync
        def _(sp):
            sp.dma_start(cT[:], cT_in).then_inc(w_loaded, 16)
            sp.dma_start(wmod_sb, wmod.rearrange("(k p) n -> p k n", p=P)).then_inc(w_loaded, 16)
            sp.dma_start(w_raw, wqkv).then_inc(w_loaded, 16)
            sp.dma_start(wo_raw, wo).then_inc(w_loaded, 16)
            sp.dma_start(mask_i[:], mask).then_inc(w_loaded, 16)
            sp.dma_start(X[:, 0], x_v[0]).then_inc(x_loaded, 16)
            for b in range(NB):
                if b + 1 < NB:
                    if b >= 1:
                        sp.wait_ge(x1_stored, 16 * NG * b)
                        sp.wait_ge(d.stats1_done, NT * b)
                    sp.wait_ge(x_loaded, 16 * (b + 1))
                    sp.dma_start(X[:, (b + 1) % 2], x_v[b + 1]).then_inc(x_loaded, 16)
                else:
                    sp.sem_inc(x_loaded, 16)
                with sp.Fori(0, NG) as g:
                    sp.wait_ge(x1_done, 2 * (NG * b + g) + 2)
                    sp.dma_start(x1_v[b, :, ds(2 * g, 2), :],
                                 X[:, b % 2, ds(2 * g, 2), :]).then_inc(x1_stored, 16)
            sp.wait_ge(x1_stored, 16 * NG * NB)

        @block.gpsimd
        def _(pool):
            def deviations(n):
                hold(pool, d, mv_done, NT * n + NT)
                pool.tensor_scalar(veps[:], mv[:, :, 1], EPS, None, ALU.add).then_inc(veps_done, 1)
                pool.wait_ge(veps_done, n + 1)
                pool.tensor_tensor(rstd[:], veps[:], d.minus_half[:], ALU.pow).then_inc(rstd_done, 1)

            deviations(0)
            with pool.Fori(0, NB) as b:
                def queries(k, G, par, g):
                    if k >= 2:
                        hold(pool, d, s_mm, 8 * G - 8)
                    pool.tensor_copy(q_hi[:, par, :], qT_hi[:, ds(GQ * g, GQ)]).then_inc(q_copied, 1)
                    pool.tensor_copy(q_lo[:, par, :], qT_lo[:, ds(GQ * g, GQ)]).then_inc(q_copied, 1)

                hold(pool, d, qkv_lo, 12 * b + 12)
                groups(pool, NG * b, queries)
                deviations(b + 1)

        @block.scalar
        def _(act):
            act.wait_ge(w_loaded, 80)
            act.activation(ce[:], cT[:], ACT.Exp, scale=-1.0).then_inc(exp_c, 1)
            for i in range(2 * NB):
                act.wait_ge(mod_mm, i + 1)
                act.activation(rows[:, i // 2, 512 * (i % 2):512 * (i % 2) + 512], bank[i % 4][:],
                               ACT.Copy).then_inc(mod_out, 1)
            act.wait_ge(mod_fix, MOD_FIXED)
            with act.Fori(0, NB) as b:
                def rows_T(f):
                    c = f % 2
                    hold(act, d, hT_mm, 8 * b + f + 1)
                    if f >= 2:
                        hold(act, d, hT_lo_done, 8 * b + f - 1)
                    act.activation(vt[:, f % 2, :], t_bank[f % 2][:], ACT.Identity,
                                   scale=mod_cols[:, 1, c, ds(b, 1)], bias=mod_cols[:, 0, c, ds(b, 1)]
                                   ).then_inc(vt_done, 1)
                    act.wait_ge(vt_done, 8 * b + f + 1)
                    act.activation(hT_hi[:, c, 512 * (f // 2):512 * (f // 2) + 512], vt[:, f % 2, :],
                                   ACT.Copy).then_inc(hT_hi_done, 1)

                def qkv_high(k):
                    for m, (src, dst) in enumerate(qkv_places(k)):
                        act.wait_ge(qkv_mm, 12 * b + 3 * k + m + 1)
                        act.activation(dst[0], src, ACT.Copy, scale=SCALE if m == 1 else 1.0
                                       ).then_inc(qkv_hi, 1)

                for k in range(NBLK):
                    rows_T(2 * k)
                    rows_T(2 * k + 1)
                    if k:
                        qkv_high(k - 1)
                qkv_high(NBLK - 1)

                def exps(G, par, c, j):
                    t = 2 * G + c
                    act.wait_ge(s_mm, 4 * t + j + 1)
                    if j == 0:
                        act.wait_ge(negmax_done, t + 1)
                    act.activation(prob[:, c, 512 * j:512 * j + 512], s_bank[j][:], ACT.Exp,
                                   bias=negmax[:, c:c + 1], accum_out=esum[:, par, c, j:j + 1]
                                   ).then_inc(exp_done, 1)

                def high(G, par, c, j):
                    act.wait_ge(pT_mm, 4 * (2 * G + c) + j + 1)
                    act.activation(pT_hi[:, par, 4 * j:4 * j + 4, P * c:P * c + P],
                                   t_bank[j % 2][:].rearrange("p (k q) -> p k q", q=P),
                                   ACT.Copy).then_inc(pT_hi_done, 1)

                def output_high(G, par):
                    act.wait_ge(o_mm, G + 1)
                    act.activation(oT_hi[:, par, :], o_bank[par][:, 0:GQ],
                                   ACT.Copy).then_inc(oT_hi_done, 1)

                def body(k, G, par, g):
                    if k >= 2:
                        output_high(G - 2, par)
                    for c in range(2):
                        exps(G, par, c, 0)
                        for j in range(1, 4):
                            exps(G, par, c, j)
                            high(G, par, c, j - 1)
                        high(G, par, c, 3)

                groups(act, NG * b, body)
                output_high(NG * b + (NG - 2), 0)
                output_high(NG * b + (NG - 1), 1)

        @block.tensor
        def _(pe):
            pe.wait_ge(d.s_const, d.n_const)
            pe.wait_ge(silu_c, 4)
            for i in range(2 * NB):
                if i >= 4:
                    pe.wait_ge(mod_out, i - 3)
                for k in range(HC):
                    mm = pe.matmul(bank[i % 4][:], silu_rows[:, k, i // 2, :],
                                   wmod_sb[:, k, 2 * H + 512 * (i % 2):2 * H + 512 * (i % 2) + 512],
                                   start=(k == 0), stop=(k == HC - 1))
                mm.then_inc(mod_mm, 1)
            for w in range(2):
                for hc in range(HC):
                    for k in range(HC):
                        o = w * H + hc * P
                        mm = pe.matmul(bank[4][:, (w * HC + hc) * NB:(w * HC + hc + 1) * NB],
                                       wmod_sb[:, k, o:o + P], silu_rows[:, k, :, 0],
                                       start=(k == 0), stop=(k == HC - 1))
            mm.then_inc(mod_mm, 1)
            pe.wait_ge(w_split, 4)
            pe.wait_ge(mod_fix, MOD_FIXED)
            with pe.Fori(0, NB) as b:
                def rows_T(f):
                    pe.wait_ge(xhat_done, NT * b + 4 * (f // 2 + 1))
                    if f >= 2:
                        pe.wait_ge(vt_done, 8 * b + f - 1)
                    for i in range(4):
                        mm = pe.transpose(t_bank[f % 2][:, P * i:P * i + P],
                                          xhat[:, 4 * (f // 2) + i, P * (f % 2):P * (f % 2) + P], ident[:])
                    mm.then_inc(hT_mm, 1)

                def qkv(k):
                    pe.wait_ge(hT_lo_done, 8 * b + 2 * k + 2)
                    if k >= 2:
                        pe.wait_ge(qkv_lo, 12 * b + 3 * (k - 1))
                    t = slice(512 * k, 512 * k + 512)
                    for m, out in ((1, bank[k % 2]), (0, bank[2 + k % 2])):
                        for c in range(HC):
                            mm = product(pe, out[:], w_hi[:, c, m * D:m * D + D], w_lo[:, c, m * D:m * D + D],
                                         hT_hi[:, c, t], hT_lo[:, c, t], c == 0, c == HC - 1)
                        mm.then_inc(qkv_mm, 1)
                    for i in range(4):
                        ti = slice(512 * k + P * i, 512 * k + P * i + P)
                        for c in range(HC):
                            mm = product(pe, bank[6 + k % 2][:, P * i:P * i + P],
                                         hT_hi[:, c, ti], hT_lo[:, c, ti],
                                         w_hi[:, c, 2 * D:3 * D], w_lo[:, c, 2 * D:3 * D], c == 0, c == HC - 1)
                    mm.then_inc(qkv_mm, 1)

                for k in range(NBLK):
                    rows_T(2 * k)
                    rows_T(2 * k + 1)
                    if k:
                        qkv(k - 1)
                qkv(NBLK - 1)

                def scores(G, par, c, j):
                    if j == 0 and c == 0:
                        pe.wait_ge(q_copied, 2 * G + 2)
                    mm = product(pe, s_bank[j][:], q_hi[:, par, P * c:P * c + P], q_lo[:, par, P * c:P * c + P],
                                 kT_hi[:, 512 * j:512 * j + 512], kT_lo[:, 512 * j:512 * j + 512])
                    mm.then_inc(s_mm, 1)

                def turn(G, c, j, fresh):
                    t = 2 * G + c
                    if not fresh:
                        pe.wait_ge(pT_lo_done, 4 * t + j - 1)
                    for i in range(4):
                        k = 4 * j + i
                        mm = pe.transpose(t_bank[j % 2][:, P * i:P * i + P],
                                          prob[:, c, P * k:P * k + P], ident[:])
                    mm.then_inc(pT_mm, 1)

                def values(k_group, G, par, k0, n):
                    if k0 == 0:
                        pe.wait_ge(pT_lo_done, 8 * G + 8)
                        if k_group >= 2:
                            pe.wait_ge(x1_done, 2 * G - 2)
                    for k in range(k0, k0 + n):
                        mm = product(pe, o_bank[par][:, 0:GQ], v_hi[:, k, :], v_lo[:, k, :],
                                     pT_hi[:, par, k, :], pT_lo[:, par, k, :], k == 0, k == NT - 1)
                    if k0 + n == NT:
                        mm.then_inc(o_mm, 1)

                def project(G, par):
                    pe.wait_ge(oT_lo_done, G + 1)
                    pe.wait_ge(wo_split, 3 * b + 3)
                    for c in range(2):
                        mm = product(pe, o_bank[par][:, H * c:H * c + H], oT_hi[:, par, P * c:P * c + P],
                                     oT_lo[:, par, P * c:P * c + P], wo_hi[:], wo_lo[:])
                    mm.then_inc(y_mm, 1)

                def body(k, G, par, g):
                    done = 0
                    for c in range(2):
                        for j in range(4):
                            if k >= 1 and PV_STEPS[j]:
                                values(k - 1, G - 1, 1 - par, done, PV_STEPS[j])
                                done += PV_STEPS[j]
                            pe.wait_ge(exp_done, 4 * (2 * G + c) + j + 1)
                            turn(G, c, j, k == 0 and c == 0 and j < 2)
                            if c == 0:
                                scores(G, par, 1, j)
                            elif k < NG - 1:
                                scores(G + 1, 1 - par, 0, j)
                            if k >= 2 and c == 0 and j == 1:
                                project(G - 2, par)

                pe.wait_ge(qkv_lo, 12 * b + 12)
                for j in range(4):
                    scores(NG * b, 0, 0, j)
                groups(pe, NG * b, body)
                values(NG - 1, NG * b + (NG - 1), 1, 0, NT)
                project(NG * b + (NG - 2), 0)
                project(NG * b + (NG - 1), 1)
                pe.wait_ge(x1_done, 2 * NG * b + 2 * NG)

        @block.vector
        def _(dve):
            dve.wait_ge(w_loaded, 80)
            dve.tensor_copy(w_hi[:], w_raw).then_inc(w_split, 1)
            dve.tensor_copy(mask_f[:], mask_i[:]).then_inc(w_split, 1)
            dve.wait_ge(w_split, 2)
            dve.tensor_scalar(wo_masked[:], wo_raw, mask_f[:], None, ALU.mult).then_inc(w_split, 1)
            dve.wait_ge(exp_c, 1)
            dve.tensor_scalar(ce[:], ce[:], 1.0, None, ALU.add).then_inc(silu_c, 1)
            dve.wait_ge(silu_c, 1)
            dve.reciprocal(ce[:], ce[:]).then_inc(silu_c, 1)
            dve.wait_ge(silu_c, 2)
            dve.tensor_tensor(cT[:], cT[:], ce[:], ALU.mult).then_inc(silu_c, 1)
            dve.wait_ge(silu_c, 3)
            dve.tensor_copy(silu_rows[:], cT[:].unsqueeze(3).to_broadcast([P, HC, NB, P])).then_inc(silu_c, 1)
            dve.tensor_tensor(w_lo[:], w_raw, w_hi[:].bitcast(F32), ALU.subtract).then_inc(w_split, 1)
            dve.wait_ge(w_split, 4)
            dve.wait_ge(mod_mm, 2 * NB + 1)
            cols = bank[4][:, 0:2 * HC * NB].rearrange("p (w c b) -> p w c b", w=2, c=HC)
            dve.tensor_copy(mod_cols[:, 0], cols[:, 0]).then_inc(mod_fix, 1)
            dve.tensor_scalar(mod_cols[:, 1], cols[:, 1], 1.0, None, ALU.add).then_inc(mod_fix, 1)
            dve.wait_ge(mod_out, 2 * NB)
            dve.tensor_scalar(rows[:, :, 2 * H:3 * H], rows[:, :, 2 * H:3 * H], 1.0, None,
                              ALU.add).then_inc(mod_fix, 1)
            mag = vt[:, :, :].rearrange("p a (b h) -> p (a b) h", h=H)
            for n, o in enumerate((0, 3 * H)):
                gate = rows[:, :, o:o + H]
                dve.wait_ge(mod_fix, 3 + n)
                dve.scalar_tensor_tensor(out=mag, in0=gate, scalar=-1.0, in1=gate, op0=ALU.mult,
                                         op1=ALU.max).then_inc(d.s_gate, 1)
                dve.wait_ge(d.s_gate, 3 * n + 1)
                dve.tensor_scalar(gate, gate, 0.0, 2.0, ALU.is_ge, ALU.mult).then_inc(d.s_gate, 1)
                dve.tensor_scalar(mag, mag, FLOOR, None, ALU.max).then_inc(d.s_gate, 1)
                dve.wait_ge(d.s_gate, 3 * n + 3)
                dve.scalar_tensor_tensor(out=gate, in0=gate, scalar=1.0, in1=mag, op0=ALU.subtract,
                                         op1=ALU.mult).then_inc(mod_fix, 1)

            def aggregate(n):
                hold(dve, d, stats_done, NT * n + NT)
                for t in range(NT):
                    dve.bn_aggr(mv[:, t, :], stats[:, t, :]).then_inc(mv_done, 1)

            def normalise(n, buffer):
                dve.wait_ge(rstd_done, n + 1)
                for t in range(NT):
                    dve.tensor_scalar(xhat[:, t, :], X[:, buffer, t, :], mv[:, t, 0:1], rstd[:, t:t + 1],
                                      ALU.subtract, ALU.mult).then_inc(xhat_done, 1)

            dve.wait_ge(x_loaded, 16)
            for t in range(NT):
                dve.bn_stats(stats[:, t, :], X[:, 0, t, :]).then_inc(stats_done, 1)
            aggregate(0)
            normalise(0, 0)
            with dve.Fori(0, NB) as b:
                xb = b & 1

                def rows_low(f):
                    dve.wait_ge(hT_hi_done, 8 * b + f + 1)
                    t = slice(512 * (f // 2), 512 * (f // 2) + 512)
                    dve.tensor_tensor(hT_lo[:, f % 2, t], vt[:, f % 2, :], hT_hi[:, f % 2, t].bitcast(F32),
                                      ALU.subtract).then_inc(hT_lo_done, 1)

                def qkv_low(k):
                    for m, (src, dst) in enumerate(qkv_places(k)):
                        dve.wait_ge(qkv_hi, 12 * b + 3 * k + m + 1)
                        if m == 1:
                            dve.scalar_tensor_tensor(out=dst[1], in0=src, scalar=SCALE, in1=dst[0].bitcast(F32),
                                                     op0=ALU.mult, op1=ALU.subtract).then_inc(qkv_lo, 1)
                        else:
                            dve.tensor_tensor(dst[1], src, dst[0].bitcast(F32), ALU.subtract).then_inc(qkv_lo, 1)

                for k in range(NBLK):
                    rows_low(2 * k)
                    rows_low(2 * k + 1)
                    if k:
                        qkv_low(k - 1)
                qkv_low(NBLK - 1)

                dve.tensor_tensor(wo_gated, wo_masked[:], rows[:, ds(b, 1), 0:H].rearrange("p o h -> p (o h)"),
                                  ALU.mult).then_inc(wo_split, 1)
                dve.wait_ge(wo_split, 3 * b + 1)
                dve.tensor_copy(wo_hi[:], wo_gated).then_inc(wo_split, 1)
                dve.wait_ge(wo_split, 3 * b + 2)
                dve.tensor_tensor(wo_lo[:], wo_gated, wo_hi[:].bitcast(F32), ALU.subtract).then_inc(wo_split, 1)

                def block_max(G, c, j):
                    t = 2 * G + c
                    dve.wait_ge(s_mm, 4 * t + j + 1)
                    dve.tensor_reduce(bmax[:, c, j:j + 1], s_bank[j][:], AX_X, ALU.max).then_inc(bmax_done, 1)
                    if j == 3:
                        dve.wait_ge(bmax_done, 4 * t + 4)
                        dve.tensor_reduce(negmax[:, c:c + 1], bmax[:, c, :], AX_X, ALU.max,
                                          negate=True).then_inc(negmax_done, 1)

                def low(G, par, c, j):
                    dve.wait_ge(pT_hi_done, 4 * (2 * G + c) + j + 1)
                    o = (slice(None), par, slice(4 * j, 4 * j + 4), slice(P * c, P * c + P))
                    dve.tensor_tensor(pT_lo[o], t_bank[j % 2][:].rearrange("p (k q) -> p k q", q=P),
                                      pT_hi[o].bitcast(F32), ALU.subtract).then_inc(pT_lo_done, 1)

                def denominators(G, par):
                    dve.wait_ge(exp_done, 8 * G + 8)
                    dve.tensor_reduce(den[:, par, :], esum[:, par, :, :], AX_X, ALU.add).then_inc(den_done, 1)
                    dve.wait_ge(den_done, G + 1)
                    dve.reciprocal(rden[:, par, :], den[:, par, :]).then_inc(rden_done, 1)

                def output_low(G, par):
                    dve.wait_ge(oT_hi_done, G + 1)
                    dve.tensor_tensor(oT_lo[:, par, :], o_bank[par][:, 0:GQ],
                                      oT_hi[:, par, :].bitcast(F32), ALU.subtract).then_inc(oT_lo_done, 1)

                def residual(G, par, g):
                    dve.wait_ge(y_mm, G + 1)
                    dve.wait_ge(rden_done, G + 1)
                    tile = lambda c: X[:, ds(xb, 1), ds(2 * g + c, 1), :].rearrange("p o t h -> p (o t h)")
                    for c in range(2):
                        dve.scalar_tensor_tensor(out=tile(c), in0=o_bank[par][:, H * c:H * c + H],
                                                 scalar=rden[:, par, c:c + 1], in1=tile(c),
                                                 op0=ALU.mult, op1=ALU.add).then_inc(x1_done, 1)
                    for c in range(2):
                        hold(dve, d, x1_done, 2 * G + c + 1)
                        dve.bn_stats(d.stats1[:, ds(2 * G + c, 1), :], tile(c)).then_inc(d.stats1_done, 1)

                def next_statistics(k, g):
                    if k == 0:
                        hold(dve, d, x_loaded, 16 * b + 32)
                    for i in range(2):
                        st = stats[:, ds(2 * g + i, 1), :]
                        dve.bn_stats(st, X[:, ds(1 - xb, 1), ds(2 * g + i, 1), :]).then_inc(stats_done, 1)

                def body(k, G, par, g):
                    next_statistics(k, g)
                    if k >= 1:
                        denominators(G - 1, 1 - par)
                    if k >= 2:
                        output_low(G - 2, par)
                    if k == NG - 1:
                        aggregate(b + 1)
                    for c in range(2):
                        if k >= 2 and c == 1:
                            residual(G - 2, par, g - 2)
                        for j in range(4):
                            if c == 0:
                                block_max(G, 1, j)
                            elif k < NG - 1:
                                block_max(G + 1, 0, j)
                            low(G, par, c, j)

                for j in range(4):
                    block_max(NG * b, 0, j)
                groups(dve, NG * b, body)
                normalise(b + 1, ds(1 - xb, 1))
                denominators(NG * b + (NG - 1), 1)
                output_low(NG * b + (NG - 2), 0)
                output_low(NG * b + (NG - 1), 1)
                residual(NG * b + (NG - 2), 0, NG - 2)
                residual(NG * b + (NG - 1), 1, NG - 1)


class Namespace:
    pass


def inside(n, count):
    return not isinstance(n, int) or 0 <= n < count


def split_weights(eng, raw, hi, lo, done, n):
    eng.tensor_copy(hi, raw).then_inc(done, 1)
    eng.wait_ge(done, n + 1)
    eng.tensor_tensor(lo, raw, hi.bitcast(F32), ALU.subtract).then_inc(done, 1)


def gated_blocks(ctx, nc, d, tag, count, H, I):
    HC, IC = H // P, I // P
    f = Namespace()
    sb = lambda n, s, t: ctx.enter_context(nc.sbuf_tensor(f"{tag}_{n}", s, t))
    sem = lambda n: ctx.enter_context(nc.semaphore(f"{tag}_{n}"))
    f.bank = [ctx.enter_context(nc.psum_tensor(f"{tag}_bank{i}", [P, 512], F32)) for i in range(8)]
    g_bank, u_bank, a_bank, x_bank = f.bank[0:4]
    f.y_bank = f.bank[4:6]
    xT_hi, xT_lo = sb("xT_hi", [P, 2, HC, P], F32R), sb("xT_lo", [P, 2, HC, P], F32R)
    f.xT_hi, f.xT_lo = xT_hi, xT_lo
    silu_g, prod = sb("silu_g", [P, 2, I], F32), sb("prod", [P, 2, I], F32)
    aT_hi, aT_lo = sb("aT_hi", [P, 2, IC, P], F32R), sb("aT_lo", [P, 2, IC, P], F32R)
    f.xT_mm, f.xT_hi_done, f.xT_lo_done = sem("xT_mm"), sem("xT_hi_done"), sem("xT_lo_done")
    f.gate_mm, f.up_mm, f.silu_done, f.prod_done = sem("gate_mm"), sem("up_mm"), sem("silu_done"), sem("prod_done")
    f.aT_mm, f.aT_hi_done, f.aT_lo_done = sem("aT_mm"), sem("aT_hi_done"), sem("aT_lo_done")
    f.y_mm, f.y_out, f.rows_ready = sem("y_mm"), sem("y_out"), sem("rows_ready")
    flat = lambda t, par: t[:, par, :, :].rearrange("p c t -> p (c t)")

    def pe_turn_rows(pe, m, par, rows):
        pe.wait_ge(f.rows_ready, f.ready_at(m))
        if inside(m - 1, count):
            pe.wait_ge(f.xT_lo_done, m)
        for c in range(HC):
            mm = pe.transpose(x_bank[:, P * c:P * c + P], rows[:, P * c:P * c + P], d.ident[:])
        mm.then_inc(f.xT_mm, 1)

    def pe_turn_products(pe, m, par):
        pe.wait_ge(f.prod_done, m + 1)
        if inside(m - 1, count):
            pe.wait_ge(f.aT_lo_done, m)
        for c in range(IC):
            mm = pe.transpose(a_bank[:, P * c:P * c + P], prod[:, par, P * c:P * c + P], d.ident[:])
        mm.then_inc(f.aT_mm, 1)

    def pe_gate_up(pe, m, par, weights):
        pe.wait_ge(f.xT_lo_done, m + 1)
        for out, hi, lo, done in ((g_bank, *weights[0], f.gate_mm), (u_bank, *weights[1], f.up_mm)):
            for c in range(HC):
                mm = product(pe, out[:, 0:I], xT_hi[:, par, c, :], xT_lo[:, par, c, :], hi(c), lo(c),
                             c == 0, c == HC - 1)
            mm.then_inc(done, 1)

    def pe_down(pe, m, par, weights):
        pe.wait_ge(f.aT_lo_done, m + 1)
        if inside(m - 2, count):
            pe.wait_ge(f.y_out, m - 1)
        hi, lo = weights[2]
        for c in range(IC):
            mm = product(pe, f.y_bank[par][:, 0:H], aT_hi[:, par, c, :], aT_lo[:, par, c, :], hi(c), lo(c),
                         c == 0, c == IC - 1)
        mm.then_inc(f.y_mm, 1)

    def act_rows_high(act, m, par):
        act.wait_ge(f.xT_mm, m + 1)
        act.activation(flat(xT_hi, par), x_bank[:, 0:H], ACT.Copy).then_inc(f.xT_hi_done, 1)

    def act_products_high(act, m, par):
        act.wait_ge(f.aT_mm, m + 1)
        act.activation(flat(aT_hi, par), a_bank[:, 0:I], ACT.Copy).then_inc(f.aT_hi_done, 1)

    def act_silu(act, m, par):
        act.wait_ge(f.gate_mm, m + 1)
        act.activation(silu_g[:, par, :], g_bank[:, 0:I], ACT.Silu).then_inc(f.silu_done, 1)

    def dve_rows_low(dve, m, par):
        dve.wait_ge(f.xT_hi_done, m + 1)
        dve.tensor_tensor(flat(xT_lo, par), x_bank[:, 0:H], flat(xT_hi, par).bitcast(F32),
                          ALU.subtract).then_inc(f.xT_lo_done, 1)

    def dve_products_low(dve, m, par):
        dve.wait_ge(f.aT_hi_done, m + 1)
        dve.tensor_tensor(flat(aT_lo, par), a_bank[:, 0:I], flat(aT_hi, par).bitcast(F32),
                          ALU.subtract).then_inc(f.aT_lo_done, 1)

    def dve_products(dve, m, par):
        dve.wait_ge(f.silu_done, m + 1)
        dve.wait_ge(f.up_mm, m + 1)
        dve.tensor_tensor(prod[:, par, :], silu_g[:, par, :], u_bank[:, 0:I], ALU.mult).then_inc(f.prod_done, 1)

    f.pe_turn_rows, f.pe_turn_products, f.pe_gate_up, f.pe_down = pe_turn_rows, pe_turn_products, pe_gate_up, pe_down
    f.act_rows_high, f.act_products_high, f.act_silu = act_rows_high, act_products_high, act_silu
    f.dve_rows_low, f.dve_products_low, f.dve_products = dve_rows_low, dve_products_low, dve_products
    return f


def shared_phase(nc, d, x1, shared_gate, shared_up, shared_down, router_w, router_bias):
    N, H = x1.shape
    I = shared_gate.shape[2]
    HC, IC = H // P, I // P
    E = d.E
    NB = d.NB
    NT = N // P
    TB = NT // NB
    Z, rows = d.Z, d.mod_rows

    with ExitStack() as ctx:
        sb = lambda n, s, t: ctx.enter_context(nc.sbuf_tensor(n, s, t))
        sem = lambda n: ctx.enter_context(nc.semaphore(n))
        f = gated_blocks(ctx, nc, d, "s", NT, H, I)
        f.ready_at = lambda m: m + 1
        l_bank, r_bank = f.bank[6], f.bank[7]

        sg_hi, sg_lo = sb("sg_hi", [P, HC, I], F32R), sb("sg_lo", [P, HC, I], F32R)
        su_hi, su_lo = sb("su_hi", [P, HC, I], F32R), sb("su_lo", [P, HC, I], F32R)
        sd_hi, sd_lo = sb("sd_hi", [P, IC, H], F32R), sb("sd_lo", [P, IC, H], F32R)
        rw_raw = sb("rw_raw", [P, HC, E], F32)
        rw_hi, rw_lo = sb("rw_hi", [P, HC, E], F32R), sb("rw_lo", [P, HC, E], F32R)
        bias = sb("bias", [P, E], F32)
        h_rows = sb("h_rows", [P, 2, TB, H], F32)
        w_raw = h_rows[:, 1, :, :].rearrange("p t h -> p (t h)")
        raw = lambda o, a, b: w_raw[:, o:o + a * b].rearrange("p (a b) -> p a b", a=a)
        sg_raw, su_raw, sd_raw = raw(0, HC, I), raw(HC * I, HC, I), raw(2 * HC * I, IC, H)
        h = sb("h", [P, 2, H], F32)
        norm = sb("norm", [P, 2, H], F32)
        scaled = sb("scaled", [P, 2, H], F32)
        gy = sb("gy", [P, 2, H], F32)
        mv = sb("s_mv", [P, NT, 2], F32)
        veps = sb("s_veps", [P, NT], F32)
        rstd = sb("s_rstd", [P, NT], F32)
        three = lambda n, t=F32: sb(n, [P, TB, E], t)
        logits, probs = three("logits"), three("probs")
        same, coded, pick1, rest, pick2, chosen = (three(n) for n in ("same", "coded", "pick1", "rest", "pick2", "chosen"))
        chosen_bf = three("chosen_bf", BF16)
        slot = three("slot")
        best1, code1, best2, code2 = (sb(n, [P, TB], F32) for n in ("best1", "code1", "best2", "code2"))
        total = sb("total", [P, TB], F32)
        base = d.base

        w_loaded, x_loaded = sem("s_w_loaded"), sem("s_x_loaded")
        w_split = sem("s_w_split")
        mv_done, veps_done, rstd_done = sem("s_mv_done"), sem("s_veps_done"), sem("s_rstd_done")
        norm_done, scaled_done, copied = sem("norm_done"), sem("scaled_done"), sem("copied")
        gy_done = sem("gy_done")
        logit_mm, logit_done, prob_done = sem("logit_mm"), sem("logit_done"), sem("prob_done")
        route, rank_mm, placed = sem("route"), sem("rank_mm"), sem("placed")
        sent = sem("sent")

        z_v = x1.rearrange("(b t p) h -> b p t h", p=P, t=TB)
        block = ctx.enter_context(nc.Block())
        CHOSEN = 13
        SCORED = CHOSEN + 4
        ROUTE = SCORED + 6
        BATCH_DMA = 16 * 2 * TB

        def pairs(eng, b, step, behind_first=None):
            first = TB * b
            peeled = 4 if b == 0 else 2
            for n in range(first, first + peeled):
                step(n, n % 2, b)
                if n == first and b and behind_first:
                    behind_first(b - 1)
            with eng.Fori(peeled // 2, TB // 2 - 1) as i:
                step(2 * i + first, 0, b)
                step(2 * i + (first + 1), 1, b)
            step(first + TB - 2, 0, b)
            step(first + TB - 1, 1, b)

        def tile(n):
            return n if isinstance(n, int) else ds(n, 1)

        def span(n):
            return slice(n, n + 1) if isinstance(n, int) else ds(n, 1)

        def batch(n, b):
            return n // TB if isinstance(n, int) else b

        @block.sync
        def _(sp):
            for b in range(NB):
                sp.dma_start(Z[:, TB * b:TB * b + TB, :], z_v[b]).then_inc(x_loaded, 16)
                if b == 0:
                    for dst, src in ((sg_raw, shared_gate), (su_raw, shared_up), (sd_raw, shared_down),
                                     (rw_raw[:], router_w), (bias[:], router_bias.to_broadcast([P, E]))):
                        sp.dma_start(dst, src).then_inc(w_loaded, 16)
                sp.wait_ge(x_loaded, 16 * (b + 1))

        def dispatch(pool, b):
            pool.wait_ge(placed, 2 * b + 2)
            pool.wait_ge(copied, TB * (b + 1))
            for t in range(TB):
                for k in range(2):
                    pool.indirect_dma_start(
                        d.x_rows, bass.IndirectOffsetOnAxis(ap=d.place_i[:, k, TB * b + t:TB * b + t + 1], axis=0),
                        h_rows[:, b % 2, t, :], None).then_inc(sent, 16)

        @block.gpsimd
        def _(pool):
            for b in range(NB):
                tb = slice(TB * b, TB * b + TB)
                pool.wait_ge(mv_done, TB * (b + 1))
                pool.tensor_scalar(veps[:, tb], mv[:, tb, 1], EPS, None, ALU.add).then_inc(veps_done, 1)
                pool.wait_ge(veps_done, b + 1)
                pool.tensor_tensor(rstd[:, tb], veps[:, tb], d.minus_half[:], ALU.pow).then_inc(rstd_done, 1)
            for b in range(NB - 1):
                dispatch(pool, b)
            dispatch(pool, NB - 1)
            pool.wait_ge(sent, BATCH_DMA * NB)

        @block.scalar
        def _(act):
            def copy_rows(m, par, b):
                act.wait_ge(f.rows_ready, m + 1)
                if isinstance(m, int) and m % TB == 0 and b >= 2:
                    act.wait_ge(sent, BATCH_DMA * (b - 1))
                act.activation(h_rows[:, b % 2, tile(m - TB * b), :], h[:, par, :], ACT.Copy).then_inc(copied, 1)

            def step(n, par, b):
                if inside(n - 1, NT):
                    f.act_products_high(act, n - 1, 1 - par)
                if inside(n + 1, NT):
                    f.act_rows_high(act, n + 1, 1 - par)
                f.act_silu(act, n, par)
                if inside(n + 2, NT):
                    copy_rows(n + 2, par, batch(n + 2, b))

            copy_rows(0, 0, 0)
            copy_rows(1, 1, 0)
            f.act_rows_high(act, 0, 0)
            for b in range(NB):
                pairs(act, b, step)
                act.wait_ge(logit_done, TB * (b + 1))
                act.activation(probs[:], logits[:], ACT.Sigmoid).then_inc(prob_done, 1)
            f.act_products_high(act, NT - 1, (NT - 1) % 2)

        @block.tensor
        def _(pe):
            weights = [(lambda c: sg_hi[:, c, :], lambda c: sg_lo[:, c, :]),
                       (lambda c: su_hi[:, c, :], lambda c: su_lo[:, c, :]),
                       (lambda c: sd_hi[:, c, :], lambda c: sd_lo[:, c, :])]

            def router(n, par):
                if inside(n - 1, NT):
                    pe.wait_ge(logit_done, n)
                for c in range(HC):
                    mm = product(pe, l_bank[:, 0:E], f.xT_hi[:, par, c, :], f.xT_lo[:, par, c, :],
                                 rw_hi[:, c, :], rw_lo[:, c, :], c == 0, c == HC - 1)
                mm.then_inc(logit_mm, 1)

            def step(n, par, b):
                if inside(n - 2, NT):
                    f.pe_down(pe, n - 2, par, weights)
                if inside(n - 1, NT):
                    f.pe_turn_products(pe, n - 1, 1 - par)
                if inside(n + 1, NT):
                    f.pe_turn_rows(pe, n + 1, 1 - par, h[:, 1 - par, :])
                f.pe_gate_up(pe, n, par, weights)
                router(n, par)

            def ranks(b):
                pe.wait_ge(route, ROUTE * b + CHOSEN)
                flat = chosen_bf[:, :, :].rearrange("p t e -> p (t e)")
                W = TB * E
                pe.matmul(r_bank[:, 0:W], d.before[:], flat, start=True, stop=False)
                for s in range(1, TB):
                    pe.matmul(r_bank[:, E * s:W], d.ones[:], flat[:, 0:W - E * s], start=False, stop=s == TB - 1)
                for t in range(TB):
                    mm = pe.matmul(r_bank[:, W:W + E], d.ones[:], flat[:, E * t:E * t + E],
                                   start=(t == 0), stop=(t == TB - 1))
                mm.then_inc(rank_mm, 1)

            f.pe_turn_rows(pe, 0, 0, h[:, 0, :])
            pe.wait_ge(w_split, 8)
            for b in range(NB):
                pairs(pe, b, step, ranks)
            ranks(NB - 1)
            f.pe_down(pe, NT - 2, NT % 2, weights)
            f.pe_turn_products(pe, NT - 1, (NT - 1) % 2)
            f.pe_down(pe, NT - 1, (NT - 1) % 2, weights)


        @block.vector
        def _(dve):
            def normalise(m, par, b):
                if isinstance(m, int) and m % TB == 0:
                    dve.wait_ge(rstd_done, b + 1)
                    dve.wait_ge(x_loaded, 16 * (b + 1))
                dve.tensor_scalar(norm[:, par, :], Z[:, tile(m), :], mv[:, tile(m), 0:1], rstd[:, span(m)],
                                  ALU.subtract, ALU.mult).then_inc(norm_done, 1)
                dve.wait_ge(norm_done, m + 1)
                dve.tensor_tensor(scaled[:, par, :], norm[:, par, :], rows[:, b, 2 * H:3 * H],
                                  ALU.mult).then_inc(scaled_done, 1)

            def shift(m, par, b):
                dve.wait_ge(scaled_done, m + 1)
                if inside(m - 2, NT):
                    dve.wait_ge(f.xT_mm, m - 1)
                    dve.wait_ge(copied, m - 1)
                dve.tensor_tensor(h[:, par, :], scaled[:, par, :], rows[:, b, H:2 * H],
                                  ALU.add).then_inc(f.rows_ready, 1)

            def add_logits(n, b):
                dve.wait_ge(logit_mm, n + 1)
                dve.tensor_tensor(logits[:, tile(n - TB * b), :], l_bank[:, 0:E], bias[:],
                                  ALU.add).then_inc(logit_done, 1)

            def gated(m, par, b):
                dve.wait_ge(f.y_mm, m + 1)
                dve.tensor_tensor(gy[:, par, :], f.y_bank[par][:, 0:H], rows[:, b, 3 * H:4 * H],
                                  ALU.mult).then_inc(f.y_out, 1)

            def shared_out(m, par):
                dve.wait_ge(f.y_out, m + 1)
                dve.tensor_tensor(Z[:, tile(m), :], gy[:, par, :], Z[:, tile(m), :], ALU.add).then_inc(gy_done, 1)

            def step(n, par, b):
                if inside(n + 2, NT):
                    normalise(n + 2, par, batch(n + 2, b))
                if inside(n - 2, NT):
                    gated(n - 2, par, batch(n - 2, b))
                if inside(n + 2, NT):
                    shift(n + 2, par, batch(n + 2, b))
                if inside(n - 2, NT):
                    shared_out(n - 2, par)
                if inside(n - 1, NT):
                    f.dve_products_low(dve, n - 1, 1 - par)
                if inside(n + 1, NT):
                    f.dve_rows_low(dve, n + 1, 1 - par)
                f.dve_products(dve, n, par)
                add_logits(n, b)

            def choose(b):
                r = [ROUTE * b]

                def op(ins):
                    ins.then_inc(route, 1)
                    r[0] += 1
                    dve.wait_ge(route, r[0])

                wide = lambda v: v[:].unsqueeze(2).to_broadcast([P, TB, E])
                codes = d.codes[:].unsqueeze(1).to_broadcast([P, TB, E])
                dve.wait_ge(prob_done, b + 1)
                op(dve.tensor_reduce(best1[:], probs[:], AX_X, ALU.max))
                op(dve.tensor_tensor(same[:], probs[:], wide(best1), ALU.is_equal))
                op(dve.tensor_tensor(coded[:], same[:], codes, ALU.mult))
                op(dve.tensor_reduce(code1[:], coded[:], AX_X, ALU.max))
                op(dve.tensor_tensor(pick1[:], coded[:], wide(code1), ALU.is_equal))
                op(dve.scalar_tensor_tensor(out=rest[:], in0=pick1[:], scalar=-4.0, in1=probs[:],
                                            op0=ALU.mult, op1=ALU.add))
                op(dve.tensor_reduce(best2[:], rest[:], AX_X, ALU.max))
                op(dve.tensor_tensor(same[:], rest[:], wide(best2), ALU.is_equal))
                op(dve.tensor_tensor(coded[:], same[:], codes, ALU.mult))
                op(dve.tensor_reduce(code2[:], coded[:], AX_X, ALU.max))
                op(dve.tensor_tensor(pick2[:], coded[:], wide(code2), ALU.is_equal))
                op(dve.tensor_tensor(chosen[:], pick1[:], pick2[:], ALU.add))
                op(dve.tensor_copy(chosen_bf[:], chosen[:]))
                assert r[0] == ROUTE * b + CHOSEN
                tb = slice(TB * b, TB * b + TB)
                op(dve.tensor_tensor(total[:], best1[:], best2[:], ALU.add))
                op(dve.reciprocal(total[:], total[:]))
                op(dve.tensor_tensor(d.score[:, 0, tb], best1[:], total[:], ALU.mult))
                op(dve.tensor_tensor(d.score[:, 1, tb], best2[:], total[:], ALU.mult))
                assert r[0] == ROUTE * b + SCORED

            def place(b):
                r = [ROUTE * b + SCORED]

                def op(ins):
                    ins.then_inc(route, 1)
                    r[0] += 1
                    dve.wait_ge(route, r[0])

                tb = slice(TB * b, TB * b + TB)
                dve.wait_ge(rank_mm, b + 1)
                W = TB * E
                op(dve.tensor_tensor(slot[:], r_bank[:, 0:W].rearrange("p (t e) -> p t e", e=E),
                                     base[:, b, :].unsqueeze(1).to_broadcast([P, TB, E]), ALU.add))
                op(dve.tensor_tensor(base[:, b + 1, :], r_bank[:, W:W + E], base[:, b, :], ALU.add))
                for k, pick in enumerate((pick1, pick2)):
                    op(dve.tensor_tensor(coded[:], slot[:], pick[:], ALU.mult))
                    op(dve.tensor_reduce(d.place[:, k, tb], coded[:], AX_X, ALU.add))
                    dve.tensor_copy(d.place_i[:, k, tb], d.place[:, k, tb]).then_inc(placed, 1)
                assert r[0] == ROUTE * (b + 1)

            for t in range(NT):
                dve.bn_aggr(mv[:, t, :], d.stats1[:, t, :]).then_inc(mv_done, 1)
            dve.tensor_copy(base[:, 0, :], d.first_row[:, 0:E]).then_inc(d.base_set, 1)
            dve.wait_ge(w_loaded, 80)
            n = 0
            for raw_w, hi, lo in ((sg_raw, sg_hi, sg_lo), (su_raw, su_hi, su_lo), (sd_raw, sd_hi, sd_lo),
                                  (rw_raw[:], rw_hi, rw_lo)):
                split_weights(dve, raw_w, hi[:], lo[:], w_split, n)
                n += 2
            for n in range(2):
                normalise(n, n, 0)
                shift(n, n, 0)
            f.dve_rows_low(dve, 0, 0)
            for b in range(NB):
                pairs(dve, b, step, place)
                choose(b)
            place(NB - 1)
            f.dve_products_low(dve, NT - 1, (NT - 1) % 2)
            for n in (NT - 2, NT - 1):
                gated(n, n % 2, NB - 1)
                shared_out(n, n % 2)


def experts_phase(nc, d, gate_w, up_w, down_w):
    E, _, HC, I = gate_w.shape
    H = HC * P
    IC = I // P
    NBLK = d.blocks
    W = HC * I

    with ExitStack() as ctx:
        sb = lambda n, s, t: ctx.enter_context(nc.sbuf_tensor(n, s, t))
        sem = lambda n: ctx.enter_context(nc.semaphore(n))
        f = gated_blocks(ctx, nc, d, "e", NBLK, H, I)
        w_raw = sb("e_w_raw", [P, 3 * W], F32)
        w_hi = sb("e_w_hi", [P, 2, 3 * W], F32R)
        w_lo = sb("e_w_lo", [P, 2, 3 * W], F32R)
        h = sb("e_h", [P, 2, H], F32)
        y = sb("e_y", [P, 2, H], F32)
        zeros = sb("zeros", [P, H], F32)
        count = sb("count", [P, E], F32)
        over = sb("over", [P, E, d.most], F32)
        nblocks = sb("nblocks", [P, E], F32)
        ends = sb("ends", [P, E], F32)
        rows_of = sb("rows_of", [P, d.place.shape[1] * d.place.shape[2]], F32)
        moved = sb("moved", [P, d.place.shape[1] * d.place.shape[2]], F32)
        starts = sb("starts", [P, E + 1], F32)
        shift = sb("shift", [P, E + 1], F32)
        jump = sb("jump", [P, E], F32)
        behind = sb("behind", [1, NBLK, E], F32)
        jumped = sb("jumped", [1, NBLK, E], F32)
        moved_by = sb("moved_by", [1, NBLK], F32)
        expert_of = sb("expert_of", [1, NBLK + 2], F32)
        packed = sb("packed", [1, 3, NBLK // 2], F32)
        row0 = sb("row0", [1, NBLK], F32)
        table = sb("table", [1, 2, NBLK], I32)
        free_i = sb("free_i", [1, E], I32)
        ends_i = sb("ends_i", [1, E], I32)

        w_loaded, w_split = sem("e_w_loaded"), sem("e_w_split")
        zeroed, padded, moving = sem("zeroed"), sem("padded"), sem("moving")
        plan = sem("plan")
        h_in = [sem("h_in0"), sem("h_in1")]
        y_stored = [sem("y_stored0"), sem("y_stored1")]
        PLAN = 20 + E
        LOG_E = E.bit_length() - 1

        block = ctx.enter_context(nc.Block())
        half = lambda m, par: m // 2 if isinstance(m, int) else (m - par) // 2

        def steps(eng, step):
            for n in range(4):
                step(n, n % 2)
            with eng.Fori(2, NBLK // 2 - 1) as i:
                step(2 * i, 0)
                step(2 * i + 1, 1)
            step(NBLK - 2, 0)
            step(NBLK - 1, 1)

        def at(m):
            return slice(m, m + 1) if isinstance(m, int) else ds(m, 1)

        def first_row(eng, m):
            return eng.value_load(table[0:1, 0, at(m)], min_val=0, max_val=d.all_rows - P)

        @block.sync
        def _(sp):
            sp.wait_ge(zeroed, 2)
            sp.wait_ge(plan, PLAN)
            for e in range(E):
                row = sp.value_load(free_i[0:1, e:e + 1], min_val=0, max_val=d.all_rows - P)
                sp.dma_start(d.x_rows[ds(row, P), :], zeros[:]).then_inc(padded, 16)
            for i in range(E):
                r = d.spare_row + P * i
                sp.dma_start(d.x_rows[r:r + P, :], zeros[:]).then_inc(padded, 16)
            sp.wait_ge(padded, 32 * E)

            def load(m, par):
                row = first_row(sp, m)
                sp.dma_start(h[:, par, :], d.x_rows[ds(row, P), :]).then_inc(h_in[par], 16)

            def store(m, par):
                sp.wait_ge(f.y_out, m + 1)
                rows = slice(P * m, P * m + P) if isinstance(m, int) else ds(P * m, P)
                sp.dma_start(d.y_rows[rows, :], y[:, par, :]).then_inc(y_stored[par], 16)

            def step(n, par):
                if inside(n + 2, NBLK):
                    hold(sp, d, f.xT_mm, n + 1)
                    load(n + 2, par)
                if inside(n - 2, NBLK):
                    store(n - 2, par)

            load(0, 0)
            load(1, 1)
            steps(sp, step)
            store(NBLK - 2, 0)
            store(NBLK - 1, 1)
            for s in y_stored:
                sp.wait_ge(s, 16 * (NBLK // 2))

        @block.gpsimd
        def _(pool):
            pool.memset(zeros[:], 0.0).then_inc(zeroed, 1)
            pool.tensor_copy(rows_of[:], d.place[:, :, :].rearrange("p k t -> p (k t)")).then_inc(zeroed, 1)
            for e in range(E):
                for m, src in enumerate((gate_w, up_w, down_w)):
                    pool.dma_start(w_raw[:, W * m:W * m + W], src[e].rearrange("p a b -> p (a b)")).then_inc(w_loaded, 16)
                if e == 0:
                    pool.wait_ge(w_split, 2)
                    continue
                pool.wait_ge(w_loaded, 48 * (e + 1))
                if e >= 2:
                    pool.wait_ge(plan, PLAN)
                    end = pool.value_load(ends_i[0:1, e - 2:e - 1], min_val=1, max_val=NBLK)
                    hold(pool, d, f.y_mm, end)
                split_weights(pool, w_raw[:], w_hi[:, e % 2, :], w_lo[:, e % 2, :], w_split, 2 * e)
                pool.wait_ge(w_split, 2 * e + 2)
            flat = d.place[:, :, :].rearrange("p k t -> p (k t)")
            for e in range(E):
                if e == 0:
                    pool.tensor_scalar(moved[:], flat, 0.0, shift[:, 0:1], ALU.is_ge, ALU.mult).then_inc(moving, 1)
                else:
                    pool.tensor_scalar(moved[:], rows_of[:], float(e * d.capacity), jump[:, e - 1:e],
                                       ALU.is_ge, ALU.mult).then_inc(moving, 1)
                pool.wait_ge(moving, 2 * e + 1)
                pool.tensor_tensor(flat, flat, moved[:], ALU.subtract).then_inc(moving, 1)
                if e < E - 1:
                    pool.wait_ge(moving, 2 * e + 2)
            pool.wait_ge(moving, 2 * E)
            pool.tensor_copy(d.place_i[:, :, :].rearrange("p k t -> p (k t)"), flat).then_inc(moving, 1)

        @block.scalar
        def _(act):
            def output(m, par):
                act.wait_ge(f.y_mm, m + 1)
                if inside(m - 2, NBLK):
                    hold(act, d, y_stored[par], 16 * half(m, par))
                act.activation(y[:, par, :], f.y_bank[par][:, 0:H], ACT.Copy).then_inc(f.y_out, 1)

            def step(n, par):
                if inside(n - 2, NBLK):
                    output(n - 2, par)
                if inside(n - 1, NBLK):
                    f.act_products_high(act, n - 1, 1 - par)
                if inside(n + 1, NBLK):
                    f.act_rows_high(act, n + 1, 1 - par)
                f.act_silu(act, n, par)

            f.act_rows_high(act, 0, 0)
            steps(act, step)
            output(NBLK - 2, 0)
            f.act_products_high(act, NBLK - 1, 1)
            output(NBLK - 1, 1)

        @block.tensor
        def _(pe):
            def weights(e):
                def columns(t, o, n):
                    return lambda c: t[:, ds(e & 1, 1), o + n * c:o + n * c + n]

                return [tuple(columns(t, W * k, n) for t in (w_hi, w_lo)) for k, n in enumerate((I, I, H))]

            def experts(i):
                packed = pe.value_load(table[0:1, 1, at(i)], min_val=0, max_val=E ** 4 - 1)
                return [(packed >> (LOG_E * k)) & (E - 1) for k in range(4)]

            def step(n, par):
                if par == 0:
                    who[:] = experts(n // 2 if isinstance(n, int) else half(n, 0))
                e = who[2 + par]
                if inside(n - 2, NBLK):
                    f.pe_down(pe, n - 2, par, weights(who[par]))
                if inside(n - 1, NBLK):
                    f.pe_turn_products(pe, n - 1, 1 - par)
                if inside(n + 1, NBLK):
                    turn_rows(n + 1, 1 - par)
                pe.wait_ge(w_split, 2 * e + 2)
                f.pe_gate_up(pe, n, par, weights(e))

            who = []
            def turn_rows(m, par):
                f.rows_ready = h_in[par]
                f.ready_at = lambda m: 16 * half(m, par) + 16
                f.pe_turn_rows(pe, m, par, h[:, par, :])

            turn_rows(0, 0)
            pe.wait_ge(plan, PLAN)
            steps(pe, step)
            f.pe_down(pe, NBLK - 2, 0, weights(who[2]))
            f.pe_turn_products(pe, NBLK - 1, 1)
            f.pe_down(pe, NBLK - 1, 1, weights(who[3]))

        @block.vector
        def _(dve):
            p = [0]

            def op(ins):
                ins.then_inc(plan, 1)
                p[0] += 1
                dve.wait_ge(plan, p[0])

            c = d.consts
            op(dve.tensor_tensor(count[:], d.base[:, d.NB, :], d.first_row[:, 0:E], ALU.subtract))
            op(dve.tensor_tensor(over[:], count[:].unsqueeze(2).to_broadcast([P, E, d.most]),
                                 c.limits[:].unsqueeze(1).to_broadcast([P, E, d.most]), ALU.is_gt))
            op(dve.tensor_reduce(nblocks[:], over[:], AX_X, ALU.add))
            op(dve.tensor_copy(ends[:], nblocks[:]))
            for e in range(1, E):
                op(dve.tensor_tensor(ends[:, e:e + 1], ends[:, e - 1:e], nblocks[:, e:e + 1], ALU.add))
            op(dve.memset(starts[:, 0:1], 0.0))
            op(dve.tensor_copy(starts[:, 1:E + 1], ends[:]))
            op(dve.scalar_tensor_tensor(out=shift[:], in0=starts[:], scalar=-float(P), in1=d.first_row[:, 0:E + 1],
                                        op0=ALU.mult, op1=ALU.add))
            op(dve.tensor_tensor(jump[:], shift[:, 1:E + 1], shift[:, 0:E], ALU.subtract))
            op(dve.tensor_tensor(behind[:], c.numbers[:].unsqueeze(2).to_broadcast([1, NBLK, E]),
                                 ends[0:1].unsqueeze(1).to_broadcast([1, NBLK, E]), ALU.is_ge))
            op(dve.tensor_tensor(jumped[:], behind[:], jump[0:1].unsqueeze(1).to_broadcast([1, NBLK, E]), ALU.mult))
            op(dve.tensor_reduce(moved_by[:], jumped[:], AX_X, ALU.add))
            op(dve.scalar_tensor_tensor(out=row0[:], in0=c.numbers[:], scalar=float(P), in1=moved_by[:],
                                        op0=ALU.mult, op1=ALU.add))
            op(dve.tensor_copy(table[:, 0], row0[:]))
            op(dve.memset(expert_of[:, 0:2], 0.0))
            op(dve.tensor_reduce(expert_of[:, 2:], behind[:, :, 0:E - 1], AX_X, ALU.add))
            by_pair = expert_of[:].rearrange("o (i two) -> o i two", two=2)
            digit = [by_pair[:, 0:NBLK // 2, 0], by_pair[:, 0:NBLK // 2, 1],
                     by_pair[:, 1:NBLK // 2 + 1, 0], by_pair[:, 1:NBLK // 2 + 1, 1]]
            so_far = digit[3]
            for k in (2, 1, 0):
                op(dve.scalar_tensor_tensor(out=packed[:, k], in0=so_far, scalar=float(E), in1=digit[k],
                                            op0=ALU.mult, op1=ALU.add))
                so_far = packed[:, k]
            op(dve.tensor_copy(table[:, 1, 0:NBLK // 2], packed[:, 0]))
            op(dve.tensor_copy(free_i[:], d.base[0:1, d.NB, :]))
            op(dve.tensor_copy(ends_i[:], ends[0:1]))
            assert p[0] == PLAN
            dve.wait_ge(w_loaded, 48)
            split_weights(dve, w_raw[:], w_hi[:, 0, :], w_lo[:, 0, :], w_split, 0)

            def step(n, par):
                if inside(n - 1, NBLK):
                    f.dve_products_low(dve, n - 1, 1 - par)
                if inside(n + 1, NBLK):
                    f.dve_rows_low(dve, n + 1, 1 - par)
                f.dve_products(dve, n, par)

            f.dve_rows_low(dve, 0, 0)
            steps(dve, step)
            f.dve_products_low(dve, NBLK - 1, 1)


def combine_phase(nc, d, out):
    H = out.shape[3]
    NT = d.NT
    TB = NT // d.NB
    with ExitStack() as ctx:
        sb = lambda n, s, t: ctx.enter_context(nc.sbuf_tensor(n, s, t))
        sem = lambda n: ctx.enter_context(nc.semaphore(n))
        DEPTH = 4
        y1, y2 = sb("y1", [P, DEPTH, H], F32), sb("y2", [P, DEPTH, H], F32)
        t1, t2, t3 = (sb(n, [P, 2, H], F32) for n in ("t1", "t2", "t3"))
        y_in = [sem(f"y_in{i}") for i in range(DEPTH)]
        first_done, sum_done, gated, out_done, stored = (sem(n) for n in ("first_done", "sum_done", "gated", "out_done", "stored"))
        block = ctx.enter_context(nc.Block())

        @block.gpsimd
        def _(pool):
            for n in range(NT):
                if n >= DEPTH:
                    pool.wait_ge(sum_done, n - DEPTH + 1)
                for k, y in enumerate((y1, y2)):
                    pool.indirect_dma_start(
                        y[:, n % DEPTH, :], None, d.y_rows,
                        bass.IndirectOffsetOnAxis(ap=d.place_i[:, k, n:n + 1], axis=0)).then_inc(y_in[n % DEPTH], 16)

        @block.scalar
        def _(act):
            for n in range(NT):
                act.wait_ge(y_in[n % DEPTH], 32 * (n // DEPTH) + 32)
                if n >= 2:
                    act.wait_ge(sum_done, n - 1)
                act.activation(t1[:, n % 2, :], y1[:, n % DEPTH, :], ACT.Copy,
                               scale=d.score[:, 0, n:n + 1]).then_inc(first_done, 1)

        @block.vector
        def _(dve):
            for n in range(NT):
                par = n % 2
                dve.wait_ge(first_done, n + 1)
                dve.scalar_tensor_tensor(out=t2[:, par, :], in0=y2[:, n % DEPTH, :], scalar=d.score[:, 1, n:n + 1],
                                         in1=t1[:, par, :], op0=ALU.mult, op1=ALU.add).then_inc(sum_done, 1)
                dve.wait_ge(sum_done, n + 1)
                dve.tensor_tensor(t3[:, par, :], t2[:, par, :], d.mod_rows[:, n // TB, 3 * H:4 * H],
                                  ALU.mult).then_inc(gated, 1)
                dve.wait_ge(gated, n + 1)
                dve.tensor_tensor(d.Z[:, n, :], t3[:, par, :], d.Z[:, n, :], ALU.add).then_inc(out_done, 1)

        @block.sync
        def _(sp):
            for i in range(NT // 4):
                b, t = 4 * i // TB, 4 * i % TB
                sp.wait_ge(out_done, 4 * i + 4)
                sp.dma_start(out[b, :, t:t + 4, :], d.Z[:, 4 * i:4 * i + 4, :]).then_inc(stored, 16)
            sp.wait_ge(stored, 16 * (NT // 4))


def constants(nc, d, sb, sem, E, NBLK):
    d.ident = sb("ident", [P, P], F32)
    d.minus_half = sb("minus_half", [P, 16], F32)
    d.before = sb("before", [P, P], BF16)
    d.ones = sb("ones", [P, P], BF16)
    d.codes = sb("codes", [P, E], F32)
    d.first_row = sb("first_row", [P, E + 1], F32)
    d.consts = c = Namespace()
    c.limits = sb("limits", [P, d.most], F32)
    c.numbers = sb("numbers", [1, NBLK], F32)
    d.s_const = sem("s_const")
    sets = [(d.ident[:], 0.0), (d.minus_half[:], -0.5), (d.before[:], 1.0), (d.ones[:], 1.0),
            (c.limits[:, 0:1], -1.0)]
    sets += [(d.codes[:, e:e + 1], float(E - e)) for e in range(E)]
    sets += [(d.first_row[:, e:e + 1], float(d.capacity * e)) for e in range(E + 1)]
    d.n_const = len(sets) + 4
    with nc.Block() as block:
        @block.gpsimd
        def _(pool):
            for out, v in sets:
                pool.memset(out, v).then_inc(d.s_const, 1)
            pool.wait_ge(d.s_const, len(sets))
            pool.affine_select(out=d.ident[:], in_=d.ident[:], compare_op=ALU.not_equal, fill=1.0, base=0,
                               pattern=[[-1, P]], channel_multiplier=1).then_inc(d.s_const, 1)
            pool.affine_select(out=d.before[:], in_=d.before[:], compare_op=ALU.is_gt, fill=0.0, base=0,
                               pattern=[[1, P]], channel_multiplier=-1).then_inc(d.s_const, 1)
            pool.iota(c.limits[:, 1:], pattern=[[P, d.most - 1]], base=P, channel_multiplier=0,
                      allow_small_or_imprecise_dtypes=True).then_inc(d.s_const, 1)
            pool.iota(c.numbers[:], pattern=[[1, NBLK]], base=0, channel_multiplier=0,
                      allow_small_or_imprecise_dtypes=True).then_inc(d.s_const, 1)
            pool.wait_ge(d.s_const, d.n_const)


def layer(nc, x, mask, cT_in, wmod, wqkv, wo, shared_gate, shared_up, shared_down, router_w, router_bias,
          gate_w, up_w, down_w, out):
    d = Namespace()
    NB, S, H = x.shape
    E = router_w.shape[2]
    T = NB * S
    TOP = 2
    d.NB, d.NT, d.E = NB, T // P, E
    d.capacity = T + P
    d.spare_row = E * d.capacity
    d.all_rows = d.spare_row + E * P
    d.most = T // P
    d.blocks = TOP * T // P + E
    d.x1 = nc.dram_tensor("x1", (T, H), F32, kind="Internal").ap()
    d.x_rows = nc.dram_tensor("x_rows", (d.all_rows, H), F32, kind="Internal").ap()
    d.y_rows = nc.dram_tensor("y_rows", (d.blocks * P, H), F32, kind="Internal").ap()
    with ExitStack() as ctx:
        sb = lambda n, s, t: ctx.enter_context(nc.sbuf_tensor(n, s, t))
        sem = lambda n: ctx.enter_context(nc.semaphore(n))
        d.mod_rows = sb("mod_rows", [P, NB, 4 * H], F32)
        d.stats1 = sb("stats1", [P, T // P, 6], F32)
        d.base = sb("base", [P, NB + 1, E], F32)
        d.place_i = sb("place_i", [P, TOP, T // P], I32)
        d.place = sb("place", [P, TOP, T // P], F32)
        d.score = sb("score", [P, TOP, T // P], F32)
        d.s_gate = sem("s_gate")
        d.passed = sem("passed")
        d.stats1_done = sem("stats1_done")
        d.base_set = sem("base_set")
        constants(nc, d, sb, sem, E, d.blocks)
        attention_phase(nc, d, x, cT_in, wmod, wqkv, wo, mask)
        d.Z = sb("Z", [P, T // P, H], F32)
        shared_phase(nc, d, d.x1, shared_gate, shared_up, shared_down, router_w, router_bias)
        experts_phase(nc, d, gate_w, up_w, down_w)
        combine_phase(nc, d, out.rearrange("b (t p) h -> b p t h", p=P))


def kernel(**inputs):
    from concourse import bacc
    from concourse.bass_utils import run_bass_kernel_spmd

    a = {k[3:]: np.asarray(v) for k, v in inputs.items()}
    c = np.ascontiguousarray
    H = a["wmod"].shape[0]
    E, _, I = a["ffn_gate_w"].shape

    def on_partitions(w):
        return c(w.reshape(w.shape[0] // P, P, -1).transpose(1, 0, 2))

    def each_on_partitions(w):
        return c(w.reshape(E, w.shape[1] // P, P, -1).transpose(0, 2, 1, 3))

    arrays = {
        "x": c(a["attn_x"]),
        "mask": c(a["attn_head_dim_mask"].reshape(P, 1)),
        "cT": on_partitions(a["c"].T),
        "wmod": c(a["wmod"]),
        "wqkv": on_partitions(np.concatenate([a["attn_w_q"], a["attn_w_k"], a["attn_w_v"]], 1)),
        "wo": c(a["attn_w_o"]),
        "shared_gate": on_partitions(a["ffn_shared_gate"].T),
        "shared_up": on_partitions(a["ffn_shared_up"].T),
        "shared_down": on_partitions(a["ffn_shared_down"].T),
        "router_w": on_partitions(a["ffn_router_w"].T),
        "router_bias": c(a["ffn_routing_bias"].reshape(1, E)),
        "gate_w": each_on_partitions(a["ffn_gate_w"]),
        "up_w": each_on_partitions(a["ffn_up_w"]),
        "down_w": each_on_partitions(a["ffn_down_w"]),
    }
    nc = bacc.Bacc("TRN2", target_bir_lowering=False, num_devices=1)
    aps = [nc.dram_tensor(f"in_{k}", v.shape, mybir.dt.from_np(v.dtype), kind="ExternalInput").ap()
           for k, v in arrays.items()]
    out = nc.dram_tensor("out_0", a["attn_x"].shape, F32, kind="ExternalOutput").ap()
    layer(nc, *aps, out)
    r = run_bass_kernel_spmd(nc, [{f"in_{k}": v for k, v in arrays.items()}], core_ids=[0])
    return r.results[0]["out_0"]
```

```python
from contextlib import ExitStack

import numpy as np

import concourse.bass as bass
from concourse import mybir

F32 = mybir.dt.float32
F32R = mybir.dt.float32r
BF16 = mybir.dt.bfloat16
I32 = mybir.dt.int32
U32 = mybir.dt.uint32
ALU = mybir.AluOpType
ACT = mybir.ActivationFunctionType
AX_X = mybir.AxisListType.X

P = 128
EPS = 1e-5
FLOOR = 0.25
ds = bass.ds


def product(pe, out, l_hi, l_lo, r_hi, r_lo, first=True, last=True):
    pe.matmul(out, l_hi, r_hi, start=first, stop=False)
    pe.matmul(out, l_hi, r_lo, start=False, stop=False)
    return pe.matmul(out, l_lo, r_hi, start=False, stop=last)


def hold(eng, d, semaphore, value):
    eng.wait_ge(semaphore, value)
    eng.sem_inc(d.passed, 1)


def attention_phase(nc, d, x, cT_in, wmod, wqkv, wo, mask):
    NB, S, H = x.shape
    D = P
    HC = H // P
    NT = S // P
    NBLK = S // 512
    GQ = 256
    NG = S // GQ
    SCALE = float(D) ** -0.5
    MOD_FIXED = 5
    PV_STEPS = (7, 1, 0, 0)

    with ExitStack() as ctx:
        sb = lambda n, s, t: ctx.enter_context(nc.sbuf_tensor(n, s, t))
        sem = lambda n: ctx.enter_context(nc.semaphore(n))
        bank = [ctx.enter_context(nc.psum_tensor(f"a_bank{i}", [P, 512], F32)) for i in range(8)]
        s_bank, t_bank, o_bank = bank[0:4], bank[4:6], bank[6:8]
        rows, ident = d.mod_rows, d.ident

        X = sb("X", [P, 2, NT, H], F32)
        w_hi = sb("w_hi", [P, HC, 3 * D], F32R)
        w_lo = sb("w_lo", [P, HC, 3 * D], F32R)
        wo_masked = sb("wo_masked", [P, H], F32)
        wo_hi = sb("wo_hi", [P, H], F32R)
        wo_lo = sb("wo_lo", [P, H], F32R)
        mask_i = sb("mask_i", [P, 1], I32)
        mask_f = sb("mask_f", [P, 1], F32)
        cT = sb("cT", [P, HC, NB], F32)
        ce = sb("ce", [P, HC, NB], F32)
        silu_rows = sb("silu_rows", [P, HC, NB, P], F32)
        mod_cols = sb("mod_cols", [P, 2, HC, NB], F32)
        stats = sb("stats", [P, NT, 6], F32)
        mv = sb("mv", [P, NT, 2], F32)
        veps = sb("veps", [P, NT], F32)
        rstd = sb("rstd", [P, NT], F32)
        vt = sb("vt", [P, 2, 512], F32)
        wo_gated = vt[:, 0, 0:H]
        kT_hi = sb("kT_hi", [P, S], F32R)
        kT_lo = sb("kT_lo", [P, S], F32R)
        qT_hi = sb("qT_hi", [P, S], F32R)
        qT_lo = sb("qT_lo", [P, S], F32R)
        v_hi = sb("v_hi", [P, NT, D], F32R)
        v_lo = sb("v_lo", [P, NT, D], F32R)
        q_hi = sb("q_hi", [P, 2, GQ], F32R)
        q_lo = sb("q_lo", [P, 2, GQ], F32R)
        prob = sb("prob", [P, 2, S], F32)
        xhat = prob[:, :, :].rearrange("p a (t h) -> p (a t) h", h=H)
        flat = prob[:, :, :].rearrange("p a s -> p (a s)")
        wmod_sb = flat[:, 0:HC * 6 * H].rearrange("p (k n) -> p k n", k=HC)
        w_raw = flat[:, HC * 6 * H:HC * (6 * H + 3 * D)].rearrange("p (k n) -> p k n", k=HC)
        wo_raw = flat[:, HC * (6 * H + 3 * D):HC * (6 * H + 3 * D) + H]
        pT_hi = sb("pT_hi", [P, 2, NT, GQ], F32R)
        pT_lo = sb("pT_lo", [P, 2, NT, GQ], F32R)
        hT_hi = pT_hi[:, 0, :, :].rearrange("p k q -> p (k q)").rearrange("p (c s) -> p c s", c=HC)
        hT_lo = pT_lo[:, 0, :, :].rearrange("p k q -> p (k q)").rearrange("p (c s) -> p c s", c=HC)
        oT_hi = sb("oT_hi", [P, 2, GQ], F32R)
        oT_lo = sb("oT_lo", [P, 2, GQ], F32R)
        bmax = sb("bmax", [P, 2, 4], F32)
        negmax = sb("negmax", [P, 2], F32)
        esum = sb("esum", [P, 2, 2, 4], F32)
        den = sb("den", [P, 2, 2], F32)
        rden = sb("rden", [P, 2, 2], F32)

        w_loaded = sem("w_loaded")
        x_loaded = sem("x_loaded")
        x1_stored = sem("x1_stored")
        exp_c = sem("exp_c")
        silu_c = sem("silu_c")
        w_split = sem("w_split")
        mod_mm = sem("mod_mm")
        mod_out = sem("mod_out")
        mod_fix = sem("mod_fix")
        stats_done = sem("stats_done")
        mv_done = sem("mv_done")
        veps_done = sem("veps_done")
        rstd_done = sem("rstd_done")
        xhat_done = sem("xhat_done")
        hT_mm = sem("hT_mm")
        vt_done = sem("vt_done")
        hT_hi_done = sem("hT_hi_done")
        hT_lo_done = sem("hT_lo_done")
        qkv_mm = sem("qkv_mm")
        qkv_hi = sem("qkv_hi")
        qkv_lo = sem("qkv_lo")
        q_copied = sem("q_copied")
        s_mm = sem("s_mm")
        bmax_done = sem("bmax_done")
        negmax_done = sem("negmax_done")
        exp_done = sem("exp_done")
        pT_mm = sem("pT_mm")
        pT_hi_done = sem("pT_hi_done")
        pT_lo_done = sem("pT_lo_done")
        den_done = sem("den_done")
        rden_done = sem("rden_done")
        o_mm = sem("o_mm")
        oT_hi_done = sem("oT_hi_done")
        oT_lo_done = sem("oT_lo_done")
        y_mm = sem("y_mm")
        wo_split = sem("wo_split")
        x1_done = sem("x1_done")

        x_v = x.rearrange("b (t p) h -> b p t h", p=P)
        x1_v = d.x1.rearrange("(b t p) h -> b p t h", p=P, t=NT)
        block = ctx.enter_context(nc.Block())

        def groups(eng, G0, body):
            body(0, G0, 0, 0)
            body(1, G0 + 1, 1, 1)
            with eng.Fori(2, NG - 2, 2) as g:
                body(2, G0 + g, 0, g)
                body(3, G0 + (g + 1), 1, g + 1)
            body(NG - 2, G0 + (NG - 2), 0, NG - 2)
            body(NG - 1, G0 + (NG - 1), 1, NG - 1)

        def qkv_places(k):
            t = slice(512 * k, 512 * k + 512)
            return [(bank[k % 2][:], (kT_hi[:, t], kT_lo[:, t])),
                    (bank[2 + k % 2][:], (qT_hi[:, t], qT_lo[:, t])),
                    (bank[6 + k % 2][:].rearrange("p (t d) -> p t d", d=D),
                     (v_hi[:, 4 * k:4 * k + 4, :], v_lo[:, 4 * k:4 * k + 4, :]))]

        @block.sync
        def _(sp):
            sp.dma_start(cT[:], cT_in).then_inc(w_loaded, 16)
            sp.dma_start(wmod_sb, wmod.rearrange("(k p) n -> p k n", p=P)).then_inc(w_loaded, 16)
            sp.dma_start(w_raw, wqkv).then_inc(w_loaded, 16)
            sp.dma_start(wo_raw, wo).then_inc(w_loaded, 16)
            sp.dma_start(mask_i[:], mask).then_inc(w_loaded, 16)
            sp.dma_start(X[:, 0], x_v[0]).then_inc(x_loaded, 16)
            for b in range(NB):
                if b + 1 < NB:
                    if b >= 1:
                        sp.wait_ge(x1_stored, 16 * NG * b)
                        sp.wait_ge(d.stats1_done, NT * b)
                    sp.wait_ge(x_loaded, 16 * (b + 1))
                    sp.dma_start(X[:, (b + 1) % 2], x_v[b + 1]).then_inc(x_loaded, 16)
                else:
                    sp.sem_inc(x_loaded, 16)
                with sp.Fori(0, NG) as g:
                    sp.wait_ge(x1_done, 2 * (NG * b + g) + 2)
                    sp.dma_start(x1_v[b, :, ds(2 * g, 2), :],
                                 X[:, b % 2, ds(2 * g, 2), :]).then_inc(x1_stored, 16)
            sp.wait_ge(x1_stored, 16 * NG * NB)

        @block.gpsimd
        def _(pool):
            def deviations(n):
                hold(pool, d, mv_done, NT * n + NT)
                pool.tensor_scalar(veps[:], mv[:, :, 1], EPS, None, ALU.add).then_inc(veps_done, 1)
                pool.wait_ge(veps_done, n + 1)
                pool.tensor_tensor(rstd[:], veps[:], d.minus_half[:], ALU.pow).then_inc(rstd_done, 1)

            deviations(0)
            with pool.Fori(0, NB) as b:
                def queries(k, G, par, g):
                    if k >= 2:
                        hold(pool, d, s_mm, 8 * G - 8)
                    pool.tensor_copy(q_hi[:, par, :], qT_hi[:, ds(GQ * g, GQ)]).then_inc(q_copied, 1)
                    pool.tensor_copy(q_lo[:, par, :], qT_lo[:, ds(GQ * g, GQ)]).then_inc(q_copied, 1)

                hold(pool, d, qkv_lo, 12 * b + 2)
                groups(pool, NG * b, queries)
                deviations(b + 1)

        @block.scalar
        def _(act):
            act.wait_ge(w_loaded, 80)
            act.activation(ce[:], cT[:], ACT.Exp, scale=-1.0).then_inc(exp_c, 1)
            for i in range(2 * NB):
                act.wait_ge(mod_mm, i + 1)
                act.activation(rows[:, i // 2, 512 * (i % 2):512 * (i % 2) + 512], bank[i % 4][:],
                               ACT.Copy).then_inc(mod_out, 1)
            act.wait_ge(mod_fix, MOD_FIXED)
            with act.Fori(0, NB) as b:
                def rows_T(f):
                    c = f % 2
                    hold(act, d, hT_mm, 8 * b + f + 1)
                    if f >= 2:
                        hold(act, d, hT_lo_done, 8 * b + f - 1)
                    act.activation(vt[:, f % 2, :], t_bank[f % 2][:], ACT.Identity,
                                   scale=mod_cols[:, 1, c, ds(b, 1)], bias=mod_cols[:, 0, c, ds(b, 1)]
                                   ).then_inc(vt_done, 1)
                    act.wait_ge(vt_done, 8 * b + f + 1)
                    act.activation(hT_hi[:, c, 512 * (f // 2):512 * (f // 2) + 512], vt[:, f % 2, :],
                                   ACT.Copy).then_inc(hT_hi_done, 1)

                def qkv_high(k):
                    for m, (src, dst) in enumerate(qkv_places(k)):
                        act.wait_ge(qkv_mm, 12 * b + 3 * k + m + 1)
                        act.activation(dst[0], src, ACT.Copy, scale=SCALE if m == 1 else 1.0
                                       ).then_inc(qkv_hi, 1)

                for k in range(NBLK):
                    rows_T(2 * k)
                    rows_T(2 * k + 1)
                    if k:
                        qkv_high(k - 1)
                qkv_high(NBLK - 1)

                def exps(G, par, c, j):
                    t = 2 * G + c
                    act.wait_ge(s_mm, 4 * t + j + 1)
                    if j == 0:
                        act.wait_ge(negmax_done, t + 1)
                    act.activation(prob[:, c, 512 * j:512 * j + 512], s_bank[j][:], ACT.Exp,
                                   bias=negmax[:, c:c + 1], accum_out=esum[:, par, c, j:j + 1]
                                   ).then_inc(exp_done, 1)

                def high(G, par, c, j):
                    act.wait_ge(pT_mm, 4 * (2 * G + c) + j + 1)
                    act.activation(pT_hi[:, par, 4 * j:4 * j + 4, P * c:P * c + P],
                                   t_bank[j % 2][:].rearrange("p (k q) -> p k q", q=P),
                                   ACT.Copy).then_inc(pT_hi_done, 1)

                def output_high(G, par):
                    act.wait_ge(o_mm, G + 1)
                    act.activation(oT_hi[:, par, :], o_bank[par][:, 0:GQ],
                                   ACT.Copy).then_inc(oT_hi_done, 1)

                def body(k, G, par, g):
                    if k >= 2:
                        output_high(G - 2, par)
                    for c in range(2):
                        exps(G, par, c, 0)
                        for j in range(1, 4):
                            exps(G, par, c, j)
                            high(G, par, c, j - 1)
                        high(G, par, c, 3)

                groups(act, NG * b, body)
                output_high(NG * b + (NG - 2), 0)
                output_high(NG * b + (NG - 1), 1)

        @block.tensor
        def _(pe):
            pe.wait_ge(d.s_const, d.n_const)
            pe.wait_ge(silu_c, 4)
            for i in range(2 * NB):
                if i >= 4:
                    pe.wait_ge(mod_out, i - 3)
                for k in range(HC):
                    mm = pe.matmul(bank[i % 4][:], silu_rows[:, k, i // 2, :],
                                   wmod_sb[:, k, 2 * H + 512 * (i % 2):2 * H + 512 * (i % 2) + 512],
                                   start=(k == 0), stop=(k == HC - 1))
                mm.then_inc(mod_mm, 1)
            for w in range(2):
                for hc in range(HC):
                    for k in range(HC):
                        o = w * H + hc * P
                        mm = pe.matmul(bank[4][:, (w * HC + hc) * NB:(w * HC + hc + 1) * NB],
                                       wmod_sb[:, k, o:o + P], silu_rows[:, k, :, 0],
                                       start=(k == 0), stop=(k == HC - 1))
            mm.then_inc(mod_mm, 1)
            pe.wait_ge(w_split, 4)
            pe.wait_ge(mod_fix, MOD_FIXED)
            with pe.Fori(0, NB) as b:
                def rows_T(f):
                    pe.wait_ge(xhat_done, NT * b + 4 * (f // 2 + 1))
                    if f >= 2:
                        pe.wait_ge(vt_done, 8 * b + f - 1)
                    for i in range(4):
                        mm = pe.transpose(t_bank[f % 2][:, P * i:P * i + P],
                                          xhat[:, 4 * (f // 2) + i, P * (f % 2):P * (f % 2) + P], ident[:])
                    mm.then_inc(hT_mm, 1)

                def qkv(k):
                    pe.wait_ge(hT_lo_done, 8 * b + 2 * k + 2)
                    if k >= 2:
                        pe.wait_ge(qkv_lo, 12 * b + 3 * (k - 1))
                    t = slice(512 * k, 512 * k + 512)
                    for m, out in ((1, bank[k % 2]), (0, bank[2 + k % 2])):
                        for c in range(HC):
                            mm = product(pe, out[:], w_hi[:, c, m * D:m * D + D], w_lo[:, c, m * D:m * D + D],
                                         hT_hi[:, c, t], hT_lo[:, c, t], c == 0, c == HC - 1)
                        mm.then_inc(qkv_mm, 1)
                    for i in range(4):
                        ti = slice(512 * k + P * i, 512 * k + P * i + P)
                        for c in range(HC):
                            mm = product(pe, bank[6 + k % 2][:, P * i:P * i + P],
                                         hT_hi[:, c, ti], hT_lo[:, c, ti],
                                         w_hi[:, c, 2 * D:3 * D], w_lo[:, c, 2 * D:3 * D], c == 0, c == HC - 1)
                    mm.then_inc(qkv_mm, 1)

                for k in range(NBLK):
                    rows_T(2 * k)
                    rows_T(2 * k + 1)
                    if k:
                        qkv(k - 1)
                qkv(NBLK - 1)

                def scores(G, par, c, j):
                    if j == 0 and c == 0:
                        pe.wait_ge(q_copied, 2 * G + 2)
                    mm = product(pe, s_bank[j][:], q_hi[:, par, P * c:P * c + P], q_lo[:, par, P * c:P * c + P],
                                 kT_hi[:, 512 * j:512 * j + 512], kT_lo[:, 512 * j:512 * j + 512])
                    mm.then_inc(s_mm, 1)

                def turn(G, c, j, fresh):
                    t = 2 * G + c
                    if not fresh:
                        pe.wait_ge(pT_lo_done, 4 * t + j - 1)
                    for i in range(4):
                        k = 4 * j + i
                        mm = pe.transpose(t_bank[j % 2][:, P * i:P * i + P],
                                          prob[:, c, P * k:P * k + P], ident[:])
                    mm.then_inc(pT_mm, 1)

                def values(k_group, G, par, k0, n):
                    pe.wait_ge(pT_lo_done, 8 * G + 4 + (k0 + n + 3) // 4)
                    if k0 == 0 and k_group >= 2:
                        pe.wait_ge(x1_done, 2 * G - 2)
                    for k in range(k0, k0 + n):
                        mm = product(pe, o_bank[par][:, 0:GQ], v_hi[:, k, :], v_lo[:, k, :],
                                     pT_hi[:, par, k, :], pT_lo[:, par, k, :], k == 0, k == NT - 1)
                    if k0 + n == NT:
                        mm.then_inc(o_mm, 1)

                def project(G, par):
                    pe.wait_ge(oT_lo_done, G + 1)
                    pe.wait_ge(wo_split, 3 * b + 3)
                    for c in range(2):
                        mm = product(pe, o_bank[par][:, H * c:H * c + H], oT_hi[:, par, P * c:P * c + P],
                                     oT_lo[:, par, P * c:P * c + P], wo_hi[:], wo_lo[:])
                    mm.then_inc(y_mm, 1)

                def body(k, G, par, g):
                    done = 0
                    for c in range(2):
                        for j in range(4):
                            if k >= 1 and PV_STEPS[j]:
                                values(k - 1, G - 1, 1 - par, done, PV_STEPS[j])
                                done += PV_STEPS[j]
                            pe.wait_ge(exp_done, 4 * (2 * G + c) + j + 1)
                            turn(G, c, j, k == 0 and c == 0 and j < 2)
                            if c == 0:
                                scores(G, par, 1, j)
                            elif k < NG - 1:
                                scores(G + 1, 1 - par, 0, j)
                            if k >= 2 and c == 0 and j == 1:
                                project(G - 2, par)

                pe.wait_ge(qkv_lo, 12 * b + 12)
                for j in range(4):
                    scores(NG * b, 0, 0, j)
                groups(pe, NG * b, body)
                values(NG - 1, NG * b + (NG - 1), 1, 0, NT)
                project(NG * b + (NG - 2), 0)
                project(NG * b + (NG - 1), 1)
                pe.wait_ge(x1_done, 2 * NG * b + 2 * NG)

        @block.vector
        def _(dve):
            dve.wait_ge(w_loaded, 80)
            dve.tensor_copy(w_hi[:], w_raw).then_inc(w_split, 1)
            dve.tensor_copy(mask_f[:], mask_i[:]).then_inc(w_split, 1)
            dve.wait_ge(w_split, 2)
            dve.tensor_scalar(wo_masked[:], wo_raw, mask_f[:], None, ALU.mult).then_inc(w_split, 1)
            dve.wait_ge(exp_c, 1)
            dve.tensor_scalar(ce[:], ce[:], 1.0, None, ALU.add).then_inc(silu_c, 1)
            dve.wait_ge(silu_c, 1)
            dve.reciprocal(ce[:], ce[:]).then_inc(silu_c, 1)
            dve.wait_ge(silu_c, 2)
            dve.tensor_tensor(cT[:], cT[:], ce[:], ALU.mult).then_inc(silu_c, 1)
            dve.wait_ge(silu_c, 3)
            dve.tensor_copy(silu_rows[:], cT[:].unsqueeze(3).to_broadcast([P, HC, NB, P])).then_inc(silu_c, 1)
            dve.tensor_tensor(w_lo[:], w_raw, w_hi[:].bitcast(F32), ALU.subtract).then_inc(w_split, 1)
            dve.wait_ge(w_split, 4)
            dve.wait_ge(mod_mm, 2 * NB + 1)
            cols = bank[4][:, 0:2 * HC * NB].rearrange("p (w c b) -> p w c b", w=2, c=HC)
            dve.tensor_copy(mod_cols[:, 0], cols[:, 0]).then_inc(mod_fix, 1)
            dve.tensor_scalar(mod_cols[:, 1], cols[:, 1], 1.0, None, ALU.add).then_inc(mod_fix, 1)
            dve.wait_ge(mod_out, 2 * NB)
            dve.tensor_scalar(rows[:, :, 2 * H:3 * H], rows[:, :, 2 * H:3 * H], 1.0, None,
                              ALU.add).then_inc(mod_fix, 1)
            mag = vt[:, :, :].rearrange("p a (b h) -> p (a b) h", h=H)
            for n, o in enumerate((0, 3 * H)):
                gate = rows[:, :, o:o + H]
                dve.wait_ge(mod_fix, 3 + n)
                dve.scalar_tensor_tensor(out=mag, in0=gate, scalar=-1.0, in1=gate, op0=ALU.mult,
                                         op1=ALU.max).then_inc(d.s_gate, 1)
                dve.wait_ge(d.s_gate, 3 * n + 1)
                dve.tensor_scalar(gate, gate, 0.0, 2.0, ALU.is_ge, ALU.mult).then_inc(d.s_gate, 1)
                dve.tensor_scalar(mag, mag, FLOOR, None, ALU.max).then_inc(d.s_gate, 1)
                dve.wait_ge(d.s_gate, 3 * n + 3)
                dve.scalar_tensor_tensor(out=gate, in0=gate, scalar=1.0, in1=mag, op0=ALU.subtract,
                                         op1=ALU.mult).then_inc(mod_fix, 1)

            def aggregate(n):
                hold(dve, d, stats_done, NT * n + NT)
                for t in range(NT):
                    dve.bn_aggr(mv[:, t, :], stats[:, t, :]).then_inc(mv_done, 1)

            def normalise(n, buffer):
                dve.wait_ge(rstd_done, n + 1)
                for t in range(NT):
                    dve.tensor_scalar(xhat[:, t, :], X[:, buffer, t, :], mv[:, t, 0:1], rstd[:, t:t + 1],
                                      ALU.subtract, ALU.mult).then_inc(xhat_done, 1)

            dve.wait_ge(x_loaded, 16)
            for t in range(NT):
                dve.bn_stats(stats[:, t, :], X[:, 0, t, :]).then_inc(stats_done, 1)
            aggregate(0)
            normalise(0, 0)
            with dve.Fori(0, NB) as b:
                xb = b & 1

                def rows_low(f):
                    dve.wait_ge(hT_hi_done, 8 * b + f + 1)
                    t = slice(512 * (f // 2), 512 * (f // 2) + 512)
                    dve.tensor_tensor(hT_lo[:, f % 2, t], vt[:, f % 2, :], hT_hi[:, f % 2, t].bitcast(F32),
                                      ALU.subtract).then_inc(hT_lo_done, 1)

                def qkv_low(k):
                    for m, (src, dst) in enumerate(qkv_places(k)):
                        dve.wait_ge(qkv_hi, 12 * b + 3 * k + m + 1)
                        if m == 1:
                            dve.scalar_tensor_tensor(out=dst[1], in0=src, scalar=SCALE, in1=dst[0].bitcast(F32),
                                                     op0=ALU.mult, op1=ALU.subtract).then_inc(qkv_lo, 1)
                        else:
                            dve.tensor_tensor(dst[1], src, dst[0].bitcast(F32), ALU.subtract).then_inc(qkv_lo, 1)

                for k in range(NBLK):
                    rows_low(2 * k)
                    rows_low(2 * k + 1)
                    if k:
                        qkv_low(k - 1)
                qkv_low(NBLK - 1)

                dve.tensor_tensor(wo_gated, wo_masked[:], rows[:, ds(b, 1), 0:H].rearrange("p o h -> p (o h)"),
                                  ALU.mult).then_inc(wo_split, 1)
                dve.wait_ge(wo_split, 3 * b + 1)
                dve.tensor_copy(wo_hi[:], wo_gated).then_inc(wo_split, 1)
                dve.wait_ge(wo_split, 3 * b + 2)
                dve.tensor_tensor(wo_lo[:], wo_gated, wo_hi[:].bitcast(F32), ALU.subtract).then_inc(wo_split, 1)

                def block_max(G, c, j):
                    t = 2 * G + c
                    dve.wait_ge(s_mm, 4 * t + j + 1)
                    dve.tensor_reduce(bmax[:, c, j:j + 1], s_bank[j][:], AX_X, ALU.max).then_inc(bmax_done, 1)
                    if j == 3:
                        dve.wait_ge(bmax_done, 4 * t + 4)
                        dve.tensor_reduce(negmax[:, c:c + 1], bmax[:, c, :], AX_X, ALU.max,
                                          negate=True).then_inc(negmax_done, 1)

                def low(G, par, c, j):
                    dve.wait_ge(pT_hi_done, 4 * (2 * G + c) + j + 1)
                    o = (slice(None), par, slice(4 * j, 4 * j + 4), slice(P * c, P * c + P))
                    dve.tensor_tensor(pT_lo[o], t_bank[j % 2][:].rearrange("p (k q) -> p k q", q=P),
                                      pT_hi[o].bitcast(F32), ALU.subtract).then_inc(pT_lo_done, 1)

                def denominators(G, par):
                    dve.wait_ge(exp_done, 8 * G + 8)
                    dve.tensor_reduce(den[:, par, :], esum[:, par, :, :], AX_X, ALU.add).then_inc(den_done, 1)
                    dve.wait_ge(den_done, G + 1)
                    dve.reciprocal(rden[:, par, :], den[:, par, :]).then_inc(rden_done, 1)

                def output_low(G, par):
                    dve.wait_ge(oT_hi_done, G + 1)
                    dve.tensor_tensor(oT_lo[:, par, :], o_bank[par][:, 0:GQ],
                                      oT_hi[:, par, :].bitcast(F32), ALU.subtract).then_inc(oT_lo_done, 1)

                def residual(G, par, g):
                    dve.wait_ge(y_mm, G + 1)
                    dve.wait_ge(rden_done, G + 1)
                    tile = lambda c: X[:, ds(xb, 1), ds(2 * g + c, 1), :].rearrange("p o t h -> p (o t h)")
                    for c in range(2):
                        dve.scalar_tensor_tensor(out=tile(c), in0=o_bank[par][:, H * c:H * c + H],
                                                 scalar=rden[:, par, c:c + 1], in1=tile(c),
                                                 op0=ALU.mult, op1=ALU.add).then_inc(x1_done, 1)
                    for c in range(2):
                        hold(dve, d, x1_done, 2 * G + c + 1)
                        dve.bn_stats(d.stats1[:, ds(2 * G + c, 1), :], tile(c)).then_inc(d.stats1_done, 1)

                def next_statistics(k, g):
                    if k == 0:
                        hold(dve, d, x_loaded, 16 * b + 32)
                    for i in range(2):
                        st = stats[:, ds(2 * g + i, 1), :]
                        dve.bn_stats(st, X[:, ds(1 - xb, 1), ds(2 * g + i, 1), :]).then_inc(stats_done, 1)

                def body(k, G, par, g):
                    next_statistics(k, g)
                    if k >= 1:
                        denominators(G - 1, 1 - par)
                    if k >= 2:
                        output_low(G - 2, par)
                    if k == NG - 1:
                        aggregate(b + 1)
                    for c in range(2):
                        if k >= 2 and c == 1:
                            residual(G - 2, par, g - 2)
                        for j in range(4):
                            if c == 0:
                                block_max(G, 1, j)
                            elif k < NG - 1:
                                block_max(G + 1, 0, j)
                            low(G, par, c, j)

                for j in range(4):
                    block_max(NG * b, 0, j)
                groups(dve, NG * b, body)
                normalise(b + 1, ds(1 - xb, 1))
                denominators(NG * b + (NG - 1), 1)
                output_low(NG * b + (NG - 2), 0)
                output_low(NG * b + (NG - 1), 1)
                residual(NG * b + (NG - 2), 0, NG - 2)
                residual(NG * b + (NG - 1), 1, NG - 1)


class Namespace:
    pass


def inside(n, count):
    return not isinstance(n, int) or 0 <= n < count


def split_weights(eng, raw, hi, lo, done, n):
    eng.tensor_copy(hi, raw).then_inc(done, 1)
    eng.wait_ge(done, n + 1)
    eng.tensor_tensor(lo, raw, hi.bitcast(F32), ALU.subtract).then_inc(done, 1)


def gated_blocks(ctx, nc, d, tag, count, H, I):
    HC, IC = H // P, I // P
    f = Namespace()
    sb = lambda n, s, t: ctx.enter_context(nc.sbuf_tensor(f"{tag}_{n}", s, t))
    sem = lambda n: ctx.enter_context(nc.semaphore(f"{tag}_{n}"))
    f.bank = [ctx.enter_context(nc.psum_tensor(f"{tag}_bank{i}", [P, 512], F32)) for i in range(8)]
    g_bank, u_bank, a_bank, x_bank = f.bank[0:4]
    f.y_bank = f.bank[4:6]
    xT_hi, xT_lo = sb("xT_hi", [P, 2, HC, P], F32R), sb("xT_lo", [P, 2, HC, P], F32R)
    f.xT_hi, f.xT_lo = xT_hi, xT_lo
    silu_g, prod = sb("silu_g", [P, 2, I], F32), sb("prod", [P, 2, I], F32)
    aT_hi, aT_lo = sb("aT_hi", [P, 2, IC, P], F32R), sb("aT_lo", [P, 2, IC, P], F32R)
    f.xT_mm, f.xT_hi_done, f.xT_lo_done = sem("xT_mm"), sem("xT_hi_done"), sem("xT_lo_done")
    f.gate_mm, f.up_mm, f.silu_done, f.prod_done = sem("gate_mm"), sem("up_mm"), sem("silu_done"), sem("prod_done")
    f.aT_mm, f.aT_hi_done, f.aT_lo_done = sem("aT_mm"), sem("aT_hi_done"), sem("aT_lo_done")
    f.y_mm, f.y_out, f.rows_ready = sem("y_mm"), sem("y_out"), sem("rows_ready")
    flat = lambda t, par: t[:, par, :, :].rearrange("p c t -> p (c t)")

    def pe_turn_rows(pe, m, par, rows):
        pe.wait_ge(f.rows_ready, f.ready_at(m))
        if inside(m - 1, count):
            pe.wait_ge(f.xT_lo_done, m)
        for c in range(HC):
            mm = pe.transpose(x_bank[:, P * c:P * c + P], rows[:, P * c:P * c + P], d.ident[:])
        mm.then_inc(f.xT_mm, 1)

    def pe_turn_products(pe, m, par):
        pe.wait_ge(f.prod_done, m + 1)
        if inside(m - 1, count):
            pe.wait_ge(f.aT_lo_done, m)
        for c in range(IC):
            mm = pe.transpose(a_bank[:, P * c:P * c + P], prod[:, par, P * c:P * c + P], d.ident[:])
        mm.then_inc(f.aT_mm, 1)

    def pe_gate_up(pe, m, par, weights):
        pe.wait_ge(f.xT_lo_done, m + 1)
        for out, hi, lo, done in ((g_bank, *weights[0], f.gate_mm), (u_bank, *weights[1], f.up_mm)):
            for c in range(HC):
                mm = product(pe, out[:, 0:I], xT_hi[:, par, c, :], xT_lo[:, par, c, :], hi(c), lo(c),
                             c == 0, c == HC - 1)
            mm.then_inc(done, 1)

    def pe_down(pe, m, par, weights):
        pe.wait_ge(f.aT_lo_done, m + 1)
        if inside(m - 2, count):
            pe.wait_ge(f.y_out, m - 1)
        hi, lo = weights[2]
        for c in range(IC):
            mm = product(pe, f.y_bank[par][:, 0:H], aT_hi[:, par, c, :], aT_lo[:, par, c, :], hi(c), lo(c),
                         c == 0, c == IC - 1)
        mm.then_inc(f.y_mm, 1)

    def act_rows_high(act, m, par):
        act.wait_ge(f.xT_mm, m + 1)
        act.activation(flat(xT_hi, par), x_bank[:, 0:H], ACT.Copy).then_inc(f.xT_hi_done, 1)

    def act_products_high(act, m, par):
        act.wait_ge(f.aT_mm, m + 1)
        act.activation(flat(aT_hi, par), a_bank[:, 0:I], ACT.Copy).then_inc(f.aT_hi_done, 1)

    def act_silu(act, m, par):
        act.wait_ge(f.gate_mm, m + 1)
        act.activation(silu_g[:, par, :], g_bank[:, 0:I], ACT.Silu).then_inc(f.silu_done, 1)

    def dve_rows_low(dve, m, par):
        dve.wait_ge(f.xT_hi_done, m + 1)
        dve.tensor_tensor(flat(xT_lo, par), x_bank[:, 0:H], flat(xT_hi, par).bitcast(F32),
                          ALU.subtract).then_inc(f.xT_lo_done, 1)

    def dve_products_low(dve, m, par):
        dve.wait_ge(f.aT_hi_done, m + 1)
        dve.tensor_tensor(flat(aT_lo, par), a_bank[:, 0:I], flat(aT_hi, par).bitcast(F32),
                          ALU.subtract).then_inc(f.aT_lo_done, 1)

    def dve_products(dve, m, par):
        dve.wait_ge(f.silu_done, m + 1)
        dve.wait_ge(f.up_mm, m + 1)
        dve.tensor_tensor(prod[:, par, :], silu_g[:, par, :], u_bank[:, 0:I], ALU.mult).then_inc(f.prod_done, 1)

    f.pe_turn_rows, f.pe_turn_products, f.pe_gate_up, f.pe_down = pe_turn_rows, pe_turn_products, pe_gate_up, pe_down
    f.act_rows_high, f.act_products_high, f.act_silu = act_rows_high, act_products_high, act_silu
    f.dve_rows_low, f.dve_products_low, f.dve_products = dve_rows_low, dve_products_low, dve_products
    return f


def dispatch(pool, d, h_rows, b, sent):
    TB = h_rows.shape[1]
    for t in range(TB):
        for k in range(2):
            pool.indirect_dma_start(
                d.x_rows, bass.IndirectOffsetOnAxis(ap=d.place_i[:, k, TB * b + t:TB * b + t + 1], axis=0),
                h_rows[:, t, :], None).then_inc(sent, 16)


def shared_phase(nc, d, x1, shared_gate, shared_up, shared_down, router_w, router_bias):
    N, H = x1.shape
    I = shared_gate.shape[2]
    HC, IC = H // P, I // P
    E = d.E
    NB = d.NB
    NT = N // P
    TB = NT // NB
    EARLY = TB * d.early
    Z, rows = d.Z, d.mod_rows

    with ExitStack() as ctx:
        sb = lambda n, s, t: ctx.enter_context(nc.sbuf_tensor(n, s, t))
        sem = lambda n: ctx.enter_context(nc.semaphore(n))
        f = gated_blocks(ctx, nc, d, "s", NT, H, I)
        f.ready_at = lambda m: m + 1
        l_bank, r_bank = f.bank[6], f.bank[7]

        sg_hi, sg_lo = sb("sg_hi", [P, HC, I], F32R), sb("sg_lo", [P, HC, I], F32R)
        su_hi, su_lo = sb("su_hi", [P, HC, I], F32R), sb("su_lo", [P, HC, I], F32R)
        sd_hi, sd_lo = sb("sd_hi", [P, IC, H], F32R), sb("sd_lo", [P, IC, H], F32R)
        rw_raw = sb("rw_raw", [P, HC, E], F32)
        rw_hi, rw_lo = sb("rw_hi", [P, HC, E], F32R), sb("rw_lo", [P, HC, E], F32R)
        bias = sb("bias", [P, E], F32)
        h_rows = [sb("h_rows", [P, TB, H], F32), d.last_rows]
        w_raw = d.last_rows[:, :, :].rearrange("p t h -> p (t h)")
        raw = lambda o, a, b: w_raw[:, o:o + a * b].rearrange("p (a b) -> p a b", a=a)
        sg_raw, su_raw, sd_raw = raw(0, HC, I), raw(HC * I, HC, I), raw(2 * HC * I, IC, H)
        h = sb("h", [P, 2, H], F32)
        norm = sb("norm", [P, 2, H], F32)
        scaled = sb("scaled", [P, 2, H], F32)
        gy = sb("gy", [P, 2, H], F32)
        mv, rstd = d.mv, d.rstd
        veps = sb("s_veps", [P, NT], F32)
        three = lambda n, t=F32: sb(n, [P, TB, E], t)
        logits, probs = three("logits"), three("probs")
        same, coded, pick1, rest, pick2, chosen = (three(n) for n in ("same", "coded", "pick1", "rest", "pick2", "chosen"))
        chosen_bf = three("chosen_bf", BF16)
        slot = three("slot")
        best1, code1, best2, code2 = (sb(n, [P, TB], F32) for n in ("best1", "code1", "best2", "code2"))
        total = sb("total", [P, TB], F32)
        base = d.base

        w_loaded = [sem(f"s_w_loaded{i}") for i in range(5)]
        x_loaded = sem("s_x_loaded")
        w_high, w_split = sem("s_w_high"), sem("s_w_split")
        weights = ((rw_raw[:], rw_hi, rw_lo), (sg_raw, sg_hi, sg_lo), (su_raw, su_hi, su_lo), (sd_raw, sd_hi, sd_lo))
        WEIGHT_DMA = (0, 2, 3, 4)
        mv_done, veps_done, rstd_done = sem("s_mv_done"), sem("s_veps_done"), sem("s_rstd_done")
        norm_done, scaled_done, copied = sem("norm_done"), sem("scaled_done"), sem("copied")
        gy_done = sem("gy_done")
        logit_mm, logit_done, prob_done = sem("logit_mm"), sem("logit_done"), sem("prob_done")
        route, rank_mm, placed = sem("route"), sem("rank_mm"), sem("placed")
        sent = sem("sent")

        z_v = x1.rearrange("(b t p) h -> b p t h", p=P, t=TB)
        block = ctx.enter_context(nc.Block())
        CHOSEN = 13
        SCORED = CHOSEN + 4
        ROUTE = SCORED + 6
        BATCH_DMA = 16 * 2 * TB

        def pairs(eng, b, step, behind_first=None):
            first = TB * b
            peeled = 4 if b == 0 else 2
            for n in range(first, first + peeled):
                step(n, n % 2, b)
                if n == first and b and behind_first:
                    behind_first(b - 1)
            with eng.Fori(peeled // 2, TB // 2 - 1) as i:
                step(2 * i + first, 0, b)
                step(2 * i + (first + 1), 1, b)
            step(first + TB - 2, 0, b)
            step(first + TB - 1, 1, b)

        def shared(n, b):
            return 0 <= n < EARLY if isinstance(n, int) else b < d.early

        def tile(n):
            return n if isinstance(n, int) else ds(n, 1)

        def span(n):
            return slice(n, n + 1) if isinstance(n, int) else ds(n, 1)

        def batch(n, b):
            return n // TB if isinstance(n, int) else b

        @block.sync
        def _(sp):
            for n, (dst, src) in enumerate(((rw_raw[:], router_w), (bias[:], router_bias.to_broadcast([P, E])),
                                            (sg_raw, shared_gate), (su_raw, shared_up), (sd_raw, shared_down))):
                sp.dma_start(dst, src).then_inc(w_loaded[n], 16)
            for b in range(NB):
                sp.dma_start(Z[:, TB * b:TB * b + TB, :], z_v[b]).then_inc(x_loaded, 16)
                sp.wait_ge(x_loaded, 16 * (b + 1))

        @block.gpsimd
        def _(pool):
            for b in range(NB):
                tb = slice(TB * b, TB * b + TB)
                pool.wait_ge(mv_done, TB * (b + 1))
                pool.tensor_scalar(veps[:, tb], mv[:, tb, 1], EPS, None, ALU.add).then_inc(veps_done, 1)
                pool.wait_ge(veps_done, b + 1)
                pool.tensor_tensor(rstd[:, tb], veps[:, tb], d.minus_half[:], ALU.pow).then_inc(rstd_done, 1)
            for b in range(NB - 1):
                pool.wait_ge(placed, 2 * b + 2)
                pool.wait_ge(copied, TB * (b + 1))
                dispatch(pool, d, h_rows[b % 2], b, sent)
            pool.wait_ge(sent, BATCH_DMA * (NB - 1))

        @block.scalar
        def _(act):
            def copy_rows(m, par, b):
                act.wait_ge(f.rows_ready, m + 1)
                if isinstance(m, int) and m == TB:
                    act.wait_ge(w_split, 4)
                if isinstance(m, int) and m % TB == 0 and b >= 2:
                    act.wait_ge(sent, BATCH_DMA * (b - 1))
                act.activation(h_rows[b % 2][:, tile(m - TB * b), :], h[:, par, :], ACT.Copy).then_inc(copied, 1)

            def step(n, par, b):
                if shared(n - 1, b):
                    f.act_products_high(act, n - 1, 1 - par)
                if inside(n + 1, NT):
                    f.act_rows_high(act, n + 1, 1 - par)
                if shared(n, b):
                    f.act_silu(act, n, par)
                if inside(n + 2, NT):
                    copy_rows(n + 2, par, batch(n + 2, b))

            for n, (raw_w, hi, lo) in enumerate(weights):
                act.wait_ge(w_loaded[WEIGHT_DMA[n]], 16)
                act.activation(hi[:], raw_w, ACT.Copy).then_inc(w_high, 1)
            copy_rows(0, 0, 0)
            copy_rows(1, 1, 0)
            f.act_rows_high(act, 0, 0)
            for b in range(NB):
                pairs(act, b, step)
                act.wait_ge(logit_done, TB * (b + 1))
                act.activation(probs[:], logits[:], ACT.Sigmoid).then_inc(prob_done, 1)

        @block.tensor
        def _(pe):
            columns = [(lambda c: sg_hi[:, c, :], lambda c: sg_lo[:, c, :]),
                       (lambda c: su_hi[:, c, :], lambda c: su_lo[:, c, :]),
                       (lambda c: sd_hi[:, c, :], lambda c: sd_lo[:, c, :])]

            def router(n, par):
                if inside(n - 1, NT):
                    pe.wait_ge(logit_done, n)
                pe.wait_ge(f.xT_lo_done, n + 1)
                for c in range(HC):
                    mm = product(pe, l_bank[:, 0:E], f.xT_hi[:, par, c, :], f.xT_lo[:, par, c, :],
                                 rw_hi[:, c, :], rw_lo[:, c, :], c == 0, c == HC - 1)
                mm.then_inc(logit_mm, 1)

            def step(n, par, b):
                if shared(n - 2, b):
                    f.pe_down(pe, n - 2, par, columns)
                if shared(n - 1, b):
                    f.pe_turn_products(pe, n - 1, 1 - par)
                if inside(n + 1, NT):
                    f.pe_turn_rows(pe, n + 1, 1 - par, h[:, 1 - par, :])
                if shared(n, b):
                    f.pe_gate_up(pe, n, par, columns)
                router(n, par)

            def ranks(b):
                pe.wait_ge(route, ROUTE * b + CHOSEN)
                flat = chosen_bf[:, :, :].rearrange("p t e -> p (t e)")
                W = TB * E
                pe.matmul(r_bank[:, 0:W], d.before[:], flat, start=True, stop=False)
                for s in range(1, TB):
                    pe.matmul(r_bank[:, E * s:W], d.ones[:], flat[:, 0:W - E * s], start=False, stop=s == TB - 1)
                for t in range(TB):
                    mm = pe.matmul(r_bank[:, W:W + E], d.ones[:], flat[:, E * t:E * t + E],
                                   start=(t == 0), stop=(t == TB - 1))
                mm.then_inc(rank_mm, 1)

            f.pe_turn_rows(pe, 0, 0, h[:, 0, :])
            pe.wait_ge(w_split, 4)
            for b in range(NB):
                pairs(pe, b, step, ranks)
            ranks(NB - 1)

        @block.vector
        def _(dve):
            def normalise(m, par, b):
                if isinstance(m, int) and m % TB == 0:
                    dve.wait_ge(rstd_done, b + 1)
                    dve.wait_ge(x_loaded, 16 * (b + 1))
                dve.tensor_scalar(norm[:, par, :], Z[:, tile(m), :], mv[:, tile(m), 0:1], rstd[:, span(m)],
                                  ALU.subtract, ALU.mult).then_inc(norm_done, 1)
                dve.wait_ge(norm_done, m + 1)
                dve.tensor_tensor(scaled[:, par, :], norm[:, par, :], rows[:, b, 2 * H:3 * H],
                                  ALU.mult).then_inc(scaled_done, 1)

            def shift(m, par, b):
                dve.wait_ge(scaled_done, m + 1)
                if inside(m - 2, NT):
                    dve.wait_ge(f.xT_mm, m - 1)
                    dve.wait_ge(copied, m - 1)
                dve.tensor_tensor(h[:, par, :], scaled[:, par, :], rows[:, b, H:2 * H],
                                  ALU.add).then_inc(f.rows_ready, 1)

            def add_logits(n, b):
                if isinstance(n, int) and n == 0:
                    dve.wait_ge(w_loaded[1], 16)
                dve.wait_ge(logit_mm, n + 1)
                dve.tensor_tensor(logits[:, tile(n - TB * b), :], l_bank[:, 0:E], bias[:],
                                  ALU.add).then_inc(logit_done, 1)

            def gated(m, par, b):
                dve.wait_ge(f.y_mm, m + 1)
                dve.tensor_tensor(gy[:, par, :], f.y_bank[par][:, 0:H], rows[:, b, 3 * H:4 * H],
                                  ALU.mult).then_inc(f.y_out, 1)

            def shared_out(m, par):
                dve.wait_ge(f.y_out, m + 1)
                dve.tensor_tensor(Z[:, tile(m), :], gy[:, par, :], Z[:, tile(m), :], ALU.add).then_inc(gy_done, 1)

            def step(n, par, b):
                if inside(n + 2, NT):
                    normalise(n + 2, par, batch(n + 2, b))
                if shared(n - 2, b):
                    gated(n - 2, par, batch(n - 2, b))
                if inside(n + 2, NT):
                    shift(n + 2, par, batch(n + 2, b))
                if shared(n - 2, b):
                    shared_out(n - 2, par)
                if shared(n - 1, b):
                    f.dve_products_low(dve, n - 1, 1 - par)
                if inside(n + 1, NT):
                    f.dve_rows_low(dve, n + 1, 1 - par)
                if shared(n, b):
                    f.dve_products(dve, n, par)
                add_logits(n, b)

            def choose(b):
                r = [ROUTE * b]

                def op(ins):
                    ins.then_inc(route, 1)
                    r[0] += 1
                    dve.wait_ge(route, r[0])

                wide = lambda v: v[:].unsqueeze(2).to_broadcast([P, TB, E])
                codes = d.codes[:].unsqueeze(1).to_broadcast([P, TB, E])
                dve.wait_ge(prob_done, b + 1)
                op(dve.tensor_reduce(best1[:], probs[:], AX_X, ALU.max))
                op(dve.tensor_tensor(same[:], probs[:], wide(best1), ALU.is_equal))
                op(dve.tensor_tensor(coded[:], same[:], codes, ALU.mult))
                op(dve.tensor_reduce(code1[:], coded[:], AX_X, ALU.max))
                op(dve.tensor_tensor(pick1[:], coded[:], wide(code1), ALU.is_equal))
                op(dve.scalar_tensor_tensor(out=rest[:], in0=pick1[:], scalar=-4.0, in1=probs[:],
                                            op0=ALU.mult, op1=ALU.add))
                op(dve.tensor_reduce(best2[:], rest[:], AX_X, ALU.max))
                op(dve.tensor_tensor(same[:], rest[:], wide(best2), ALU.is_equal))
                op(dve.tensor_tensor(coded[:], same[:], codes, ALU.mult))
                op(dve.tensor_reduce(code2[:], coded[:], AX_X, ALU.max))
                op(dve.tensor_tensor(pick2[:], coded[:], wide(code2), ALU.is_equal))
                op(dve.tensor_tensor(chosen[:], pick1[:], pick2[:], ALU.add))
                op(dve.tensor_copy(chosen_bf[:], chosen[:]))
                assert r[0] == ROUTE * b + CHOSEN
                tb = slice(TB * b, TB * b + TB)
                op(dve.tensor_tensor(total[:], best1[:], best2[:], ALU.add))
                op(dve.reciprocal(total[:], total[:]))
                op(dve.tensor_tensor(d.score[:, 0, tb], best1[:], total[:], ALU.mult))
                op(dve.tensor_tensor(d.score[:, 1, tb], best2[:], total[:], ALU.mult))
                assert r[0] == ROUTE * b + SCORED

            def place(b):
                r = [ROUTE * b + SCORED]

                def op(ins):
                    ins.then_inc(route, 1)
                    r[0] += 1
                    dve.wait_ge(route, r[0])

                tb = slice(TB * b, TB * b + TB)
                dve.wait_ge(rank_mm, b + 1)
                W = TB * E
                op(dve.tensor_tensor(slot[:], r_bank[:, 0:W].rearrange("p (t e) -> p t e", e=E),
                                     base[:, b, :].unsqueeze(1).to_broadcast([P, TB, E]), ALU.add))
                op(dve.tensor_tensor(base[:, b + 1, :], r_bank[:, W:W + E], base[:, b, :], ALU.add))
                for k, pick in enumerate((pick1, pick2)):
                    op(dve.tensor_tensor(coded[:], slot[:], pick[:], ALU.mult))
                    op(dve.tensor_reduce(d.place[:, k, tb], coded[:], AX_X, ALU.add))
                    dve.tensor_copy(d.place_i[:, k, tb], d.place[:, k, tb]).then_inc(placed, 1)
                assert r[0] == ROUTE * (b + 1)

            def aggregate(b):
                for t in range(TB * b, TB * b + TB):
                    dve.bn_aggr(mv[:, t, :], d.stats1[:, t, :]).then_inc(mv_done, 1)

            aggregate(0)
            dve.tensor_copy(base[:, 0, :], d.first_row[:, 0:E]).then_inc(d.base_set, 1)
            for n, (raw_w, hi, lo) in enumerate(weights):
                dve.wait_ge(w_high, n + 1)
                dve.tensor_tensor(lo[:], raw_w, hi[:].bitcast(F32), ALU.subtract).then_inc(w_split, 1)
            for n in range(2):
                normalise(n, n, 0)
                shift(n, n, 0)
            f.dve_rows_low(dve, 0, 0)
            for b in range(1, NB):
                aggregate(b)
            for b in range(NB):
                pairs(dve, b, step, place)
                choose(b)
            place(NB - 1)


def experts_phase(nc, d, gate_w, up_w, down_w):
    E, _, HC, I = gate_w.shape
    H = HC * P
    IC = I // P
    NBLK = d.blocks
    W = HC * I

    with ExitStack() as ctx:
        sb = lambda n, s, t: ctx.enter_context(nc.sbuf_tensor(n, s, t))
        sem = lambda n: ctx.enter_context(nc.semaphore(n))
        f = gated_blocks(ctx, nc, d, "e", NBLK, H, I)
        w_raw = sb("e_w_raw", [P, 3 * W], F32)
        w_hi = sb("e_w_hi", [P, 2, 3 * W], F32R)
        w_lo = sb("e_w_lo", [P, 2, 3 * W], F32R)
        h = sb("e_h", [P, 2, H], F32)
        y = sb("e_y", [P, 2, H], F32)
        zeros = sb("zeros", [P, H], F32)
        count = sb("count", [P, E], F32)
        over = sb("over", [P, E, d.most], F32)
        nblocks = sb("nblocks", [P, E], F32)
        ends = sb("ends", [P, E], F32)
        rows_of = sb("rows_of", [P, d.place.shape[1] * d.place.shape[2]], F32)
        moved = sb("moved", [P, d.place.shape[1] * d.place.shape[2]], F32)
        starts = sb("starts", [P, E + 1], F32)
        shift = sb("shift", [P, E + 1], F32)
        jump = sb("jump", [P, E], F32)
        behind = sb("behind", [1, NBLK, E], F32)
        jumped = sb("jumped", [1, NBLK, E], F32)
        moved_by = sb("moved_by", [1, NBLK], F32)
        expert_of = sb("expert_of", [1, NBLK + 2], F32)
        packed = sb("packed", [1, 3, NBLK // 2], F32)
        row0 = sb("row0", [1, NBLK], F32)
        table = sb("table", [1, 2, NBLK], I32)
        free_i = sb("free_i", [1, E], I32)
        ends_i = sb("ends_i", [1, E], I32)

        w_loaded, w_split = sem("e_w_loaded"), sem("e_w_split")
        zeroed, padded, moving = sem("zeroed"), sem("padded"), sem("moving")
        plan, last_sent = sem("plan"), sem("last_sent")
        first_loaded = sem("first_loaded")
        h_in = [sem("h_in0"), sem("h_in1")]
        y_stored = [sem("y_stored0"), sem("y_stored1")]
        PLAN = 20 + E
        LOG_E = E.bit_length() - 1

        block = ctx.enter_context(nc.Block())
        half = lambda m, par: m // 2 if isinstance(m, int) else (m - par) // 2

        def steps(eng, step):
            for n in range(4):
                step(n, n % 2)
            with eng.Fori(2, NBLK // 2 - 1) as i:
                step(2 * i, 0)
                step(2 * i + 1, 1)
            step(NBLK - 2, 0)
            step(NBLK - 1, 1)

        def at(m):
            return slice(m, m + 1) if isinstance(m, int) else ds(m, 1)

        def first_row(eng, m):
            return eng.value_load(table[0:1, 0, at(m)], min_val=0, max_val=d.all_rows - P)

        @block.sync
        def _(sp):
            for m, src in enumerate((gate_w, up_w, down_w)):
                sp.dma_start(w_raw[:, W * m:W * m + W], src[0].rearrange("p a b -> p (a b)")).then_inc(first_loaded, 16)
            sp.wait_ge(zeroed, 2)
            sp.wait_ge(plan, PLAN)
            for e in range(E):
                row = sp.value_load(free_i[0:1, e:e + 1], min_val=0, max_val=d.all_rows - P)
                sp.dma_start(d.x_rows[ds(row, P), :], zeros[:]).then_inc(padded, 16)
            for i in range(E):
                r = d.spare_row + P * i
                sp.dma_start(d.x_rows[r:r + P, :], zeros[:]).then_inc(padded, 16)
            sp.wait_ge(padded, 32 * E)
            sp.wait_ge(last_sent, 16 * 2 * d.last_rows.shape[1])

            def load(m, par):
                row = first_row(sp, m)
                sp.dma_start(h[:, par, :], d.x_rows[ds(row, P), :]).then_inc(h_in[par], 16)

            def store(m, par):
                sp.wait_ge(f.y_out, m + 1)
                rows = slice(P * m, P * m + P) if isinstance(m, int) else ds(P * m, P)
                sp.dma_start(d.y_rows[rows, :], y[:, par, :]).then_inc(y_stored[par], 16)

            def step(n, par):
                if inside(n + 2, NBLK):
                    hold(sp, d, f.xT_mm, n + 1)
                    load(n + 2, par)
                if inside(n - 2, NBLK):
                    store(n - 2, par)

            load(0, 0)
            load(1, 1)
            steps(sp, step)
            store(NBLK - 2, 0)
            store(NBLK - 1, 1)
            for s in y_stored:
                sp.wait_ge(s, 16 * (NBLK // 2))

        @block.gpsimd
        def _(pool):
            pool.memset(zeros[:], 0.0).then_inc(zeroed, 1)
            pool.tensor_copy(rows_of[:], d.place[:, :, :].rearrange("p k t -> p (k t)")).then_inc(zeroed, 1)
            dispatch(pool, d, d.last_rows, d.NB - 1, last_sent)
            for e in range(1, E):
                if e == 1:
                    pool.wait_ge(w_split, 2)
                for m, src in enumerate((gate_w, up_w, down_w)):
                    pool.dma_start(w_raw[:, W * m:W * m + W], src[e].rearrange("p a b -> p (a b)")).then_inc(w_loaded, 16)
                pool.wait_ge(w_loaded, 48 * e)
                if e >= 2:
                    pool.wait_ge(plan, PLAN)
                    end = pool.value_load(ends_i[0:1, e - 2:e - 1], min_val=1, max_val=NBLK)
                    hold(pool, d, f.y_mm, end)
                split_weights(pool, w_raw[:], w_hi[:, e % 2, :], w_lo[:, e % 2, :], w_split, 2 * e)
                pool.wait_ge(w_split, 2 * e + 2)
            flat = d.place[:, :, :].rearrange("p k t -> p (k t)")
            for e in range(E):
                if e == 0:
                    pool.tensor_scalar(moved[:], flat, 0.0, shift[:, 0:1], ALU.is_ge, ALU.mult).then_inc(moving, 1)
                else:
                    pool.tensor_scalar(moved[:], rows_of[:], float(e * d.capacity), jump[:, e - 1:e],
                                       ALU.is_ge, ALU.mult).then_inc(moving, 1)
                pool.wait_ge(moving, 2 * e + 1)
                pool.tensor_tensor(flat, flat, moved[:], ALU.subtract).then_inc(moving, 1)
                if e < E - 1:
                    pool.wait_ge(moving, 2 * e + 2)
            pool.wait_ge(moving, 2 * E)
            pool.tensor_copy(d.place_i[:, :, :].rearrange("p k t -> p (k t)"), flat).then_inc(moving, 1)

        @block.scalar
        def _(act):
            def output(m, par):
                act.wait_ge(f.y_mm, m + 1)
                if inside(m - 2, NBLK):
                    hold(act, d, y_stored[par], 16 * half(m, par))
                act.activation(y[:, par, :], f.y_bank[par][:, 0:H], ACT.Copy).then_inc(f.y_out, 1)

            def step(n, par):
                if inside(n - 2, NBLK):
                    output(n - 2, par)
                if inside(n - 1, NBLK):
                    f.act_products_high(act, n - 1, 1 - par)
                if inside(n + 1, NBLK):
                    f.act_rows_high(act, n + 1, 1 - par)
                f.act_silu(act, n, par)

            f.act_rows_high(act, 0, 0)
            steps(act, step)
            output(NBLK - 2, 0)
            f.act_products_high(act, NBLK - 1, 1)
            output(NBLK - 1, 1)

        @block.tensor
        def _(pe):
            def weights(e):
                def columns(t, o, n):
                    return lambda c: t[:, ds(e & 1, 1), o + n * c:o + n * c + n]

                return [tuple(columns(t, W * k, n) for t in (w_hi, w_lo)) for k, n in enumerate((I, I, H))]

            def experts(i):
                packed = pe.value_load(table[0:1, 1, at(i)], min_val=0, max_val=E ** 4 - 1)
                return [(packed >> (LOG_E * k)) & (E - 1) for k in range(4)]

            def step(n, par):
                if par == 0:
                    who[:] = experts(n // 2 if isinstance(n, int) else half(n, 0))
                e = who[2 + par]
                if inside(n - 2, NBLK):
                    f.pe_down(pe, n - 2, par, weights(who[par]))
                if inside(n - 1, NBLK):
                    f.pe_turn_products(pe, n - 1, 1 - par)
                if inside(n + 1, NBLK):
                    turn_rows(n + 1, 1 - par)
                pe.wait_ge(w_split, 2 * e + 2)
                f.pe_gate_up(pe, n, par, weights(e))

            who = []
            def turn_rows(m, par):
                f.rows_ready = h_in[par]
                f.ready_at = lambda m: 16 * half(m, par) + 16
                f.pe_turn_rows(pe, m, par, h[:, par, :])

            turn_rows(0, 0)
            pe.wait_ge(plan, PLAN)
            steps(pe, step)
            f.pe_down(pe, NBLK - 2, 0, weights(who[2]))
            f.pe_turn_products(pe, NBLK - 1, 1)
            f.pe_down(pe, NBLK - 1, 1, weights(who[3]))

        @block.vector
        def _(dve):
            p = [0]

            def op(ins):
                ins.then_inc(plan, 1)
                p[0] += 1
                dve.wait_ge(plan, p[0])

            c = d.consts
            op(dve.tensor_tensor(count[:], d.base[:, d.NB, :], d.first_row[:, 0:E], ALU.subtract))
            op(dve.tensor_tensor(over[:], count[:].unsqueeze(2).to_broadcast([P, E, d.most]),
                                 c.limits[:].unsqueeze(1).to_broadcast([P, E, d.most]), ALU.is_gt))
            op(dve.tensor_reduce(nblocks[:], over[:], AX_X, ALU.add))
            op(dve.tensor_copy(ends[:], nblocks[:]))
            for e in range(1, E):
                op(dve.tensor_tensor(ends[:, e:e + 1], ends[:, e - 1:e], nblocks[:, e:e + 1], ALU.add))
            op(dve.memset(starts[:, 0:1], 0.0))
            op(dve.tensor_copy(starts[:, 1:E + 1], ends[:]))
            op(dve.scalar_tensor_tensor(out=shift[:], in0=starts[:], scalar=-float(P), in1=d.first_row[:, 0:E + 1],
                                        op0=ALU.mult, op1=ALU.add))
            op(dve.tensor_tensor(jump[:], shift[:, 1:E + 1], shift[:, 0:E], ALU.subtract))
            op(dve.tensor_tensor(behind[:], c.numbers[:].unsqueeze(2).to_broadcast([1, NBLK, E]),
                                 ends[0:1].unsqueeze(1).to_broadcast([1, NBLK, E]), ALU.is_ge))
            op(dve.tensor_tensor(jumped[:], behind[:], jump[0:1].unsqueeze(1).to_broadcast([1, NBLK, E]), ALU.mult))
            op(dve.tensor_reduce(moved_by[:], jumped[:], AX_X, ALU.add))
            op(dve.scalar_tensor_tensor(out=row0[:], in0=c.numbers[:], scalar=float(P), in1=moved_by[:],
                                        op0=ALU.mult, op1=ALU.add))
            op(dve.tensor_copy(table[:, 0], row0[:]))
            op(dve.memset(expert_of[:, 0:2], 0.0))
            op(dve.tensor_reduce(expert_of[:, 2:], behind[:, :, 0:E - 1], AX_X, ALU.add))
            by_pair = expert_of[:].rearrange("o (i two) -> o i two", two=2)
            digit = [by_pair[:, 0:NBLK // 2, 0], by_pair[:, 0:NBLK // 2, 1],
                     by_pair[:, 1:NBLK // 2 + 1, 0], by_pair[:, 1:NBLK // 2 + 1, 1]]
            so_far = digit[3]
            for k in (2, 1, 0):
                op(dve.scalar_tensor_tensor(out=packed[:, k], in0=so_far, scalar=float(E), in1=digit[k],
                                            op0=ALU.mult, op1=ALU.add))
                so_far = packed[:, k]
            op(dve.tensor_copy(table[:, 1, 0:NBLK // 2], packed[:, 0]))
            op(dve.tensor_copy(free_i[:], d.base[0:1, d.NB, :]))
            op(dve.tensor_copy(ends_i[:], ends[0:1]))
            assert p[0] == PLAN
            dve.wait_ge(first_loaded, 48)
            split_weights(dve, w_raw[:], w_hi[:, 0, :], w_lo[:, 0, :], w_split, 0)

            def step(n, par):
                if inside(n - 1, NBLK):
                    f.dve_products_low(dve, n - 1, 1 - par)
                if inside(n + 1, NBLK):
                    f.dve_rows_low(dve, n + 1, 1 - par)
                f.dve_products(dve, n, par)

            f.dve_rows_low(dve, 0, 0)
            steps(dve, step)
            f.dve_products_low(dve, NBLK - 1, 1)


def last_phase(nc, d, shared_gate, shared_up, shared_down, out):
    H = out.shape[3]
    I = shared_gate.shape[2]
    HC, IC = H // P, I // P
    NT, TB = d.NT, d.NT // d.NB
    EARLY = TB * d.early
    LATE = NT - EARLY
    DEPTH = 4
    with ExitStack() as ctx:
        sb = lambda n, s, t: ctx.enter_context(nc.sbuf_tensor(n, s, t))
        sem = lambda n: ctx.enter_context(nc.semaphore(n))
        f = gated_blocks(ctx, nc, d, "l", LATE, H, I)
        f.ready_at = lambda m: m + 1
        matrix = lambda n, a, c, t: sb(n, [P, a, c], t)
        g_raw, g_hi, g_lo = (matrix("l_g_" + n, HC, I, t) for n, t in (("raw", F32), ("hi", F32R), ("lo", F32R)))
        u_raw, u_hi, u_lo = (matrix("l_u_" + n, HC, I, t) for n, t in (("raw", F32), ("hi", F32R), ("lo", F32R)))
        w_raw, w_hi, w_lo = (matrix("l_d_" + n, IC, H, t) for n, t in (("raw", F32), ("hi", F32R), ("lo", F32R)))
        y1, y2 = sb("y1", [P, 2, DEPTH, H], F32), sb("y2", [P, 2, DEPTH, H], F32)
        first = sb("first", [P, 2, 2, H], F32)
        both = sb("both", [P, 2, 2, H], F32)
        with_shared = sb("with_shared", [P, 2, H], F32)
        gated = sb("l_gated", [P, 2, 2, H], F32)
        offset = sb("offset", [P, LATE], F32)
        norm = sb("l_norm", [P, 2, H], F32)
        scaled = sb("l_scaled", [P, 2, H], F32)
        h = sb("l_h", [P, 2, H], F32)

        w_loaded = [sem(f"l_w_loaded{i}") for i in range(3)]
        w_high, w_split = sem("l_w_high"), sem("l_w_split")
        offset_done, norm_done, scaled_done = sem("offset_done"), sem("l_norm_done"), sem("l_scaled_done")
        y_in = [[sem(f"y_in{g}_{i}") for i in range(DEPTH)] for g in range(2)]
        two = lambda n: [sem(n + "_early"), sem(n + "_late")]
        first_done, both_done, gated_done, out_done = (two(n) for n in ("first", "both", "gated", "out_done"))
        stored = sem("stored")
        weights = ((g_raw, g_hi, g_lo), (u_raw, u_hi, u_lo), (w_raw, w_hi, w_lo))
        block = ctx.enter_context(nc.Block())

        def tile(g, i):
            return EARLY * g + i

        def gate_row(n):
            return d.mod_rows[:, n // TB, 3 * H:4 * H]

        @block.gpsimd
        def _(pool):
            for i in range(LATE):
                for g in range(2):
                    if i >= DEPTH:
                        pool.wait_ge(both_done[g], i - DEPTH + 1)
                    for k, y in enumerate((y1, y2)):
                        n = tile(g, i)
                        pool.indirect_dma_start(
                            y[:, g, i % DEPTH, :], None, d.y_rows,
                            bass.IndirectOffsetOnAxis(ap=d.place_i[:, k, n:n + 1], axis=0)
                        ).then_inc(y_in[g][i % DEPTH], 16)

        @block.sync
        def _(sp):
            for n, src in enumerate((shared_gate, shared_up, shared_down)):
                sp.dma_start(weights[n][0][:], src).then_inc(w_loaded[n], 16)
            for i in range(LATE // 4):
                for g in range(2):
                    n = tile(g, 4 * i)
                    sp.wait_ge(out_done[g], 4 * i + 4)
                    sp.dma_start(out[n // TB, :, n % TB:n % TB + 4, :], d.Z[:, n:n + 4, :]).then_inc(stored, 16)
            sp.wait_ge(stored, 16 * (NT // 4))

        @block.scalar
        def _(act):
            def normalise(i):
                if i >= 2:
                    act.wait_ge(scaled_done, i - 1)
                n = tile(1, i)
                act.activation(norm[:, i % 2, :], d.Z[:, n, :], ACT.Identity, scale=d.rstd[:, n:n + 1],
                               bias=offset[:, i:i + 1]).then_inc(norm_done, 1)

            def first_score(g, i):
                act.wait_ge(y_in[g][i % DEPTH], 32 * (i // DEPTH) + 32)
                if i >= 2:
                    act.wait_ge(both_done[g], i - 1)
                n = tile(g, i)
                act.activation(first[:, g, i % 2, :], y1[:, g, i % DEPTH, :], ACT.Copy,
                               scale=d.score[:, 0, n:n + 1]).then_inc(first_done[g], 1)

            act.wait_ge(offset_done, 1)
            normalise(0)
            normalise(1)
            for n, (raw, hi, lo) in enumerate(weights):
                act.wait_ge(w_loaded[n], 16)
                act.activation(hi[:], raw[:], ACT.Copy).then_inc(w_high, 1)
            f.act_rows_high(act, 0, 0)
            for i in range(LATE):
                par = i % 2
                if i + 2 < LATE:
                    normalise(i + 2)
                if i:
                    f.act_products_high(act, i - 1, 1 - par)
                if i + 1 < LATE:
                    f.act_rows_high(act, i + 1, 1 - par)
                first_score(0, i)
                if i >= 1:
                    first_score(1, i - 1)
                f.act_silu(act, i, par)
            f.act_products_high(act, LATE - 1, 1)
            first_score(1, LATE - 1)

        @block.tensor
        def _(pe):
            columns = [(lambda c: g_hi[:, c, :], lambda c: g_lo[:, c, :]),
                       (lambda c: u_hi[:, c, :], lambda c: u_lo[:, c, :]),
                       (lambda c: w_hi[:, c, :], lambda c: w_lo[:, c, :])]

            def step(i, par):
                if inside(i - 2, LATE):
                    f.pe_down(pe, i - 2, par, columns)
                if inside(i - 1, LATE):
                    f.pe_turn_products(pe, i - 1, 1 - par)
                if inside(i + 1, LATE):
                    f.pe_turn_rows(pe, i + 1, 1 - par, h[:, 1 - par, :])
                f.pe_gate_up(pe, i, par, columns)

            f.pe_turn_rows(pe, 0, 0, h[:, 0, :])
            pe.wait_ge(w_split, 3)
            for i in range(4):
                step(i, i % 2)
            with pe.Fori(2, LATE // 2 - 1) as i:
                step(2 * i, 0)
                step(2 * i + 1, 1)
            step(LATE - 2, 0)
            step(LATE - 1, 1)
            f.pe_down(pe, LATE - 2, 0, columns)
            f.pe_turn_products(pe, LATE - 1, 1)
            f.pe_down(pe, LATE - 1, 1, columns)

        @block.vector
        def _(dve):
            def scale(i):
                row = d.mod_rows[:, tile(1, i) // TB, 2 * H:3 * H]
                dve.wait_ge(norm_done, i + 1)
                dve.tensor_tensor(scaled[:, i % 2, :], norm[:, i % 2, :], row, ALU.mult).then_inc(scaled_done, 1)

            def shift(i):
                row = d.mod_rows[:, tile(1, i) // TB, H:2 * H]
                dve.wait_ge(scaled_done, i + 1)
                if i >= 2:
                    dve.wait_ge(f.xT_mm, i - 1)
                dve.tensor_tensor(h[:, i % 2, :], scaled[:, i % 2, :], row, ALU.add).then_inc(f.rows_ready, 1)

            def both_scores(g, i):
                n = tile(g, i)
                dve.wait_ge(first_done[g], i + 1)
                dve.scalar_tensor_tensor(out=both[:, g, i % 2, :], in0=y2[:, g, i % DEPTH, :],
                                         scalar=d.score[:, 1, n:n + 1], in1=first[:, g, i % 2, :],
                                         op0=ALU.mult, op1=ALU.add).then_inc(both_done[g], 1)

            def add_shared(i):
                dve.wait_ge(both_done[1], i + 1)
                dve.wait_ge(f.y_mm, i + 1)
                dve.tensor_tensor(with_shared[:, i % 2, :], f.y_bank[i % 2][:, 0:H], both[:, 1, i % 2, :],
                                  ALU.add).then_inc(f.y_out, 1)

            def gate(g, i):
                if g:
                    dve.wait_ge(f.y_out, i + 1)
                else:
                    dve.wait_ge(both_done[0], i + 1)
                src = with_shared[:, i % 2, :] if g else both[:, 0, i % 2, :]
                dve.tensor_tensor(gated[:, g, i % 2, :], src, gate_row(tile(g, i)), ALU.mult).then_inc(gated_done[g], 1)

            def output(g, i):
                n = tile(g, i)
                dve.wait_ge(gated_done[g], i + 1)
                dve.tensor_tensor(d.Z[:, n, :], gated[:, g, i % 2, :], d.Z[:, n, :], ALU.add).then_inc(out_done[g], 1)

            dve.scalar_tensor_tensor(out=offset[:], in0=d.mv[:, EARLY:, 0], scalar=-1.0, in1=d.rstd[:, EARLY:],
                                     op0=ALU.mult, op1=ALU.mult).then_inc(offset_done, 1)
            for i in range(2):
                scale(i)
                shift(i)
            for n, (raw, hi, lo) in enumerate(weights):
                dve.wait_ge(w_high, n + 1)
                dve.tensor_tensor(lo[:], raw[:], hi[:].bitcast(F32), ALU.subtract).then_inc(w_split, 1)
            f.dve_rows_low(dve, 0, 0)
            for i in range(LATE):
                par = i % 2
                if i >= 1:
                    both_scores(0, i - 1)
                if i + 2 < LATE:
                    scale(i + 2)
                if i >= 1:
                    gate(0, i - 1)
                if i + 2 < LATE:
                    shift(i + 2)
                if i >= 1:
                    output(0, i - 1)
                if i >= 2:
                    both_scores(1, i - 2)
                if i >= 1:
                    f.dve_products_low(dve, i - 1, 1 - par)
                if i >= 2:
                    add_shared(i - 2)
                if i + 1 < LATE:
                    f.dve_rows_low(dve, i + 1, 1 - par)
                if i >= 2:
                    gate(1, i - 2)
                f.dve_products(dve, i, par)
                if i >= 2:
                    output(1, i - 2)
            i = LATE - 1
            both_scores(0, i)
            f.dve_products_low(dve, i, 1)
            both_scores(1, i - 1)
            gate(0, i)
            add_shared(i - 1)
            output(0, i)
            gate(1, i - 1)
            both_scores(1, i)
            output(1, i - 1)
            add_shared(i)
            gate(1, i)
            output(1, i)


def constants(nc, d, sb, sem, E, NBLK):
    d.ident = sb("ident", [P, P], F32)
    d.minus_half = sb("minus_half", [P, 16], F32)
    d.before = sb("before", [P, P], BF16)
    d.ones = sb("ones", [P, P], BF16)
    d.codes = sb("codes", [P, E], F32)
    d.first_row = sb("first_row", [P, E + 1], F32)
    d.consts = c = Namespace()
    c.limits = sb("limits", [P, d.most], F32)
    c.numbers = sb("numbers", [1, NBLK], F32)
    d.s_const = sem("s_const")
    sets = [(d.ident[:], 0.0), (d.minus_half[:], -0.5), (d.before[:], 1.0), (d.ones[:], 1.0),
            (c.limits[:, 0:1], -1.0)]
    sets += [(d.codes[:, e:e + 1], float(E - e)) for e in range(E)]
    sets += [(d.first_row[:, e:e + 1], float(d.capacity * e)) for e in range(E + 1)]
    d.n_const = len(sets) + 4
    with nc.Block() as block:
        @block.gpsimd
        def _(pool):
            for out, v in sets:
                pool.memset(out, v).then_inc(d.s_const, 1)
            pool.wait_ge(d.s_const, len(sets))
            pool.affine_select(out=d.ident[:], in_=d.ident[:], compare_op=ALU.not_equal, fill=1.0, base=0,
                               pattern=[[-1, P]], channel_multiplier=1).then_inc(d.s_const, 1)
            pool.affine_select(out=d.before[:], in_=d.before[:], compare_op=ALU.is_gt, fill=0.0, base=0,
                               pattern=[[1, P]], channel_multiplier=-1).then_inc(d.s_const, 1)
            pool.iota(c.limits[:, 1:], pattern=[[P, d.most - 1]], base=P, channel_multiplier=0,
                      allow_small_or_imprecise_dtypes=True).then_inc(d.s_const, 1)
            pool.iota(c.numbers[:], pattern=[[1, NBLK]], base=0, channel_multiplier=0,
                      allow_small_or_imprecise_dtypes=True).then_inc(d.s_const, 1)
            pool.wait_ge(d.s_const, d.n_const)


def layer(nc, x, mask, cT_in, wmod, wqkv, wo, shared_gate, shared_up, shared_down, router_w, router_bias,
          gate_w, up_w, down_w, out):
    d = Namespace()
    NB, S, H = x.shape
    E = router_w.shape[2]
    T = NB * S
    TOP = 2
    d.NB, d.NT, d.E = NB, T // P, E
    d.capacity = T + P
    d.spare_row = E * d.capacity
    d.all_rows = d.spare_row + E * P
    d.most = T // P
    d.blocks = TOP * T // P + E
    d.x1 = nc.dram_tensor("x1", (T, H), F32, kind="Internal").ap()
    d.x_rows = nc.dram_tensor("x_rows", (d.all_rows, H), F32, kind="Internal").ap()
    d.y_rows = nc.dram_tensor("y_rows", (d.blocks * P, H), F32, kind="Internal").ap()
    with ExitStack() as ctx:
        sb = lambda n, s, t: ctx.enter_context(nc.sbuf_tensor(n, s, t))
        sem = lambda n: ctx.enter_context(nc.semaphore(n))
        d.mod_rows = sb("mod_rows", [P, NB, 4 * H], F32)
        d.stats1 = sb("stats1", [P, T // P, 6], F32)
        d.base = sb("base", [P, NB + 1, E], F32)
        d.place_i = sb("place_i", [P, TOP, T // P], I32)
        d.place = sb("place", [P, TOP, T // P], F32)
        d.score = sb("score", [P, TOP, T // P], F32)
        d.s_gate = sem("s_gate")
        d.passed = sem("passed")
        d.stats1_done = sem("stats1_done")
        d.base_set = sem("base_set")
        constants(nc, d, sb, sem, E, d.blocks)
        attention_phase(nc, d, x, cT_in, wmod, wqkv, wo, mask)
        d.Z = sb("Z", [P, T // P, H], F32)
        d.early = NB // 2
        d.mv = sb("s_mv", [P, T // P, 2], F32)
        d.rstd = sb("s_rstd", [P, T // P], F32)
        d.last_rows = sb("last_rows", [P, T // P // NB, H], F32)
        shared_phase(nc, d, d.x1, shared_gate, shared_up, shared_down, router_w, router_bias)
        experts_phase(nc, d, gate_w, up_w, down_w)
        last_phase(nc, d, shared_gate, shared_up, shared_down, out.rearrange("b (t p) h -> b p t h", p=P))


def kernel(**inputs):
    from concourse import bacc
    from concourse.bass_utils import run_bass_kernel_spmd

    a = {k[3:]: np.asarray(v) for k, v in inputs.items()}
    c = np.ascontiguousarray
    H = a["wmod"].shape[0]
    E, _, I = a["ffn_gate_w"].shape

    def on_partitions(w):
        return c(w.reshape(w.shape[0] // P, P, -1).transpose(1, 0, 2))

    def each_on_partitions(w):
        return c(w.reshape(E, w.shape[1] // P, P, -1).transpose(0, 2, 1, 3))

    arrays = {
        "x": c(a["attn_x"]),
        "mask": c(a["attn_head_dim_mask"].reshape(P, 1)),
        "cT": on_partitions(a["c"].T),
        "wmod": c(a["wmod"]),
        "wqkv": on_partitions(np.concatenate([a["attn_w_q"], a["attn_w_k"], a["attn_w_v"]], 1)),
        "wo": c(a["attn_w_o"]),
        "shared_gate": on_partitions(a["ffn_shared_gate"].T),
        "shared_up": on_partitions(a["ffn_shared_up"].T),
        "shared_down": on_partitions(a["ffn_shared_down"].T),
        "router_w": on_partitions(a["ffn_router_w"].T),
        "router_bias": c(a["ffn_routing_bias"].reshape(1, E)),
        "gate_w": each_on_partitions(a["ffn_gate_w"]),
        "up_w": each_on_partitions(a["ffn_up_w"]),
        "down_w": each_on_partitions(a["ffn_down_w"]),
    }
    nc = bacc.Bacc("TRN2", target_bir_lowering=False, num_devices=1)
    aps = [nc.dram_tensor(f"in_{k}", v.shape, mybir.dt.from_np(v.dtype), kind="ExternalInput").ap()
           for k, v in arrays.items()]
    out = nc.dram_tensor("out_0", a["attn_x"].shape, F32, kind="ExternalOutput").ap()
    layer(nc, *aps, out)
    r = run_bass_kernel_spmd(nc, [{f"in_{k}": v for k, v in arrays.items()}], core_ids=[0])
    return r.results[0]["out_0"]
```

```python
from contextlib import ExitStack

import numpy as np

import concourse.bass as bass
from concourse import mybir

F32 = mybir.dt.float32
F32R = mybir.dt.float32r
BF16 = mybir.dt.bfloat16
I32 = mybir.dt.int32
U32 = mybir.dt.uint32
ALU = mybir.AluOpType
ACT = mybir.ActivationFunctionType
AX_X = mybir.AxisListType.X

P = 128
EPS = 1e-5
FLOOR = 0.25
ds = bass.ds


def product(pe, out, l_hi, l_lo, r_hi, r_lo, first=True, last=True):
    pe.matmul(out, l_hi, r_hi, start=first, stop=False)
    pe.matmul(out, l_hi, r_lo, start=False, stop=False)
    return pe.matmul(out, l_lo, r_hi, start=False, stop=last)


def hold(eng, d, semaphore, value):
    eng.wait_ge(semaphore, value)
    eng.sem_inc(d.passed, 1)


def attention_phase(nc, d, x, cT_in, wmod, wqkv, wo, mask):
    NB, S, H = x.shape
    D = P
    HC = H // P
    NT = S // P
    NBLK = S // 512
    GQ = 256
    NG = S // GQ
    SCALE = float(D) ** -0.5
    MOD_FIXED = 4
    PV_STEPS = (7, 1, 0, 0)

    with ExitStack() as ctx:
        sb = lambda n, s, t: ctx.enter_context(nc.sbuf_tensor(n, s, t))
        sem = lambda n: ctx.enter_context(nc.semaphore(n))
        bank = [ctx.enter_context(nc.psum_tensor(f"a_bank{i}", [P, 512], F32)) for i in range(8)]
        s_bank, t_bank, o_bank = bank[0:4], bank[4:6], bank[6:8]
        rows, ident = d.mod_rows, d.ident

        X = sb("X", [P, 2, NT, H], F32)
        w_hi = sb("w_hi", [P, HC, 3 * D], F32R)
        w_lo = sb("w_lo", [P, HC, 3 * D], F32R)
        wo_masked = sb("wo_masked", [P, H], F32)
        wo_hi = sb("wo_hi", [P, H], F32R)
        wo_lo = sb("wo_lo", [P, H], F32R)
        mask_i = sb("mask_i", [P, 1], I32)
        mask_f = sb("mask_f", [P, 1], F32)
        cT = sb("cT", [P, HC, NB], F32)
        ce = sb("ce", [P, HC, NB], F32)
        silu_rows = sb("silu_rows", [P, HC, NB, P], F32)
        mod_cols = sb("mod_cols", [P, 2, HC, NB], F32)
        stats = sb("stats", [P, NT, 6], F32)
        mv = sb("mv", [P, NT, 2], F32)
        veps = sb("veps", [P, NT], F32)
        rstd = sb("rstd", [P, NT], F32)
        vt = sb("vt", [P, 2, 512], F32)
        wo_gated = vt[:, 0, 0:H]
        kT_hi = sb("kT_hi", [P, S], F32R)
        kT_lo = sb("kT_lo", [P, S], F32R)
        qT_hi = sb("qT_hi", [P, S], F32R)
        qT_lo = sb("qT_lo", [P, S], F32R)
        v_hi = sb("v_hi", [P, NT, D], F32R)
        v_lo = sb("v_lo", [P, NT, D], F32R)
        q_hi = sb("q_hi", [P, 2, GQ], F32R)
        q_lo = sb("q_lo", [P, 2, GQ], F32R)
        prob = sb("prob", [P, 2, S], F32)
        xhat = prob[:, :, :].rearrange("p a (t h) -> p (a t) h", h=H)
        flat = prob[:, :, :].rearrange("p a s -> p (a s)")
        wmod_sb = flat[:, 0:HC * 6 * H].rearrange("p (k n) -> p k n", k=HC)
        w_raw = flat[:, HC * 6 * H:HC * (6 * H + 3 * D)].rearrange("p (k n) -> p k n", k=HC)
        wo_raw = flat[:, HC * (6 * H + 3 * D):HC * (6 * H + 3 * D) + H]
        pT_hi = sb("pT_hi", [P, 2, NT, GQ], F32R)
        pT_lo = sb("pT_lo", [P, 2, NT, GQ], F32R)
        hT_hi = pT_hi[:, 0, :, :].rearrange("p k q -> p (k q)").rearrange("p (c s) -> p c s", c=HC)
        hT_lo = pT_lo[:, 0, :, :].rearrange("p k q -> p (k q)").rearrange("p (c s) -> p c s", c=HC)
        oT_hi = sb("oT_hi", [P, 2, GQ], F32R)
        oT_lo = sb("oT_lo", [P, 2, GQ], F32R)
        bmax = sb("bmax", [P, 2, 4], F32)
        negmax = sb("negmax", [P, 2], F32)
        esum = sb("esum", [P, 2, 2, 4], F32)
        den = sb("den", [P, 2, 2], F32)
        rden = sb("rden", [P, 2, 2], F32)

        w_loaded = sem("w_loaded")
        x_loaded = sem("x_loaded")
        x1_stored = sem("x1_stored")
        exp_c = sem("exp_c")
        silu_c = sem("silu_c")
        w_split = sem("w_split")
        mod_mm = sem("mod_mm")
        mod_out = sem("mod_out")
        mod_fix = sem("mod_fix")
        ga_fix = sem("ga_fix")
        stats_done = sem("stats_done")
        mv_done = sem("mv_done")
        veps_done = sem("veps_done")
        rstd_done = sem("rstd_done")
        xhat_done = sem("xhat_done")
        hT_mm = sem("hT_mm")
        vt_done = sem("vt_done")
        hT_hi_done = sem("hT_hi_done")
        hT_lo_done = sem("hT_lo_done")
        qkv_mm = sem("qkv_mm")
        qkv_hi = sem("qkv_hi")
        qkv_lo = sem("qkv_lo")
        q_copied = sem("q_copied")
        s_mm = sem("s_mm")
        bmax_done = sem("bmax_done")
        negmax_done = sem("negmax_done")
        exp_done = sem("exp_done")
        pT_mm = sem("pT_mm")
        pT_hi_done = sem("pT_hi_done")
        pT_lo_done = sem("pT_lo_done")
        den_done = sem("den_done")
        rden_done = sem("rden_done")
        o_mm = sem("o_mm")
        oT_hi_done = sem("oT_hi_done")
        oT_lo_done = sem("oT_lo_done")
        y_mm = sem("y_mm")
        wo_split = sem("wo_split")
        x1_done = sem("x1_done")

        x_v = x.rearrange("b (t p) h -> b p t h", p=P)
        x1_v = d.x1.rearrange("(b t p) h -> b p t h", p=P, t=NT)
        block = ctx.enter_context(nc.Block())

        def groups(eng, G0, body):
            body(0, G0, 0, 0)
            body(1, G0 + 1, 1, 1)
            with eng.Fori(2, NG - 2, 2) as g:
                body(2, G0 + g, 0, g)
                body(3, G0 + (g + 1), 1, g + 1)
            body(NG - 2, G0 + (NG - 2), 0, NG - 2)
            body(NG - 1, G0 + (NG - 1), 1, NG - 1)

        def qkv_places(k):
            t = slice(512 * k, 512 * k + 512)
            return [(bank[k % 2][:], (kT_hi[:, t], kT_lo[:, t])),
                    (bank[2 + k % 2][:], (qT_hi[:, t], qT_lo[:, t])),
                    (bank[6 + k % 2][:].rearrange("p (t d) -> p t d", d=D),
                     (v_hi[:, 4 * k:4 * k + 4, :], v_lo[:, 4 * k:4 * k + 4, :]))]

        @block.sync
        def _(sp):
            sp.dma_start(cT[:], cT_in).then_inc(w_loaded, 16)
            sp.dma_start(wmod_sb, wmod.rearrange("(k p) n -> p k n", p=P)).then_inc(w_loaded, 16)
            sp.dma_start(w_raw, wqkv).then_inc(w_loaded, 16)
            sp.dma_start(wo_raw, wo).then_inc(w_loaded, 16)
            sp.dma_start(mask_i[:], mask).then_inc(w_loaded, 16)
            sp.dma_start(X[:, 0], x_v[0]).then_inc(x_loaded, 16)
            for b in range(NB):
                if b + 1 < NB:
                    if b >= 1:
                        sp.wait_ge(x1_stored, 16 * NG * b)
                        sp.wait_ge(d.stats1_done, NT * b)
                    sp.wait_ge(x_loaded, 16 * (b + 1))
                    sp.dma_start(X[:, (b + 1) % 2], x_v[b + 1]).then_inc(x_loaded, 16)
                else:
                    sp.sem_inc(x_loaded, 16)
                with sp.Fori(0, NG) as g:
                    sp.wait_ge(x1_done, 2 * (NG * b + g) + 2)
                    sp.dma_start(x1_v[b, :, ds(2 * g, 2), :],
                                 X[:, b % 2, ds(2 * g, 2), :]).then_inc(x1_stored, 16)
            sp.wait_ge(x1_stored, 16 * NG * NB)

        @block.gpsimd
        def _(pool):
            def deviations(n):
                hold(pool, d, mv_done, NT * n + NT)
                pool.tensor_scalar(veps[:], mv[:, :, 1], EPS, None, ALU.add).then_inc(veps_done, 1)
                pool.wait_ge(veps_done, n + 1)
                pool.tensor_tensor(rstd[:], veps[:], d.minus_half[:], ALU.pow).then_inc(rstd_done, 1)

            deviations(0)
            gate = rows[:, :, 0:H]
            sign = silu_rows[:, :, :, :].rearrange("p k b q -> p (k b q)").rearrange("p (b h) -> p b h", h=H)
            pool.wait_ge(mod_out, 2 * NB)
            pool.tensor_scalar(sign, gate, 0.0, 2.0, ALU.is_ge, ALU.mult).then_inc(ga_fix, 1)
            pool.wait_ge(ga_fix, 1)
            pool.tensor_scalar(sign, sign, 1.0, None, ALU.subtract).then_inc(ga_fix, 1)
            pool.wait_ge(ga_fix, 2)
            pool.tensor_tensor(gate, gate, sign, ALU.mult).then_inc(ga_fix, 1)
            pool.wait_ge(ga_fix, 3)
            pool.tensor_scalar(gate, gate, FLOOR, None, ALU.max).then_inc(ga_fix, 1)
            pool.wait_ge(ga_fix, 4)
            pool.tensor_tensor(gate, gate, sign, ALU.mult).then_inc(ga_fix, 1)
            with pool.Fori(0, NB) as b:
                def queries(k, G, par, g):
                    if k >= 2:
                        hold(pool, d, s_mm, 8 * G - 8)
                    pool.tensor_copy(q_hi[:, par, :], qT_hi[:, ds(GQ * g, GQ)]).then_inc(q_copied, 1)
                    pool.tensor_copy(q_lo[:, par, :], qT_lo[:, ds(GQ * g, GQ)]).then_inc(q_copied, 1)

                hold(pool, d, qkv_lo, 12 * b + 2)
                groups(pool, NG * b, queries)
                deviations(b + 1)

        @block.scalar
        def _(act):
            act.wait_ge(w_loaded, 80)
            act.activation(ce[:], cT[:], ACT.Exp, scale=-1.0).then_inc(exp_c, 1)
            for i in range(2 * NB):
                act.wait_ge(mod_mm, i + 2)
                o = 512 * (1 - i // NB)
                act.activation(rows[:, i % NB, o:o + 512], bank[i % 4][:], ACT.Copy).then_inc(mod_out, 1)
            act.wait_ge(mod_fix, MOD_FIXED)
            with act.Fori(0, NB) as b:
                def rows_T(f):
                    c = f % 2
                    hold(act, d, hT_mm, 8 * b + f + 1)
                    if f >= 2:
                        hold(act, d, hT_lo_done, 8 * b + f - 1)
                    act.activation(vt[:, f % 2, :], t_bank[f % 2][:], ACT.Identity,
                                   scale=mod_cols[:, 1, c, ds(b, 1)], bias=mod_cols[:, 0, c, ds(b, 1)]
                                   ).then_inc(vt_done, 1)
                    act.wait_ge(vt_done, 8 * b + f + 1)
                    act.activation(hT_hi[:, c, 512 * (f // 2):512 * (f // 2) + 512], vt[:, f % 2, :],
                                   ACT.Copy).then_inc(hT_hi_done, 1)

                def qkv_high(k):
                    for m, (src, dst) in enumerate(qkv_places(k)):
                        act.wait_ge(qkv_mm, 12 * b + 3 * k + m + 1)
                        act.activation(dst[0], src, ACT.Copy, scale=SCALE if m == 1 else 1.0
                                       ).then_inc(qkv_hi, 1)

                for k in range(NBLK):
                    rows_T(2 * k)
                    rows_T(2 * k + 1)
                    if k:
                        qkv_high(k - 1)
                qkv_high(NBLK - 1)

                def exps(G, par, c, j):
                    t = 2 * G + c
                    act.wait_ge(s_mm, 4 * t + j + 1)
                    if j == 0:
                        act.wait_ge(negmax_done, t + 1)
                    act.activation(prob[:, c, 512 * j:512 * j + 512], s_bank[j][:], ACT.Exp,
                                   bias=negmax[:, c:c + 1], accum_out=esum[:, par, c, j:j + 1]
                                   ).then_inc(exp_done, 1)

                def high(G, par, c, j):
                    act.wait_ge(pT_mm, 4 * (2 * G + c) + j + 1)
                    act.activation(pT_hi[:, par, 4 * j:4 * j + 4, P * c:P * c + P],
                                   t_bank[j % 2][:].rearrange("p (k q) -> p k q", q=P),
                                   ACT.Copy).then_inc(pT_hi_done, 1)

                def output_high(G, par):
                    act.wait_ge(o_mm, G + 1)
                    act.activation(oT_hi[:, par, :], o_bank[par][:, 0:GQ],
                                   ACT.Copy).then_inc(oT_hi_done, 1)

                def body(k, G, par, g):
                    if k >= 2:
                        output_high(G - 2, par)
                    for c in range(2):
                        exps(G, par, c, 0)
                        for j in range(1, 4):
                            exps(G, par, c, j)
                            high(G, par, c, j - 1)
                        high(G, par, c, 3)

                groups(act, NG * b, body)
                output_high(NG * b + (NG - 2), 0)
                output_high(NG * b + (NG - 1), 1)

        @block.tensor
        def _(pe):
            pe.wait_ge(d.s_const, d.n_const)
            pe.wait_ge(silu_c, 4)
            for w in range(2):
                for hc in range(HC):
                    for k in range(HC):
                        o = w * H + hc * P
                        mm = pe.matmul(bank[4][:, (w * HC + hc) * NB:(w * HC + hc + 1) * NB],
                                       wmod_sb[:, k, o:o + P], silu_rows[:, k, :, 0],
                                       start=(k == 0), stop=(k == HC - 1))
            mm.then_inc(mod_mm, 1)
            for i in range(2 * NB):
                if i >= 4:
                    pe.wait_ge(mod_out, i - 3)
                o = 2 * H + 512 * (1 - i // NB)
                for k in range(HC):
                    mm = pe.matmul(bank[i % 4][:], silu_rows[:, k, i % NB, :], wmod_sb[:, k, o:o + 512],
                                   start=(k == 0), stop=(k == HC - 1))
                mm.then_inc(mod_mm, 1)
            pe.wait_ge(w_split, 4)
            pe.wait_ge(mod_fix, MOD_FIXED)
            with pe.Fori(0, NB) as b:
                def rows_T(f):
                    pe.wait_ge(xhat_done, NT * b + 4 * (f // 2 + 1))
                    if f >= 2:
                        pe.wait_ge(vt_done, 8 * b + f - 1)
                    for i in range(4):
                        mm = pe.transpose(t_bank[f % 2][:, P * i:P * i + P],
                                          xhat[:, 4 * (f // 2) + i, P * (f % 2):P * (f % 2) + P], ident[:])
                    mm.then_inc(hT_mm, 1)

                def qkv(k):
                    pe.wait_ge(hT_lo_done, 8 * b + 2 * k + 2)
                    if k >= 2:
                        pe.wait_ge(qkv_lo, 12 * b + 3 * (k - 1))
                    t = slice(512 * k, 512 * k + 512)
                    for m, out in ((1, bank[k % 2]), (0, bank[2 + k % 2])):
                        for c in range(HC):
                            mm = product(pe, out[:], w_hi[:, c, m * D:m * D + D], w_lo[:, c, m * D:m * D + D],
                                         hT_hi[:, c, t], hT_lo[:, c, t], c == 0, c == HC - 1)
                        mm.then_inc(qkv_mm, 1)
                    for i in range(4):
                        ti = slice(512 * k + P * i, 512 * k + P * i + P)
                        for c in range(HC):
                            mm = product(pe, bank[6 + k % 2][:, P * i:P * i + P],
                                         hT_hi[:, c, ti], hT_lo[:, c, ti],
                                         w_hi[:, c, 2 * D:3 * D], w_lo[:, c, 2 * D:3 * D], c == 0, c == HC - 1)
                    mm.then_inc(qkv_mm, 1)

                for k in range(NBLK):
                    rows_T(2 * k)
                    rows_T(2 * k + 1)
                    if k:
                        qkv(k - 1)
                qkv(NBLK - 1)

                def scores(G, par, c, j):
                    if j == 0 and c == 0:
                        pe.wait_ge(q_copied, 2 * G + 2)
                    mm = product(pe, s_bank[j][:], q_hi[:, par, P * c:P * c + P], q_lo[:, par, P * c:P * c + P],
                                 kT_hi[:, 512 * j:512 * j + 512], kT_lo[:, 512 * j:512 * j + 512])
                    mm.then_inc(s_mm, 1)

                def turn(G, c, j, fresh):
                    t = 2 * G + c
                    if not fresh:
                        pe.wait_ge(pT_lo_done, 4 * t + j - 1)
                    for i in range(4):
                        k = 4 * j + i
                        mm = pe.transpose(t_bank[j % 2][:, P * i:P * i + P],
                                          prob[:, c, P * k:P * k + P], ident[:])
                    mm.then_inc(pT_mm, 1)

                def values(k_group, G, par, k0, n):
                    pe.wait_ge(pT_lo_done, 8 * G + 4 + (k0 + n + 3) // 4)
                    if k0 == 0 and k_group >= 2:
                        pe.wait_ge(x1_done, 2 * G - 2)
                    for k in range(k0, k0 + n):
                        mm = product(pe, o_bank[par][:, 0:GQ], v_hi[:, k, :], v_lo[:, k, :],
                                     pT_hi[:, par, k, :], pT_lo[:, par, k, :], k == 0, k == NT - 1)
                    if k0 + n == NT:
                        mm.then_inc(o_mm, 1)

                def project(G, par):
                    pe.wait_ge(oT_lo_done, G + 1)
                    pe.wait_ge(wo_split, 3 * b + 3)
                    for c in range(2):
                        mm = product(pe, o_bank[par][:, H * c:H * c + H], oT_hi[:, par, P * c:P * c + P],
                                     oT_lo[:, par, P * c:P * c + P], wo_hi[:], wo_lo[:])
                    mm.then_inc(y_mm, 1)

                def body(k, G, par, g):
                    done = 0
                    for c in range(2):
                        for j in range(4):
                            if k >= 1 and PV_STEPS[j]:
                                values(k - 1, G - 1, 1 - par, done, PV_STEPS[j])
                                done += PV_STEPS[j]
                            pe.wait_ge(exp_done, 4 * (2 * G + c) + j + 1)
                            turn(G, c, j, k == 0 and c == 0 and j < 2)
                            if c == 0:
                                scores(G, par, 1, j)
                            elif k < NG - 1:
                                scores(G + 1, 1 - par, 0, j)
                            if k >= 2 and c == 0 and j == 1:
                                project(G - 2, par)

                pe.wait_ge(qkv_lo, 12 * b + 12)
                for j in range(4):
                    scores(NG * b, 0, 0, j)
                groups(pe, NG * b, body)
                values(NG - 1, NG * b + (NG - 1), 1, 0, NT)
                project(NG * b + (NG - 2), 0)
                project(NG * b + (NG - 1), 1)
                pe.wait_ge(x1_done, 2 * NG * b + 2 * NG)

        @block.vector
        def _(dve):
            dve.wait_ge(w_loaded, 80)
            dve.tensor_copy(w_hi[:], w_raw).then_inc(w_split, 1)
            dve.tensor_copy(mask_f[:], mask_i[:]).then_inc(w_split, 1)
            dve.wait_ge(w_split, 2)
            dve.tensor_scalar(wo_masked[:], wo_raw, mask_f[:], None, ALU.mult).then_inc(w_split, 1)
            dve.wait_ge(exp_c, 1)
            dve.tensor_scalar(ce[:], ce[:], 1.0, None, ALU.add).then_inc(silu_c, 1)
            dve.wait_ge(silu_c, 1)
            dve.reciprocal(ce[:], ce[:]).then_inc(silu_c, 1)
            dve.wait_ge(silu_c, 2)
            dve.tensor_tensor(cT[:], cT[:], ce[:], ALU.mult).then_inc(silu_c, 1)
            dve.wait_ge(silu_c, 3)
            dve.tensor_copy(silu_rows[:], cT[:].unsqueeze(3).to_broadcast([P, HC, NB, P])).then_inc(silu_c, 1)
            dve.tensor_tensor(w_lo[:], w_raw, w_hi[:].bitcast(F32), ALU.subtract).then_inc(w_split, 1)
            dve.wait_ge(w_split, 4)
            dve.wait_ge(mod_mm, 1)
            cols = bank[4][:, 0:2 * HC * NB].rearrange("p (w c b) -> p w c b", w=2, c=HC)
            dve.tensor_copy(mod_cols[:, 0], cols[:, 0]).then_inc(mod_fix, 1)
            dve.tensor_scalar(mod_cols[:, 1], cols[:, 1], 1.0, None, ALU.add).then_inc(mod_fix, 1)

            def aggregate(n):
                hold(dve, d, stats_done, NT * n + NT)
                for t in range(NT):
                    dve.bn_aggr(mv[:, t, :], stats[:, t, :]).then_inc(mv_done, 1)

            def normalise(n, buffer):
                dve.wait_ge(rstd_done, n + 1)
                for t in range(NT):
                    dve.tensor_scalar(xhat[:, t, :], X[:, buffer, t, :], mv[:, t, 0:1], rstd[:, t:t + 1],
                                      ALU.subtract, ALU.mult).then_inc(xhat_done, 1)

            dve.wait_ge(x_loaded, 16)
            for t in range(NT):
                dve.bn_stats(stats[:, t, :], X[:, 0, t, :]).then_inc(stats_done, 1)
            aggregate(0)
            dve.wait_ge(mod_out, NB)
            dve.tensor_scalar(rows[:, :, 2 * H:3 * H], rows[:, :, 2 * H:3 * H], 1.0, None,
                              ALU.add).then_inc(mod_fix, 1)
            mag = vt[:, :, :].rearrange("p a (b h) -> p (a b) h", h=H)
            gate = rows[:, :, 3 * H:4 * H]
            dve.scalar_tensor_tensor(out=mag, in0=gate, scalar=-1.0, in1=gate, op0=ALU.mult,
                                     op1=ALU.max).then_inc(d.s_gate, 1)
            dve.wait_ge(d.s_gate, 1)
            dve.tensor_scalar(gate, gate, 0.0, 2.0, ALU.is_ge, ALU.mult).then_inc(d.s_gate, 1)
            dve.tensor_scalar(mag, mag, FLOOR, None, ALU.max).then_inc(d.s_gate, 1)
            dve.wait_ge(d.s_gate, 3)
            dve.scalar_tensor_tensor(out=gate, in0=gate, scalar=1.0, in1=mag, op0=ALU.subtract,
                                     op1=ALU.mult).then_inc(mod_fix, 1)
            dve.wait_ge(mod_mm, 2 * NB + 1)
            normalise(0, 0)
            with dve.Fori(0, NB) as b:
                xb = b & 1

                def rows_low(f):
                    dve.wait_ge(hT_hi_done, 8 * b + f + 1)
                    t = slice(512 * (f // 2), 512 * (f // 2) + 512)
                    dve.tensor_tensor(hT_lo[:, f % 2, t], vt[:, f % 2, :], hT_hi[:, f % 2, t].bitcast(F32),
                                      ALU.subtract).then_inc(hT_lo_done, 1)

                def qkv_low(k):
                    for m, (src, dst) in enumerate(qkv_places(k)):
                        dve.wait_ge(qkv_hi, 12 * b + 3 * k + m + 1)
                        if m == 1:
                            dve.scalar_tensor_tensor(out=dst[1], in0=src, scalar=SCALE, in1=dst[0].bitcast(F32),
                                                     op0=ALU.mult, op1=ALU.subtract).then_inc(qkv_lo, 1)
                        else:
                            dve.tensor_tensor(dst[1], src, dst[0].bitcast(F32), ALU.subtract).then_inc(qkv_lo, 1)

                for k in range(NBLK):
                    rows_low(2 * k)
                    rows_low(2 * k + 1)
                    if k:
                        qkv_low(k - 1)
                qkv_low(NBLK - 1)

                dve.wait_ge(ga_fix, 5)
                dve.tensor_tensor(wo_gated, wo_masked[:], rows[:, ds(b, 1), 0:H].rearrange("p o h -> p (o h)"),
                                  ALU.mult).then_inc(wo_split, 1)
                dve.wait_ge(wo_split, 3 * b + 1)
                dve.tensor_copy(wo_hi[:], wo_gated).then_inc(wo_split, 1)
                dve.wait_ge(wo_split, 3 * b + 2)
                dve.tensor_tensor(wo_lo[:], wo_gated, wo_hi[:].bitcast(F32), ALU.subtract).then_inc(wo_split, 1)

                def block_max(G, c, j):
                    t = 2 * G + c
                    dve.wait_ge(s_mm, 4 * t + j + 1)
                    dve.tensor_reduce(bmax[:, c, j:j + 1], s_bank[j][:], AX_X, ALU.max).then_inc(bmax_done, 1)
                    if j == 3:
                        dve.wait_ge(bmax_done, 4 * t + 4)
                        dve.tensor_reduce(negmax[:, c:c + 1], bmax[:, c, :], AX_X, ALU.max,
                                          negate=True).then_inc(negmax_done, 1)

                def low(G, par, c, j):
                    dve.wait_ge(pT_hi_done, 4 * (2 * G + c) + j + 1)
                    o = (slice(None), par, slice(4 * j, 4 * j + 4), slice(P * c, P * c + P))
                    dve.tensor_tensor(pT_lo[o], t_bank[j % 2][:].rearrange("p (k q) -> p k q", q=P),
                                      pT_hi[o].bitcast(F32), ALU.subtract).then_inc(pT_lo_done, 1)

                def denominators(G, par):
                    dve.wait_ge(exp_done, 8 * G + 8)
                    dve.tensor_reduce(den[:, par, :], esum[:, par, :, :], AX_X, ALU.add).then_inc(den_done, 1)
                    dve.wait_ge(den_done, G + 1)
                    dve.reciprocal(rden[:, par, :], den[:, par, :]).then_inc(rden_done, 1)

                def output_low(G, par):
                    dve.wait_ge(oT_hi_done, G + 1)
                    dve.tensor_tensor(oT_lo[:, par, :], o_bank[par][:, 0:GQ],
                                      oT_hi[:, par, :].bitcast(F32), ALU.subtract).then_inc(oT_lo_done, 1)

                def residual(G, par, g):
                    dve.wait_ge(y_mm, G + 1)
                    dve.wait_ge(rden_done, G + 1)
                    tile = lambda c: X[:, ds(xb, 1), ds(2 * g + c, 1), :].rearrange("p o t h -> p (o t h)")
                    for c in range(2):
                        dve.scalar_tensor_tensor(out=tile(c), in0=o_bank[par][:, H * c:H * c + H],
                                                 scalar=rden[:, par, c:c + 1], in1=tile(c),
                                                 op0=ALU.mult, op1=ALU.add).then_inc(x1_done, 1)
                    for c in range(2):
                        hold(dve, d, x1_done, 2 * G + c + 1)
                        dve.bn_stats(d.stats1[:, ds(2 * G + c, 1), :], tile(c)).then_inc(d.stats1_done, 1)

                def next_statistics(k, g):
                    if k == 0:
                        hold(dve, d, x_loaded, 16 * b + 32)
                    for i in range(2):
                        st = stats[:, ds(2 * g + i, 1), :]
                        dve.bn_stats(st, X[:, ds(1 - xb, 1), ds(2 * g + i, 1), :]).then_inc(stats_done, 1)

                def body(k, G, par, g):
                    next_statistics(k, g)
                    if k >= 1:
                        denominators(G - 1, 1 - par)
                    if k >= 2:
                        output_low(G - 2, par)
                    if k == NG - 1:
                        aggregate(b + 1)
                    for c in range(2):
                        if k >= 2 and c == 1:
                            residual(G - 2, par, g - 2)
                        for j in range(4):
                            if c == 0:
                                block_max(G, 1, j)
                            elif k < NG - 1:
                                block_max(G + 1, 0, j)
                            low(G, par, c, j)

                for j in range(4):
                    block_max(NG * b, 0, j)
                groups(dve, NG * b, body)
                normalise(b + 1, ds(1 - xb, 1))
                denominators(NG * b + (NG - 1), 1)
                output_low(NG * b + (NG - 2), 0)
                output_low(NG * b + (NG - 1), 1)
                residual(NG * b + (NG - 2), 0, NG - 2)
                residual(NG * b + (NG - 1), 1, NG - 1)


class Namespace:
    pass


def inside(n, count):
    return not isinstance(n, int) or 0 <= n < count


def split_weights(eng, raw, hi, lo, done, n):
    eng.tensor_copy(hi, raw).then_inc(done, 1)
    eng.wait_ge(done, n + 1)
    eng.tensor_tensor(lo, raw, hi.bitcast(F32), ALU.subtract).then_inc(done, 1)


def gated_blocks(ctx, nc, d, tag, count, H, I, streams=1):
    HC, IC = H // P, I // P
    f = Namespace()
    sb = lambda n, s, t: ctx.enter_context(nc.sbuf_tensor(f"{tag}_{n}", s, t))
    sem = lambda n: ctx.enter_context(nc.semaphore(f"{tag}_{n}"))
    f.bank = [ctx.enter_context(nc.psum_tensor(f"{tag}_bank{i}", [P, 512], F32)) for i in range(8)]
    g_bank, u_bank, a_bank, x_bank = f.bank[0:4]
    f.y_bank = f.bank[4:6]
    xT_hi, xT_lo = sb("xT_hi", [P, 2, streams * HC, P], F32R), sb("xT_lo", [P, 2, streams * HC, P], F32R)
    f.xT_hi, f.xT_lo = xT_hi, xT_lo
    silu_g, prod = sb("silu_g", [P, 2, I], F32), sb("prod", [P, 2, I], F32)
    aT_hi, aT_lo = sb("aT_hi", [P, 2, IC, P], F32R), sb("aT_lo", [P, 2, IC, P], F32R)
    f.xT_mm, f.xT_hi_done, f.xT_lo_done = sem("xT_mm"), sem("xT_hi_done"), sem("xT_lo_done")
    f.gate_mm, f.up_mm, f.silu_done, f.prod_done = sem("gate_mm"), sem("up_mm"), sem("silu_done"), sem("prod_done")
    f.aT_mm, f.aT_hi_done, f.aT_lo_done = sem("aT_mm"), sem("aT_hi_done"), sem("aT_lo_done")
    f.y_mm, f.y_out, f.rows_ready = sem("y_mm"), sem("y_out"), sem("rows_ready")
    flat = lambda t, par: t[:, par, :, :].rearrange("p c t -> p (c t)")

    def pe_turn_rows(pe, m, par, rows):
        pe.wait_ge(f.rows_ready, f.ready_at(m))
        if inside(m - 1, count):
            pe.wait_ge(f.xT_lo_done, m)
        for c in range(streams * HC):
            mm = pe.transpose(x_bank[:, P * c:P * c + P], rows[:, P * c:P * c + P], d.ident[:])
        mm.then_inc(f.xT_mm, 1)

    def pe_turn_products(pe, m, par):
        pe.wait_ge(f.prod_done, m + 1)
        if inside(m - 1, count):
            pe.wait_ge(f.aT_lo_done, m)
        for c in range(IC):
            mm = pe.transpose(a_bank[:, P * c:P * c + P], prod[:, par, P * c:P * c + P], d.ident[:])
        mm.then_inc(f.aT_mm, 1)

    def pe_gate_up(pe, m, par, weights, beside=iter(())):
        pe.wait_ge(f.xT_lo_done, m + 1)
        for out, hi, lo, done in ((g_bank, *weights[0], f.gate_mm), (u_bank, *weights[1], f.up_mm)):
            for c in range(HC):
                x_hi, x_lo = xT_hi[:, par, c, :], xT_lo[:, par, c, :]
                for k, (l, w) in enumerate(((x_hi, hi(c)), (x_hi, lo(c)), (x_lo, hi(c)))):
                    mm = pe.matmul(out[:, 0:I], l, w, start=(c == 0 and k == 0), stop=(c == HC - 1 and k == 2))
                    if c == HC - 1 and k == 2:
                        mm.then_inc(done, 1)
                    small = next(beside, None)
                    if small:
                        small()

    def pe_down(pe, m, par, weights):
        pe.wait_ge(f.aT_lo_done, m + 1)
        if inside(m - 2, count):
            pe.wait_ge(f.y_out, m - 1)
        hi, lo = weights[2]
        for c in range(IC):
            mm = product(pe, f.y_bank[par][:, 0:H], aT_hi[:, par, c, :], aT_lo[:, par, c, :], hi(c), lo(c),
                         c == 0, c == IC - 1)
        mm.then_inc(f.y_mm, 1)

    def act_rows_high(act, m, par):
        act.wait_ge(f.xT_mm, m + 1)
        act.activation(flat(xT_hi, par), x_bank[:, 0:streams * H], ACT.Copy).then_inc(f.xT_hi_done, 1)

    def act_products_high(act, m, par):
        act.wait_ge(f.aT_mm, m + 1)
        act.activation(flat(aT_hi, par), a_bank[:, 0:I], ACT.Copy).then_inc(f.aT_hi_done, 1)

    def act_silu(act, m, par):
        act.wait_ge(f.gate_mm, m + 1)
        act.activation(silu_g[:, par, :], g_bank[:, 0:I], ACT.Silu).then_inc(f.silu_done, 1)

    def dve_rows_low(dve, m, par):
        dve.wait_ge(f.xT_hi_done, m + 1)
        dve.tensor_tensor(flat(xT_lo, par), x_bank[:, 0:streams * H], flat(xT_hi, par).bitcast(F32),
                          ALU.subtract).then_inc(f.xT_lo_done, 1)

    def dve_products_low(dve, m, par):
        dve.wait_ge(f.aT_hi_done, m + 1)
        dve.tensor_tensor(flat(aT_lo, par), a_bank[:, 0:I], flat(aT_hi, par).bitcast(F32),
                          ALU.subtract).then_inc(f.aT_lo_done, 1)

    def dve_products(dve, m, par):
        dve.wait_ge(f.silu_done, m + 1)
        dve.wait_ge(f.up_mm, m + 1)
        dve.tensor_tensor(prod[:, par, :], silu_g[:, par, :], u_bank[:, 0:I], ALU.mult).then_inc(f.prod_done, 1)

    f.pe_turn_rows, f.pe_turn_products, f.pe_gate_up, f.pe_down = pe_turn_rows, pe_turn_products, pe_gate_up, pe_down
    f.act_rows_high, f.act_products_high, f.act_silu = act_rows_high, act_products_high, act_silu
    f.dve_rows_low, f.dve_products_low, f.dve_products = dve_rows_low, dve_products_low, dve_products
    return f


def dispatch(pool, d, h_rows, g, sent):
    first, size = d.groups[g]
    CHUNK = h_rows.shape[2]
    for i in range(first, first + size):
        for half in range(2):
            n = d.steps * half + i
            for k in range(2):
                pool.indirect_dma_start(
                    d.x_rows, bass.IndirectOffsetOnAxis(ap=d.place_i[:, k, n:n + 1], axis=0),
                    h_rows[:, half, i % CHUNK, :], None).then_inc(sent, 16)


def shared_phase(nc, d, x1, shared_gate, shared_up, shared_down, router_w, router_bias):
    N, H = x1.shape
    I = shared_gate.shape[2]
    HC, IC = H // P, I // P
    E = d.E
    NB = d.NB
    NT = N // P
    TB = NT // NB
    STEPS = d.steps
    CHUNK = TB // 2
    Z, rows = d.Z, d.mod_rows

    with ExitStack() as ctx:
        sb = lambda n, s, t: ctx.enter_context(nc.sbuf_tensor(n, s, t))
        sem = lambda n: ctx.enter_context(nc.semaphore(n))
        f = gated_blocks(ctx, nc, d, "s", STEPS, H, I, streams=2)
        f.ready_at = lambda m: m + 1
        l_bank, r_bank = f.bank[6], f.bank[7]

        sg_hi, sg_lo = sb("sg_hi", [P, HC, I], F32R), sb("sg_lo", [P, HC, I], F32R)
        su_hi, su_lo = sb("su_hi", [P, HC, I], F32R), sb("su_lo", [P, HC, I], F32R)
        sd_hi, sd_lo = sb("sd_hi", [P, IC, H], F32R), sb("sd_lo", [P, IC, H], F32R)
        rw_raw = sb("rw_raw", [P, HC, E], F32)
        rw_hi, rw_lo = sb("rw_hi", [P, HC, E], F32R), sb("rw_lo", [P, HC, E], F32R)
        bias = sb("bias", [P, E], F32)
        h_rows = [sb("h_rows", [P, 2, CHUNK, H], F32), d.last_rows]
        w_raw = d.last_rows[:, :, :, :].rearrange("p s t h -> p (s t h)")
        raw = lambda o, a, b: w_raw[:, o:o + a * b].rearrange("p (a b) -> p a b", a=a)
        sg_raw, su_raw, sd_raw = raw(0, HC, I), raw(HC * I, HC, I), raw(2 * HC * I, IC, H)
        h = sb("h", [P, 2, 2, H], F32)
        norm = sb("norm", [P, 2, 2, H], F32)
        scaled = sb("scaled", [P, 2, 2, H], F32)
        gy = sb("gy", [P, 2, H], F32)
        mv, rstd, offset = d.mv, d.rstd, d.offset
        veps = sb("s_veps", [P, NT], F32)
        three = lambda n, t=F32: sb(n, [P, CHUNK, 2, E], t)
        logits, probs = three("logits"), three("probs")
        same, coded, pick1, rest, pick2, chosen = (three(n) for n in ("same", "coded", "pick1", "rest", "pick2", "chosen"))
        chosen_bf = three("chosen_bf", BF16)
        slot = three("slot")
        best1, code1, best2, code2 = (sb(n, [P, CHUNK, 2], F32) for n in ("best1", "code1", "best2", "code2"))
        total = sb("total", [P, CHUNK, 2], F32)
        base = d.base

        w_loaded = [sem(f"s_w_loaded{i}") for i in range(5)]
        x_loaded = [sem(f"s_x_loaded{b}") for b in range(NB)]
        x_first = sem("s_x_first")
        w_high, w_split = sem("s_w_high"), sem("s_w_split")
        weights = ((rw_raw[:], rw_hi, rw_lo), (sg_raw, sg_hi, sg_lo), (su_raw, su_hi, su_lo), (sd_raw, sd_hi, sd_lo))
        WEIGHT_DMA = (0, 2, 3, 4)
        mv_done, veps_done, rstd_done = sem("s_mv_done"), sem("s_veps_done"), sem("s_rstd_done")
        offset_done = sem("s_offset_done")
        norm_done, scaled_done, copied = sem("norm_done"), sem("scaled_done"), sem("copied")
        gy_done = sem("gy_done")
        logit_mm, logit_done, prob_done = sem("logit_mm"), sem("logit_done"), sem("prob_done")
        route, rank_mm, placed = sem("route"), sem("rank_mm"), sem("placed")
        sent = [sem(f"sent{g}") for g in range(len(d.groups) - 1)]

        z_v = x1.rearrange("(b t p) h -> b p t h", p=P, t=TB)
        block = ctx.enter_context(nc.Block())
        CHOSEN = 13
        SCORED = CHOSEN + 4
        ROUTE = SCORED + 6
        FEW = 4
        ORDER = [b + NB // 2 * half for b in range(NB // 2) for half in range(2)]

        def pairs(eng, g, step, behind_first=None):
            first, size = d.groups[g]
            b = first // TB
            peeled = 4 if g == 0 else 2
            for n in range(first, first + peeled):
                step(n, n % 2, b)
                if n == first and g and behind_first:
                    behind_first(g - 1)
            if size > peeled + 2:
                with eng.Fori(peeled // 2, size // 2 - 1) as i:
                    step(2 * i + first, 0, b)
                    step(2 * i + (first + 1), 1, b)
            step(first + size - 2, 0, b)
            step(first + size - 1, 1, b)

        def tile(n):
            return n if isinstance(n, int) else ds(n, 1)

        def span(n):
            return slice(n, n + 1) if isinstance(n, int) else ds(n, 1)

        def batch(n, b):
            return n // TB if isinstance(n, int) else b

        def both_halves(b, o):
            return rows[:, b:b + NB // 2 + 1:NB // 2, o:o + H]

        @block.sync
        def _(sp):
            for half in range(2):
                b = NB // 2 * half
                sp.dma_start(Z[:, TB * b:TB * b + FEW, :], z_v[b, :, 0:FEW, :]).then_inc(x_first, 16)
            for n, (dst, src) in enumerate(((rw_raw[:], router_w), (bias[:], router_bias.to_broadcast([P, E])),
                                            (sg_raw, shared_gate), (su_raw, shared_up), (sd_raw, shared_down))):
                sp.dma_start(dst, src).then_inc(w_loaded[n], 16)
            for b in ORDER:
                o = FEW if b % (NB // 2) == 0 else 0
                sp.dma_start(Z[:, TB * b + o:TB * b + TB, :], z_v[b, :, o:TB, :]).then_inc(x_loaded[b], 16)
            for b in ORDER:
                sp.wait_ge(x_loaded[b], 16)

        @block.gpsimd
        def _(pool):
            for n, b in enumerate(ORDER):
                tb = slice(TB * b, TB * b + TB)
                pool.wait_ge(mv_done, TB * (n + 1))
                pool.tensor_scalar(veps[:, tb], mv[:, tb, 1], EPS, None, ALU.add).then_inc(veps_done, 1)
                pool.wait_ge(veps_done, n + 1)
                pool.tensor_tensor(rstd[:, tb], veps[:, tb], d.minus_half[:], ALU.pow).then_inc(rstd_done, 1)
            for g, (first, size) in enumerate(d.groups[:-1]):
                pool.wait_ge(placed, 2 * g + 2)
                pool.wait_ge(copied, first + size)
                dispatch(pool, d, h_rows[first // CHUNK % 2], g, sent[g])
            for g, (first, size) in enumerate(d.groups[:-1]):
                pool.wait_ge(sent[g], 64 * size)

        @block.scalar
        def _(act):
            def normalise(m, par, b):
                if isinstance(m, int) and m == 0:
                    act.wait_ge(x_first, 32)
                if isinstance(m, int) and m == FEW:
                    for k in (b, b + NB // 2):
                        act.wait_ge(x_loaded[k], 16)
                if isinstance(m, int) and m % TB == 0:
                    act.wait_ge(offset_done, 2 * b + 2)
                    if m:
                        for k in (b, b + NB // 2):
                            act.wait_ge(x_loaded[k], 16)
                for half in range(2):
                    n = m + STEPS * half
                    if inside(m - 2, STEPS) and not half:
                        act.wait_ge(scaled_done, m - 1)
                    if isinstance(m, int):
                        src, scale, shift = Z[:, n, :], rstd[:, n:n + 1], offset[:, n:n + 1]
                    else:
                        src, scale, shift = Z[:, ds(n, 1), :], rstd[:, ds(n, 1)], offset[:, ds(n, 1)]
                    act.activation(norm[:, par, half, :], src, ACT.Identity, scale=scale, bias=shift
                                   ).then_inc(norm_done, 1)

            def copy_rows(m, par, b):
                act.wait_ge(f.rows_ready, m + 1)
                if isinstance(m, int):
                    chunk, place = m // CHUNK, m % CHUNK
                    if m == CHUNK:
                        act.wait_ge(w_split, 4)
                    if place == 0 and chunk >= 2:
                        for g, (first, size) in enumerate(d.groups):
                            if first // CHUNK == chunk - 2:
                                act.wait_ge(sent[g], 64 * size)
                else:
                    chunk = now[0]
                    place = m - CHUNK * chunk
                act.activation(h_rows[chunk % 2][:, :, tile(place), :], h[:, par, :, :], ACT.Copy).then_inc(copied, 1)

            def step(n, par, b):
                if inside(n + 2, STEPS):
                    normalise(n + 2, par, batch(n + 2, b))
                if inside(n - 1, STEPS):
                    f.act_products_high(act, n - 1, 1 - par)
                if inside(n + 1, STEPS):
                    f.act_rows_high(act, n + 1, 1 - par)
                f.act_silu(act, n, par)
                if inside(n + 2, STEPS):
                    copy_rows(n + 2, par, batch(n + 2, b))

            now = [0]
            normalise(0, 0, 0)
            for n, (raw_w, hi, lo) in enumerate(weights):
                act.wait_ge(w_loaded[WEIGHT_DMA[n]], 16)
                act.activation(hi[:], raw_w, ACT.Copy).then_inc(w_high, 1)
            normalise(1, 1, 0)
            copy_rows(0, 0, 0)
            f.act_rows_high(act, 0, 0)
            copy_rows(1, 1, 0)
            for g, (first, size) in enumerate(d.groups):
                now[0] = first // CHUNK
                pairs(act, g, step)
                act.wait_ge(logit_done, first + size)
                own = slice(first % CHUNK, first % CHUNK + size)
                act.activation(probs[:, own], logits[:, own], ACT.Sigmoid).then_inc(prob_done, 1)
            f.act_products_high(act, STEPS - 1, 1)

        @block.tensor
        def _(pe):
            columns = [(lambda c: sg_hi[:, c, :], lambda c: sg_lo[:, c, :]),
                       (lambda c: su_hi[:, c, :], lambda c: su_lo[:, c, :]),
                       (lambda c: sd_hi[:, c, :], lambda c: sd_lo[:, c, :])]

            def router(n, par):
                def small(half, c, k):
                    x = (f.xT_lo if k == 2 else f.xT_hi)[:, par, HC * half + c, :]
                    w = (rw_lo if k == 1 else rw_hi)[:, c, :]
                    mm = pe.matmul(l_bank[:, E * half:E * half + E], x, w, start=(c == 0 and k == 0),
                                   stop=(c == HC - 1 and k == 2))
                    if half == 1 and c == HC - 1 and k == 2:
                        mm.then_inc(logit_mm, 1)

                return iter([lambda half=half, c=c, k=k: small(half, c, k)
                             for half in range(2) for c in range(HC) for k in range(3)])

            def step(n, par, b):
                if inside(n - 2, STEPS):
                    f.pe_down(pe, n - 2, par, columns)
                if inside(n - 1, STEPS):
                    f.pe_turn_products(pe, n - 1, 1 - par)
                if inside(n + 1, STEPS):
                    f.pe_turn_rows(pe, n + 1, 1 - par, flat(h, 1 - par))
                if inside(n - 1, STEPS):
                    pe.wait_ge(logit_done, n)
                f.pe_gate_up(pe, n, par, columns, router(n, par))

            flat = lambda t, par: t[:, par, :, :].rearrange("p s h -> p (s h)")

            def ranks(g):
                first, size = d.groups[g]
                pe.wait_ge(route, ROUTE * g + CHOSEN)
                picks = chosen_bf[:, first % CHUNK:first % CHUNK + size].rearrange("p t s e -> p (t s e)")
                W = 2 * size * E
                pe.matmul(r_bank[:, 0:W], d.before[:], picks, start=True, stop=False)
                for s in range(1, 2 * size):
                    pe.matmul(r_bank[:, E * s:W], d.ones[:], picks[:, 0:W - E * s], start=False,
                              stop=s == 2 * size - 1)
                for t in range(2 * size):
                    mm = pe.matmul(r_bank[:, W:W + E], d.ones[:], picks[:, E * t:E * t + E],
                                   start=(t == 0), stop=(t == 2 * size - 1))
                mm.then_inc(rank_mm, 1)

            f.pe_turn_rows(pe, 0, 0, flat(h, 0))
            pe.wait_ge(w_split, 4)
            for g in range(len(d.groups)):
                pairs(pe, g, step, ranks)
            ranks(len(d.groups) - 1)
            f.pe_down(pe, STEPS - 2, 0, columns)
            f.pe_turn_products(pe, STEPS - 1, 1)
            f.pe_down(pe, STEPS - 1, 1, columns)

        @block.vector
        def _(dve):
            def scale(m, par, b):
                dve.wait_ge(norm_done, 2 * m + 2)
                dve.tensor_tensor(scaled[:, par, :, :], norm[:, par, :, :], both_halves(b, 2 * H),
                                  ALU.mult).then_inc(scaled_done, 1)

            def shift(m, par, b):
                dve.wait_ge(scaled_done, m + 1)
                if inside(m - 2, STEPS):
                    dve.wait_ge(f.xT_mm, m - 1)
                    dve.wait_ge(copied, m - 1)
                dve.tensor_tensor(h[:, par, :, :], scaled[:, par, :, :], both_halves(b, H),
                                  ALU.add).then_inc(f.rows_ready, 1)

            def add_logits(n):
                if isinstance(n, int) and n == 0:
                    dve.wait_ge(w_loaded[1], 16)
                dve.wait_ge(logit_mm, n + 1)
                place = n % CHUNK if isinstance(n, int) else ds(n - CHUNK * now[0], 1)
                out = logits[:, place].rearrange("p s e -> p (s e)") if isinstance(n, int) else \
                    logits[:, place].rearrange("p o s e -> p (o s e)")
                dve.tensor_tensor(out.rearrange("p (s e) -> p s e", s=2),
                                  l_bank[:, 0:2 * E].rearrange("p (s e) -> p s e", s=2),
                                  bias[:].unsqueeze(1).to_broadcast([P, 2, E]), ALU.add).then_inc(logit_done, 1)

            def gated(m, par, b):
                dve.wait_ge(f.y_mm, m + 1)
                dve.tensor_tensor(gy[:, par, :], f.y_bank[par][:, 0:H], rows[:, b, 3 * H:4 * H],
                                  ALU.mult).then_inc(f.y_out, 1)

            def shared_out(m, par):
                dve.wait_ge(f.y_out, m + 1)
                dve.tensor_tensor(Z[:, tile(m), :], gy[:, par, :], Z[:, tile(m), :], ALU.add).then_inc(gy_done, 1)

            def step(n, par, b):
                if inside(n + 2, STEPS):
                    scale(n + 2, par, batch(n + 2, b))
                if inside(n - 2, STEPS):
                    gated(n - 2, par, batch(n - 2, b))
                if inside(n + 2, STEPS):
                    shift(n + 2, par, batch(n + 2, b))
                if inside(n - 2, STEPS):
                    shared_out(n - 2, par)
                if inside(n - 1, STEPS):
                    f.dve_products_low(dve, n - 1, 1 - par)
                if inside(n + 1, STEPS):
                    f.dve_rows_low(dve, n + 1, 1 - par)
                f.dve_products(dve, n, par)
                add_logits(n)

            def halves(t, first, size):
                return t.rearrange("p (s t) -> p t s", s=2)[:, first:first + size]

            def choose(g):
                first, size = d.groups[g]
                own = slice(first % CHUNK, first % CHUNK + size)
                r = [ROUTE * g]

                def op(ins):
                    ins.then_inc(route, 1)
                    r[0] += 1
                    dve.wait_ge(route, r[0])

                three_d = lambda v: v[:, own].rearrange("p t s e -> p (t s) e")
                two_d = lambda v: v[:, own].rearrange("p t s -> p (t s)")
                wide = lambda v: two_d(v).unsqueeze(2).to_broadcast([P, 2 * size, E])
                codes = d.codes[:].unsqueeze(1).to_broadcast([P, 2 * size, E])
                dve.wait_ge(prob_done, g + 1)
                op(dve.tensor_reduce(two_d(best1), three_d(probs), AX_X, ALU.max))
                op(dve.tensor_tensor(three_d(same), three_d(probs), wide(best1), ALU.is_equal))
                op(dve.tensor_tensor(three_d(coded), three_d(same), codes, ALU.mult))
                op(dve.tensor_reduce(two_d(code1), three_d(coded), AX_X, ALU.max))
                op(dve.tensor_tensor(three_d(pick1), three_d(coded), wide(code1), ALU.is_equal))
                op(dve.scalar_tensor_tensor(out=three_d(rest), in0=three_d(pick1), scalar=-4.0, in1=three_d(probs),
                                            op0=ALU.mult, op1=ALU.add))
                op(dve.tensor_reduce(two_d(best2), three_d(rest), AX_X, ALU.max))
                op(dve.tensor_tensor(three_d(same), three_d(rest), wide(best2), ALU.is_equal))
                op(dve.tensor_tensor(three_d(coded), three_d(same), codes, ALU.mult))
                op(dve.tensor_reduce(two_d(code2), three_d(coded), AX_X, ALU.max))
                op(dve.tensor_tensor(three_d(pick2), three_d(coded), wide(code2), ALU.is_equal))
                op(dve.tensor_tensor(three_d(chosen), three_d(pick1), three_d(pick2), ALU.add))
                op(dve.tensor_copy(three_d(chosen_bf), three_d(chosen)))
                assert r[0] == ROUTE * g + CHOSEN
                op(dve.tensor_tensor(two_d(total), two_d(best1), two_d(best2), ALU.add))
                op(dve.reciprocal(two_d(total), two_d(total)))
                for k, best in enumerate((best1, best2)):
                    op(dve.tensor_tensor(halves(d.score[:, k, :], first, size), best[:, own], total[:, own], ALU.mult))
                assert r[0] == ROUTE * g + SCORED

            def place(g):
                first, size = d.groups[g]
                own = slice(first % CHUNK, first % CHUNK + size)
                r = [ROUTE * g + SCORED]

                def op(ins):
                    ins.then_inc(route, 1)
                    r[0] += 1
                    dve.wait_ge(route, r[0])

                three_d = lambda v: v[:, own].rearrange("p t s e -> p (t s) e")
                dve.wait_ge(rank_mm, g + 1)
                W = 2 * size * E
                op(dve.tensor_tensor(three_d(slot), r_bank[:, 0:W].rearrange("p (t e) -> p t e", e=E),
                                     base[:, g, :].unsqueeze(1).to_broadcast([P, 2 * size, E]), ALU.add))
                op(dve.tensor_tensor(base[:, g + 1, :], r_bank[:, W:W + E], base[:, g, :], ALU.add))
                for k, pick in enumerate((pick1, pick2)):
                    op(dve.tensor_tensor(three_d(coded), three_d(slot), three_d(pick), ALU.mult))
                    op(dve.tensor_reduce(halves(d.place[:, k, :], first, size), coded[:, own], AX_X, ALU.add))
                    dve.tensor_copy(halves(d.place_i[:, k, :], first, size),
                                    halves(d.place[:, k, :], first, size)).then_inc(placed, 1)
                assert r[0] == ROUTE * (g + 1)

            def aggregate(b):
                for t in range(TB * b, TB * b + TB):
                    dve.bn_aggr(mv[:, t, :], d.stats1[:, t, :]).then_inc(mv_done, 1)

            def offsets(n, b):
                tb = slice(TB * b, TB * b + TB)
                dve.wait_ge(rstd_done, n + 1)
                dve.scalar_tensor_tensor(out=offset[:, tb], in0=mv[:, tb, 0], scalar=-1.0, in1=rstd[:, tb],
                                         op0=ALU.mult, op1=ALU.mult).then_inc(offset_done, 1)

            now = [0]
            for b in ORDER:
                aggregate(b)
            dve.tensor_copy(base[:, 0, :], d.first_row[:, 0:E]).then_inc(d.base_set, 1)
            offsets(0, ORDER[0])
            offsets(1, ORDER[1])
            scale(0, 0, 0)
            shift(0, 0, 0)
            for n, (raw_w, hi, lo) in enumerate(weights):
                dve.wait_ge(w_high, n + 1)
                dve.tensor_tensor(lo[:], raw_w, hi[:].bitcast(F32), ALU.subtract).then_inc(w_split, 1)
            scale(1, 1, 0)
            shift(1, 1, 0)
            f.dve_rows_low(dve, 0, 0)
            for n in range(2, NB):
                offsets(n, ORDER[n])
            for g, (first, size) in enumerate(d.groups):
                now[0] = first // CHUNK
                pairs(dve, g, step, place)
                choose(g)
            place(len(d.groups) - 1)
            f.dve_products_low(dve, STEPS - 1, 1)
            for n in (STEPS - 2, STEPS - 1):
                gated(n, n % 2, n // TB)
                shared_out(n, n % 2)


def experts_phase(nc, d, gate_w, up_w, down_w):
    E, _, HC, I = gate_w.shape
    H = HC * P
    IC = I // P
    NBLK = d.blocks
    W = HC * I

    with ExitStack() as ctx:
        sb = lambda n, s, t: ctx.enter_context(nc.sbuf_tensor(n, s, t))
        sem = lambda n: ctx.enter_context(nc.semaphore(n))
        f = gated_blocks(ctx, nc, d, "e", NBLK, H, I)
        w_raw = sb("e_w_raw", [P, 3 * W], F32)
        w_hi = sb("e_w_hi", [P, 2, 3 * W], F32R)
        w_lo = sb("e_w_lo", [P, 2, 3 * W], F32R)
        h = sb("e_h", [P, 2, H], F32)
        y = sb("e_y", [P, 2, H], F32)
        zeros = sb("zeros", [P, H], F32)
        count = sb("count", [P, E], F32)
        over = sb("over", [P, E, d.most], F32)
        nblocks = sb("nblocks", [P, E], F32)
        ends = sb("ends", [P, E], F32)
        rows_of = sb("rows_of", [P, d.place.shape[1] * d.place.shape[2]], F32)
        moved = sb("moved", [P, d.place.shape[1] * d.place.shape[2]], F32)
        starts = sb("starts", [P, E + 1], F32)
        shift = sb("shift", [P, E + 1], F32)
        jump = sb("jump", [P, E], F32)
        behind = sb("behind", [1, NBLK, E], F32)
        jumped = sb("jumped", [1, NBLK, E], F32)
        moved_by = sb("moved_by", [1, NBLK], F32)
        expert_of = sb("expert_of", [1, NBLK + 2], F32)
        packed = sb("packed", [1, 3, NBLK // 2], F32)
        row0 = sb("row0", [1, NBLK], F32)
        table = sb("table", [1, 2, NBLK], I32)
        free_i = sb("free_i", [1, E], I32)
        ends_i = sb("ends_i", [1, E], I32)

        w_loaded, w_split = sem("e_w_loaded"), sem("e_w_split")
        zeroed, padded, moving = sem("zeroed"), sem("padded"), sem("moving")
        plan, last_sent = sem("plan"), sem("last_sent")
        first_loaded, free_known = sem("first_loaded"), sem("free_known")
        h_in = [sem("h_in0"), sem("h_in1")]
        y_stored = [sem("y_stored0"), sem("y_stored1")]
        PLAN = 19 + E
        LOG_E = E.bit_length() - 1

        block = ctx.enter_context(nc.Block())
        half = lambda m, par: m // 2 if isinstance(m, int) else (m - par) // 2

        def steps(eng, step):
            for n in range(4):
                step(n, n % 2)
            with eng.Fori(2, NBLK // 2 - 1) as i:
                step(2 * i, 0)
                step(2 * i + 1, 1)
            step(NBLK - 2, 0)
            step(NBLK - 1, 1)

        def at(m):
            return slice(m, m + 1) if isinstance(m, int) else ds(m, 1)

        def first_row(eng, m):
            return eng.value_load(table[0:1, 0, at(m)], min_val=0, max_val=d.all_rows - P)

        @block.sync
        def _(sp):
            for m, src in enumerate((gate_w, up_w, down_w)):
                sp.dma_start(w_raw[:, W * m:W * m + W], src[0].rearrange("p a b -> p (a b)")).then_inc(first_loaded, 16)
            sp.wait_ge(zeroed, 2)
            sp.dma_start(d.x_rows[d.spare_row:d.spare_row + P * E, :].rearrange("(e p) h -> p e h", p=P),
                         zeros[:].unsqueeze(1).to_broadcast([P, E, H])).then_inc(padded, 16)
            sp.wait_ge(free_known, 1)
            for e in range(E):
                row = sp.value_load(free_i[0:1, e:e + 1], min_val=0, max_val=d.all_rows - P)
                sp.dma_start(d.x_rows[ds(row, P), :], zeros[:]).then_inc(padded, 16)
            sp.wait_ge(padded, 16 * (E + 1))
            sp.wait_ge(plan, PLAN)
            sp.wait_ge(last_sent, 64 * d.groups[-1][1])

            def load(m, par):
                row = first_row(sp, m)
                sp.dma_start(h[:, par, :], d.x_rows[ds(row, P), :]).then_inc(h_in[par], 16)

            def store(m, par):
                sp.wait_ge(f.y_out, m + 1)
                rows = slice(P * m, P * m + P) if isinstance(m, int) else ds(P * m, P)
                sp.dma_start(d.y_rows[rows, :], y[:, par, :]).then_inc(y_stored[par], 16)

            def step(n, par):
                if inside(n + 2, NBLK):
                    hold(sp, d, f.xT_mm, n + 1)
                    load(n + 2, par)
                if inside(n - 2, NBLK):
                    store(n - 2, par)

            load(0, 0)
            load(1, 1)
            steps(sp, step)
            store(NBLK - 2, 0)
            store(NBLK - 1, 1)
            for s in y_stored:
                sp.wait_ge(s, 16 * (NBLK // 2))

        @block.gpsimd
        def _(pool):
            pool.memset(zeros[:], 0.0).then_inc(zeroed, 1)
            pool.tensor_copy(rows_of[:], d.place[:, :, :].rearrange("p k t -> p (k t)")).then_inc(zeroed, 1)
            dispatch(pool, d, d.last_rows, len(d.groups) - 1, last_sent)
            for e in range(1, E):
                if e == 1:
                    pool.wait_ge(w_split, 2)
                for m, src in enumerate((gate_w, up_w, down_w)):
                    pool.dma_start(w_raw[:, W * m:W * m + W], src[e].rearrange("p a b -> p (a b)")).then_inc(w_loaded, 16)
                pool.wait_ge(w_loaded, 48 * e)
                if e >= 2:
                    pool.wait_ge(plan, PLAN)
                    end = pool.value_load(ends_i[0:1, e - 2:e - 1], min_val=1, max_val=NBLK)
                    hold(pool, d, f.y_mm, end)
                split_weights(pool, w_raw[:], w_hi[:, e % 2, :], w_lo[:, e % 2, :], w_split, 2 * e)
                pool.wait_ge(w_split, 2 * e + 2)
            flat = d.place[:, :, :].rearrange("p k t -> p (k t)")
            for e in range(E):
                if e == 0:
                    pool.tensor_scalar(moved[:], flat, 0.0, shift[:, 0:1], ALU.is_ge, ALU.mult).then_inc(moving, 1)
                else:
                    pool.tensor_scalar(moved[:], rows_of[:], float(e * d.capacity), jump[:, e - 1:e],
                                       ALU.is_ge, ALU.mult).then_inc(moving, 1)
                pool.wait_ge(moving, 2 * e + 1)
                pool.tensor_tensor(flat, flat, moved[:], ALU.subtract).then_inc(moving, 1)
                if e < E - 1:
                    pool.wait_ge(moving, 2 * e + 2)
            pool.wait_ge(moving, 2 * E)
            pool.tensor_copy(d.place_i[:, :, :].rearrange("p k t -> p (k t)"), flat).then_inc(moving, 1)

        @block.scalar
        def _(act):
            def output(m, par):
                act.wait_ge(f.y_mm, m + 1)
                if inside(m - 2, NBLK):
                    hold(act, d, y_stored[par], 16 * half(m, par))
                act.activation(y[:, par, :], f.y_bank[par][:, 0:H], ACT.Copy).then_inc(f.y_out, 1)

            def step(n, par):
                if inside(n - 2, NBLK):
                    output(n - 2, par)
                if inside(n - 1, NBLK):
                    f.act_products_high(act, n - 1, 1 - par)
                if inside(n + 1, NBLK):
                    f.act_rows_high(act, n + 1, 1 - par)
                f.act_silu(act, n, par)

            f.act_rows_high(act, 0, 0)
            steps(act, step)
            output(NBLK - 2, 0)
            f.act_products_high(act, NBLK - 1, 1)
            output(NBLK - 1, 1)

        @block.tensor
        def _(pe):
            def weights(e):
                def columns(t, o, n):
                    return lambda c: t[:, ds(e & 1, 1), o + n * c:o + n * c + n]

                return [tuple(columns(t, W * k, n) for t in (w_hi, w_lo)) for k, n in enumerate((I, I, H))]

            def experts(i):
                packed = pe.value_load(table[0:1, 1, at(i)], min_val=0, max_val=E ** 4 - 1)
                return [(packed >> (LOG_E * k)) & (E - 1) for k in range(4)]

            def step(n, par):
                if par == 0:
                    who[:] = experts(n // 2 if isinstance(n, int) else half(n, 0))
                e = who[2 + par]
                if inside(n - 2, NBLK):
                    f.pe_down(pe, n - 2, par, weights(who[par]))
                if inside(n - 1, NBLK):
                    f.pe_turn_products(pe, n - 1, 1 - par)
                if inside(n + 1, NBLK):
                    turn_rows(n + 1, 1 - par)
                pe.wait_ge(w_split, 2 * e + 2)
                f.pe_gate_up(pe, n, par, weights(e))

            who = []
            def turn_rows(m, par):
                f.rows_ready = h_in[par]
                f.ready_at = lambda m: 16 * half(m, par) + 16
                f.pe_turn_rows(pe, m, par, h[:, par, :])

            turn_rows(0, 0)
            pe.wait_ge(plan, PLAN)
            steps(pe, step)
            f.pe_down(pe, NBLK - 2, 0, weights(who[2]))
            f.pe_turn_products(pe, NBLK - 1, 1)
            f.pe_down(pe, NBLK - 1, 1, weights(who[3]))

        @block.vector
        def _(dve):
            p = [0]

            def op(ins):
                ins.then_inc(plan, 1)
                p[0] += 1
                dve.wait_ge(plan, p[0])

            c = d.consts
            dve.tensor_copy(free_i[:], d.base[0:1, len(d.groups), :]).then_inc(free_known, 1)
            op(dve.tensor_tensor(count[:], d.base[:, len(d.groups), :], d.first_row[:, 0:E], ALU.subtract))
            op(dve.tensor_tensor(over[:], count[:].unsqueeze(2).to_broadcast([P, E, d.most]),
                                 c.limits[:].unsqueeze(1).to_broadcast([P, E, d.most]), ALU.is_gt))
            op(dve.tensor_reduce(nblocks[:], over[:], AX_X, ALU.add))
            op(dve.tensor_copy(ends[:], nblocks[:]))
            for e in range(1, E):
                op(dve.tensor_tensor(ends[:, e:e + 1], ends[:, e - 1:e], nblocks[:, e:e + 1], ALU.add))
            op(dve.memset(starts[:, 0:1], 0.0))
            op(dve.tensor_copy(starts[:, 1:E + 1], ends[:]))
            op(dve.scalar_tensor_tensor(out=shift[:], in0=starts[:], scalar=-float(P), in1=d.first_row[:, 0:E + 1],
                                        op0=ALU.mult, op1=ALU.add))
            op(dve.tensor_tensor(jump[:], shift[:, 1:E + 1], shift[:, 0:E], ALU.subtract))
            op(dve.tensor_tensor(behind[:], c.numbers[:].unsqueeze(2).to_broadcast([1, NBLK, E]),
                                 ends[0:1].unsqueeze(1).to_broadcast([1, NBLK, E]), ALU.is_ge))
            op(dve.tensor_tensor(jumped[:], behind[:], jump[0:1].unsqueeze(1).to_broadcast([1, NBLK, E]), ALU.mult))
            op(dve.tensor_reduce(moved_by[:], jumped[:], AX_X, ALU.add))
            op(dve.scalar_tensor_tensor(out=row0[:], in0=c.numbers[:], scalar=float(P), in1=moved_by[:],
                                        op0=ALU.mult, op1=ALU.add))
            op(dve.tensor_copy(table[:, 0], row0[:]))
            op(dve.memset(expert_of[:, 0:2], 0.0))
            op(dve.tensor_reduce(expert_of[:, 2:], behind[:, :, 0:E - 1], AX_X, ALU.add))
            by_pair = expert_of[:].rearrange("o (i two) -> o i two", two=2)
            digit = [by_pair[:, 0:NBLK // 2, 0], by_pair[:, 0:NBLK // 2, 1],
                     by_pair[:, 1:NBLK // 2 + 1, 0], by_pair[:, 1:NBLK // 2 + 1, 1]]
            so_far = digit[3]
            for k in (2, 1, 0):
                op(dve.scalar_tensor_tensor(out=packed[:, k], in0=so_far, scalar=float(E), in1=digit[k],
                                            op0=ALU.mult, op1=ALU.add))
                so_far = packed[:, k]
            op(dve.tensor_copy(table[:, 1, 0:NBLK // 2], packed[:, 0]))
            op(dve.tensor_copy(ends_i[:], ends[0:1]))
            assert p[0] == PLAN
            dve.wait_ge(first_loaded, 48)
            split_weights(dve, w_raw[:], w_hi[:, 0, :], w_lo[:, 0, :], w_split, 0)

            def step(n, par):
                if inside(n - 1, NBLK):
                    f.dve_products_low(dve, n - 1, 1 - par)
                if inside(n + 1, NBLK):
                    f.dve_rows_low(dve, n + 1, 1 - par)
                f.dve_products(dve, n, par)

            f.dve_rows_low(dve, 0, 0)
            steps(dve, step)
            f.dve_products_low(dve, NBLK - 1, 1)


def last_phase(nc, d, shared_gate, shared_up, shared_down, out):
    H = out.shape[3]
    I = shared_gate.shape[2]
    HC, IC = H // P, I // P
    NT, TB = d.NT, d.NT // d.NB
    EARLY = TB * d.early
    LATE = NT - EARLY
    DEPTH = 4
    with ExitStack() as ctx:
        sb = lambda n, s, t: ctx.enter_context(nc.sbuf_tensor(n, s, t))
        sem = lambda n: ctx.enter_context(nc.semaphore(n))
        f = gated_blocks(ctx, nc, d, "l", LATE, H, I)
        f.ready_at = lambda m: m + 1
        matrix = lambda n, a, c, t: sb(n, [P, a, c], t)
        g_raw, g_hi, g_lo = (matrix("l_g_" + n, HC, I, t) for n, t in (("raw", F32), ("hi", F32R), ("lo", F32R)))
        u_raw, u_hi, u_lo = (matrix("l_u_" + n, HC, I, t) for n, t in (("raw", F32), ("hi", F32R), ("lo", F32R)))
        w_raw, w_hi, w_lo = (matrix("l_d_" + n, IC, H, t) for n, t in (("raw", F32), ("hi", F32R), ("lo", F32R)))
        y1, y2 = sb("y1", [P, 2, DEPTH, H], F32), sb("y2", [P, 2, DEPTH, H], F32)
        first = sb("first", [P, 2, 2, H], F32)
        both = sb("both", [P, 2, 2, H], F32)
        with_shared = sb("with_shared", [P, 2, H], F32)
        gated = sb("l_gated", [P, 2, 2, H], F32)
        norm = sb("l_norm", [P, 2, H], F32)
        scaled = sb("l_scaled", [P, 2, H], F32)
        h = sb("l_h", [P, 2, H], F32)

        w_loaded = [sem(f"l_w_loaded{i}") for i in range(3)]
        w_high, w_split = sem("l_w_high"), sem("l_w_split")
        norm_done, scaled_done = sem("l_norm_done"), sem("l_scaled_done")
        y_in = [[sem(f"y_in{g}_{i}") for i in range(DEPTH)] for g in range(2)]
        two = lambda n: [sem(n + "_early"), sem(n + "_late")]
        first_done, both_done, gated_done, out_done = (two(n) for n in ("first", "both", "gated", "out_done"))
        stored = sem("stored")
        weights = ((g_raw, g_hi, g_lo), (u_raw, u_hi, u_lo), (w_raw, w_hi, w_lo))
        block = ctx.enter_context(nc.Block())

        def tile(g, i):
            return EARLY * g + i

        def gate_row(n):
            return d.mod_rows[:, n // TB, 3 * H:4 * H]

        @block.gpsimd
        def _(pool):
            for i in range(LATE):
                for g in range(2):
                    if i >= DEPTH:
                        pool.wait_ge(both_done[g], i - DEPTH + 1)
                    for k, y in enumerate((y1, y2)):
                        n = tile(g, i)
                        pool.indirect_dma_start(
                            y[:, g, i % DEPTH, :], None, d.y_rows,
                            bass.IndirectOffsetOnAxis(ap=d.place_i[:, k, n:n + 1], axis=0)
                        ).then_inc(y_in[g][i % DEPTH], 16)

        @block.sync
        def _(sp):
            for n, src in enumerate((shared_gate, shared_up, shared_down)):
                sp.dma_start(weights[n][0][:], src).then_inc(w_loaded[n], 16)
            for i in range(LATE // 4):
                for g in range(2):
                    n = tile(g, 4 * i)
                    sp.wait_ge(out_done[g], 4 * i + 4)
                    sp.dma_start(out[n // TB, :, n % TB:n % TB + 4, :], d.Z[:, n:n + 4, :]).then_inc(stored, 16)
            sp.wait_ge(stored, 16 * (NT // 4))

        @block.scalar
        def _(act):
            def normalise(i):
                if i >= 2:
                    act.wait_ge(scaled_done, i - 1)
                n = tile(1, i)
                act.activation(norm[:, i % 2, :], d.Z[:, n, :], ACT.Identity, scale=d.rstd[:, n:n + 1],
                               bias=d.offset[:, n:n + 1]).then_inc(norm_done, 1)

            def first_score(g, i):
                act.wait_ge(y_in[g][i % DEPTH], 32 * (i // DEPTH) + 32)
                if i >= 2:
                    act.wait_ge(both_done[g], i - 1)
                n = tile(g, i)
                act.activation(first[:, g, i % 2, :], y1[:, g, i % DEPTH, :], ACT.Copy,
                               scale=d.score[:, 0, n:n + 1]).then_inc(first_done[g], 1)

            normalise(0)
            normalise(1)
            for n, (raw, hi, lo) in enumerate(weights):
                act.wait_ge(w_loaded[n], 16)
                act.activation(hi[:], raw[:], ACT.Copy).then_inc(w_high, 1)
            f.act_rows_high(act, 0, 0)
            for i in range(LATE):
                par = i % 2
                if i + 2 < LATE:
                    normalise(i + 2)
                if i:
                    f.act_products_high(act, i - 1, 1 - par)
                if i + 1 < LATE:
                    f.act_rows_high(act, i + 1, 1 - par)
                first_score(0, i)
                if i >= 1:
                    first_score(1, i - 1)
                f.act_silu(act, i, par)
            f.act_products_high(act, LATE - 1, 1)
            first_score(1, LATE - 1)

        @block.tensor
        def _(pe):
            columns = [(lambda c: g_hi[:, c, :], lambda c: g_lo[:, c, :]),
                       (lambda c: u_hi[:, c, :], lambda c: u_lo[:, c, :]),
                       (lambda c: w_hi[:, c, :], lambda c: w_lo[:, c, :])]

            def step(i, par):
                if inside(i - 2, LATE):
                    f.pe_down(pe, i - 2, par, columns)
                if inside(i - 1, LATE):
                    f.pe_turn_products(pe, i - 1, 1 - par)
                if inside(i + 1, LATE):
                    f.pe_turn_rows(pe, i + 1, 1 - par, h[:, 1 - par, :])
                f.pe_gate_up(pe, i, par, columns)

            f.pe_turn_rows(pe, 0, 0, h[:, 0, :])
            pe.wait_ge(w_split, 3)
            for i in range(4):
                step(i, i % 2)
            with pe.Fori(2, LATE // 2 - 1) as i:
                step(2 * i, 0)
                step(2 * i + 1, 1)
            step(LATE - 2, 0)
            step(LATE - 1, 1)
            f.pe_down(pe, LATE - 2, 0, columns)
            f.pe_turn_products(pe, LATE - 1, 1)
            f.pe_down(pe, LATE - 1, 1, columns)

        @block.vector
        def _(dve):
            def scale(i):
                row = d.mod_rows[:, tile(1, i) // TB, 2 * H:3 * H]
                dve.wait_ge(norm_done, i + 1)
                dve.tensor_tensor(scaled[:, i % 2, :], norm[:, i % 2, :], row, ALU.mult).then_inc(scaled_done, 1)

            def shift(i):
                row = d.mod_rows[:, tile(1, i) // TB, H:2 * H]
                dve.wait_ge(scaled_done, i + 1)
                if i >= 2:
                    dve.wait_ge(f.xT_mm, i - 1)
                dve.tensor_tensor(h[:, i % 2, :], scaled[:, i % 2, :], row, ALU.add).then_inc(f.rows_ready, 1)

            def both_scores(g, i):
                n = tile(g, i)
                dve.wait_ge(first_done[g], i + 1)
                dve.scalar_tensor_tensor(out=both[:, g, i % 2, :], in0=y2[:, g, i % DEPTH, :],
                                         scalar=d.score[:, 1, n:n + 1], in1=first[:, g, i % 2, :],
                                         op0=ALU.mult, op1=ALU.add).then_inc(both_done[g], 1)

            def add_shared(i):
                dve.wait_ge(both_done[1], i + 1)
                dve.wait_ge(f.y_mm, i + 1)
                dve.tensor_tensor(with_shared[:, i % 2, :], f.y_bank[i % 2][:, 0:H], both[:, 1, i % 2, :],
                                  ALU.add).then_inc(f.y_out, 1)

            def gate(g, i):
                if g:
                    dve.wait_ge(f.y_out, i + 1)
                else:
                    dve.wait_ge(both_done[0], i + 1)
                src = with_shared[:, i % 2, :] if g else both[:, 0, i % 2, :]
                dve.tensor_tensor(gated[:, g, i % 2, :], src, gate_row(tile(g, i)), ALU.mult).then_inc(gated_done[g], 1)

            def output(g, i):
                n = tile(g, i)
                dve.wait_ge(gated_done[g], i + 1)
                dve.tensor_tensor(d.Z[:, n, :], gated[:, g, i % 2, :], d.Z[:, n, :], ALU.add).then_inc(out_done[g], 1)

            for i in range(2):
                scale(i)
                shift(i)
            for n, (raw, hi, lo) in enumerate(weights):
                dve.wait_ge(w_high, n + 1)
                dve.tensor_tensor(lo[:], raw[:], hi[:].bitcast(F32), ALU.subtract).then_inc(w_split, 1)
            f.dve_rows_low(dve, 0, 0)
            for i in range(LATE):
                par = i % 2
                if i >= 1:
                    both_scores(0, i - 1)
                if i + 2 < LATE:
                    scale(i + 2)
                if i >= 1:
                    gate(0, i - 1)
                if i + 2 < LATE:
                    shift(i + 2)
                if i >= 1:
                    output(0, i - 1)
                if i >= 2:
                    both_scores(1, i - 2)
                if i >= 1:
                    f.dve_products_low(dve, i - 1, 1 - par)
                if i >= 2:
                    add_shared(i - 2)
                if i + 1 < LATE:
                    f.dve_rows_low(dve, i + 1, 1 - par)
                if i >= 2:
                    gate(1, i - 2)
                f.dve_products(dve, i, par)
                if i >= 2:
                    output(1, i - 2)
            i = LATE - 1
            both_scores(0, i)
            f.dve_products_low(dve, i, 1)
            both_scores(1, i - 1)
            gate(0, i)
            add_shared(i - 1)
            output(0, i)
            gate(1, i - 1)
            both_scores(1, i)
            output(1, i - 1)
            add_shared(i)
            gate(1, i)
            output(1, i)


def constants(nc, d, sb, sem, E, NBLK):
    d.ident = sb("ident", [P, P], F32)
    d.minus_half = sb("minus_half", [P, 16], F32)
    d.before = sb("before", [P, P], BF16)
    d.ones = sb("ones", [P, P], BF16)
    d.codes = sb("codes", [P, E], F32)
    d.first_row = sb("first_row", [P, E + 1], F32)
    d.consts = c = Namespace()
    c.limits = sb("limits", [P, d.most], F32)
    c.numbers = sb("numbers", [1, NBLK], F32)
    d.s_const = sem("s_const")
    sets = [(d.ident[:], 0.0), (d.minus_half[:], -0.5), (d.before[:], 1.0), (d.ones[:], 1.0),
            (c.limits[:, 0:1], -1.0)]
    sets += [(d.codes[:, e:e + 1], float(E - e)) for e in range(E)]
    sets += [(d.first_row[:, e:e + 1], float(d.capacity * e)) for e in range(E + 1)]
    d.n_const = len(sets) + 4
    with nc.Block() as block:
        @block.gpsimd
        def _(pool):
            for out, v in sets:
                pool.memset(out, v).then_inc(d.s_const, 1)
            pool.wait_ge(d.s_const, len(sets))
            pool.affine_select(out=d.ident[:], in_=d.ident[:], compare_op=ALU.not_equal, fill=1.0, base=0,
                               pattern=[[-1, P]], channel_multiplier=1).then_inc(d.s_const, 1)
            pool.affine_select(out=d.before[:], in_=d.before[:], compare_op=ALU.is_gt, fill=0.0, base=0,
                               pattern=[[1, P]], channel_multiplier=-1).then_inc(d.s_const, 1)
            pool.iota(c.limits[:, 1:], pattern=[[P, d.most - 1]], base=P, channel_multiplier=0,
                      allow_small_or_imprecise_dtypes=True).then_inc(d.s_const, 1)
            pool.iota(c.numbers[:], pattern=[[1, NBLK]], base=0, channel_multiplier=0,
                      allow_small_or_imprecise_dtypes=True).then_inc(d.s_const, 1)
            pool.wait_ge(d.s_const, d.n_const)


def layer(nc, x, mask, cT_in, wmod, wqkv, wo, shared_gate, shared_up, shared_down, router_w, router_bias,
          gate_w, up_w, down_w, out):
    d = Namespace()
    NB, S, H = x.shape
    E = router_w.shape[2]
    T = NB * S
    TOP = 2
    d.NB, d.NT, d.E = NB, T // P, E
    d.capacity = T + P
    d.spare_row = E * d.capacity
    d.all_rows = d.spare_row + E * P
    d.most = T // P
    d.blocks = TOP * T // P + E
    d.x1 = nc.dram_tensor("x1", (T, H), F32, kind="Internal").ap()
    d.x_rows = nc.dram_tensor("x_rows", (d.all_rows, H), F32, kind="Internal").ap()
    d.y_rows = nc.dram_tensor("y_rows", (d.blocks * P, H), F32, kind="Internal").ap()
    with ExitStack() as ctx:
        sb = lambda n, s, t: ctx.enter_context(nc.sbuf_tensor(n, s, t))
        sem = lambda n: ctx.enter_context(nc.semaphore(n))
        d.mod_rows = sb("mod_rows", [P, NB, 4 * H], F32)
        d.stats1 = sb("stats1", [P, T // P, 6], F32)
        d.early = NB // 2
        d.steps = T // P // 2
        chunk = T // P // NB // 2
        d.groups = [(n, chunk) for n in range(0, d.steps - chunk, chunk)]
        d.groups += [(n, chunk // 2) for n in range(d.steps - chunk, d.steps, chunk // 2)]
        d.base = sb("base", [P, len(d.groups) + 1, E], F32)
        d.place_i = sb("place_i", [P, TOP, T // P], I32)
        d.place = sb("place", [P, TOP, T // P], F32)
        d.score = sb("score", [P, TOP, T // P], F32)
        d.s_gate = sem("s_gate")
        d.passed = sem("passed")
        d.stats1_done = sem("stats1_done")
        d.base_set = sem("base_set")
        constants(nc, d, sb, sem, E, d.blocks)
        attention_phase(nc, d, x, cT_in, wmod, wqkv, wo, mask)
        d.Z = sb("Z", [P, T // P, H], F32)
        d.mv = sb("s_mv", [P, T // P, 2], F32)
        d.rstd = sb("s_rstd", [P, T // P], F32)
        d.offset = sb("s_offset", [P, T // P], F32)
        d.last_rows = sb("last_rows", [P, 2, chunk, H], F32)
        shared_phase(nc, d, d.x1, shared_gate, shared_up, shared_down, router_w, router_bias)
        experts_phase(nc, d, gate_w, up_w, down_w)
        last_phase(nc, d, shared_gate, shared_up, shared_down, out.rearrange("b (t p) h -> b p t h", p=P))


def kernel(**inputs):
    from concourse import bacc
    from concourse.bass_utils import run_bass_kernel_spmd

    a = {k[3:]: np.asarray(v) for k, v in inputs.items()}
    c = np.ascontiguousarray
    H = a["wmod"].shape[0]
    E, _, I = a["ffn_gate_w"].shape

    def on_partitions(w):
        return c(w.reshape(w.shape[0] // P, P, -1).transpose(1, 0, 2))

    def each_on_partitions(w):
        return c(w.reshape(E, w.shape[1] // P, P, -1).transpose(0, 2, 1, 3))

    arrays = {
        "x": c(a["attn_x"]),
        "mask": c(a["attn_head_dim_mask"].reshape(P, 1)),
        "cT": on_partitions(a["c"].T),
        "wmod": c(a["wmod"]),
        "wqkv": on_partitions(np.concatenate([a["attn_w_q"], a["attn_w_k"], a["attn_w_v"]], 1)),
        "wo": c(a["attn_w_o"]),
        "shared_gate": on_partitions(a["ffn_shared_gate"].T),
        "shared_up": on_partitions(a["ffn_shared_up"].T),
        "shared_down": on_partitions(a["ffn_shared_down"].T),
        "router_w": on_partitions(a["ffn_router_w"].T),
        "router_bias": c(a["ffn_routing_bias"].reshape(1, E)),
        "gate_w": each_on_partitions(a["ffn_gate_w"]),
        "up_w": each_on_partitions(a["ffn_up_w"]),
        "down_w": each_on_partitions(a["ffn_down_w"]),
    }
    nc = bacc.Bacc("TRN2", target_bir_lowering=False, num_devices=1)
    aps = [nc.dram_tensor(f"in_{k}", v.shape, mybir.dt.from_np(v.dtype), kind="ExternalInput").ap()
           for k, v in arrays.items()]
    out = nc.dram_tensor("out_0", a["attn_x"].shape, F32, kind="ExternalOutput").ap()
    layer(nc, *aps, out)
    r = run_bass_kernel_spmd(nc, [{f"in_{k}": v for k, v in arrays.items()}], core_ids=[0])
    return r.results[0]["out_0"]
```
